# Optimizing a Trainium2 kernel written in Bass

```python
import numpy as np
import jax
import jax.numpy as jnp

def _softmax(x, axis=-1):
    return jax.nn.softmax(x, axis=axis)

def _gelu(x):
    return jax.nn.gelu(x, approximate=True)

def _silu(x):
    return jax.nn.silu(x)

def _sigmoid(x):
    return jax.nn.sigmoid(x)

def _layernorm(x, axis=-1, eps=1e-05):
    m = jnp.mean(x, axis=axis, keepdims=True)
    v = jnp.var(x, axis=axis, keepdims=True)
    return (x - m) / jnp.sqrt(v + eps)

def _scatter_add(tgt, idx, src, axis=0):
    return tgt.at[idx].add(src)

def _segment_sum(src, seg, n):
    return jax.ops.segment_sum(src, seg, n)
kernel_name = 'mk_perceiver_d2_seqx_r2_5acb4f'

def setup_inputs(seed: int=0):
    np.random.seed(seed)
    _w = jnp.asarray

    def _rec_inputs():
        import jax
        import jax.numpy as jnp
        _rk = jax.random.key(seed)
        x = 7.22e-05 + 1 * jax.random.normal(jax.random.fold_in(_rk, 1), (32, 32, 512), jnp.float32)
        _lenS = 32 - jax.random.randint(jax.random.fold_in(_rk, 7), (32,), 0, max(1, 32 // 4) + 1, jnp.int32)
        _lenS2 = 257 - jax.random.randint(jax.random.fold_in(_rk, 8), (32,), 0, max(1, 257 // 4) + 1, jnp.int32)
        _ctx_1024P = jax.random.normal(jax.random.fold_in(_rk, 11), (32, 16, 512), jnp.float32)
        _ctx_1024c = jax.random.dirichlet(jax.random.fold_in(_rk, 511), 0.3 * jnp.ones((16,), jnp.float32), (32, 257))
        _ctx_1024t = jnp.einsum('bsk,bkd->bsd', _ctx_1024c, _ctx_1024P)
        _ctx_1024t = _ctx_1024t * jax.lax.rsqrt(jnp.mean(jnp.square(_ctx_1024t)) + 1e-12) * 0.953939
        ctx_1024 = 4.13588e-05 + 0.999923 * (_ctx_1024t + 0.3 * jax.random.normal(jax.random.fold_in(_rk, 611), (32, 257, 512), jnp.float32))
        return (x, ctx_1024)
    x, ctx_1024 = _rec_inputs()

    def _L0_xattn_setup():
        import math
        import jax, jax.numpy as jnp
        import numpy as np
        H = 16
        D_MODEL = 512
        DK = D_MODEL // H
        K_FACTOR = 2

        def _time_delay_agg_inference(v, corr):
            B, _, _, L = v.shape
            top_k = min(int(K_FACTOR * math.log(L)), L)
            mean_value = jnp.mean(corr, axis=(1, 2))
            weights, delay = jax.lax.top_k(mean_value, top_k)
            tmp_corr = jax.nn.softmax(weights, axis=-1)
            idx = (delay[:, :, None] + jnp.arange(L)) % L
            gathered = jnp.take_along_axis(v[:, None], idx[:, :, None, None, :], axis=-1)
            return jnp.einsum('bk,bkhdl->bhdl', tmp_corr, gathered)
        key = jax.random.key(seed)
        ks = jax.random.split(key, 11)
        B, L, D = (4, 1024, D_MODEL)
        s = 1.0 / math.sqrt(D)
        return {'queries': jax.random.normal(ks[0], (B, L, D), jnp.float32), 'keys': jax.random.normal(ks[1], (B, L, D), jnp.float32), 'values': jax.random.normal(ks[2], (B, L, D), jnp.float32), 'Wq': jax.random.normal(ks[3], (D, H * DK), jnp.float32) * s, 'bq': jnp.zeros((H * DK,), jnp.float32), 'Wk': jax.random.normal(ks[4], (D, H * DK), jnp.float32) * s, 'bk': jnp.zeros((H * DK,), jnp.float32), 'Wv': jax.random.normal(ks[5], (D, H * DK), jnp.float32) * s, 'bv': jnp.zeros((H * DK,), jnp.float32), 'Wo': jax.random.normal(ks[6], (H * DK, D), jnp.float32) * s, 'bo': jnp.zeros((D,), jnp.float32)}
    _L0_xattn_all = _L0_xattn_setup()
    _L0_xattn_in = {k: v for k, v in _L0_xattn_all.items() if k in ('Wq', 'bq', 'Wk', 'bk', 'Wv', 'bv', 'Wo', 'bo')}
    del _L0_xattn_all

    def _L0_attn_setup():
        import math
        import jax, jax.numpy as jnp
        import numpy as np
        D_MODEL = 512
        N_HEAD = 16
        HEAD_DIM = D_MODEL // N_HEAD
        B, T = (2, 1024)

        def _layernorm(x, g, b, eps=1e-05):
            mu = jnp.mean(x, axis=-1, keepdims=True)
            var = jnp.mean(jnp.square(x - mu), axis=-1, keepdims=True)
            return (x - mu) * jax.lax.rsqrt(var + eps) * g + b

        def _l2norm(x, eps=1e-12):
            n = jnp.sqrt(jnp.sum(jnp.square(x), axis=-1, keepdims=True))
            return x / jnp.maximum(n, eps)

        def _rope(x, times):
            half = x.shape[-1] // 2
            freqs = jnp.exp(-jnp.arange(half, dtype=x.dtype) * (math.log(10000.0) / half))
            theta = times[:, None] * freqs[None, :]
            cos = jnp.cos(theta)[None, :, None, :]
            sin = jnp.sin(theta)[None, :, None, :]
            xr = x.reshape(*x.shape[:-1], half, 2)
            x1, x2 = (xr[..., 0], xr[..., 1])
            r1 = x1 * cos - x2 * sin
            r2 = x1 * sin + x2 * cos
            return jnp.stack([r1, r2], axis=-1).reshape(x.shape)
        key = jax.random.key(seed)
        ks = jax.random.split(key, 16)
        s = 0.02
        f32 = jnp.float32
        inp = {'x': jax.random.normal(ks[0], (B, T, D_MODEL), f32), 'Wq': jax.random.normal(ks[1], (D_MODEL, D_MODEL), f32) * s, 'Wk': jax.random.normal(ks[2], (D_MODEL, D_MODEL), f32) * s, 'Wv': jax.random.normal(ks[3], (D_MODEL, D_MODEL), f32) * s, 'gate_w': jax.random.normal(ks[4], (D_MODEL, D_MODEL), f32) * s, 'gate_b': jnp.zeros((D_MODEL,), f32), 'p_w': jax.random.normal(ks[5], (D_MODEL, D_MODEL), f32) * s, 'p_b': jnp.zeros((D_MODEL,), f32), 'out_w': jax.random.normal(ks[6], (D_MODEL, D_MODEL), f32) * s, 'out_b': jnp.zeros((D_MODEL,), f32), 'clock_w': jax.random.normal(ks[7], (D_MODEL, N_HEAD), f32) * s, 'clock_b': jnp.zeros((N_HEAD,), f32), 'ln1_g': jnp.ones((D_MODEL,), f32), 'ln1_b': jnp.zeros((D_MODEL,), f32), 'ln2_g': jnp.ones((D_MODEL,), f32), 'ln2_b': jnp.zeros((D_MODEL,), f32), 'mlp_w1': jax.random.normal(ks[8], (D_MODEL, 4 * D_MODEL), f32) * s, 'mlp_b1': jnp.zeros((4 * D_MODEL,), f32), 'mlp_w2': jax.random.normal(ks[9], (4 * D_MODEL, D_MODEL), f32) * s, 'mlp_b2': jnp.zeros((D_MODEL,), f32)}
        return inp
    _L0_attn_all = _L0_attn_setup()
    _L0_attn_in = {k: v for k, v in _L0_attn_all.items() if k in ('Wq', 'Wk', 'Wv', 'gate_w', 'gate_b', 'p_w', 'p_b', 'out_w', 'out_b', 'clock_w', 'clock_b', 'ln1_g', 'ln1_b', 'ln2_g', 'ln2_b', 'mlp_w1', 'mlp_b1', 'mlp_w2', 'mlp_b2')}
    del _L0_attn_all

    def _L0_ffn_setup():
        import jax, jax.numpy as jnp
        import numpy as np
        B, T, D = (2, 1024, 512)
        DCD = 2048
        RET = 128
        NEXP = 2048
        NKEYS = 64
        H = 4
        KPH = 8
        key = jax.random.key(seed)
        ks = jax.random.split(key, 10)
        s = lambda k, shape, scale: jax.random.normal(k, shape, jnp.float32) * scale
        return {'hidden_states': jax.random.normal(ks[0], (B, T, D), jnp.float32), 'Wg': s(ks[1], (D, DCD), 0.02), 'bg': jnp.zeros((DCD,), jnp.float32), 'Wu': s(ks[2], (D, DCD), 0.02), 'bu': jnp.zeros((DCD,), jnp.float32), 'Wd': s(ks[3], (DCD, D), 0.02), 'bd': jnp.zeros((D,), jnp.float32), 'Wq': s(ks[4], (D, RET * H), 0.02), 'keys': s(ks[5], (H, NKEYS, 2, RET // 2), 0.02), 'down_embed': s(ks[6], (NEXP, D), 0.02), 'up_embed': s(ks[7], (NEXP, D), 0.02)}
    _L0_ffn_all = _L0_ffn_setup()
    _L0_ffn_in = {k: v for k, v in _L0_ffn_all.items() if k in ('Wg', 'bg', 'Wu', 'bu', 'Wd', 'bd', 'Wq', 'keys', 'down_embed', 'up_embed')}
    del _L0_ffn_all

    def _L1_xattn_setup():
        import jax, jax.numpy as jnp
        import numpy as np
        DIM = 512
        HEADS = 16
        DIM_HEAD = 64
        INNER = HEADS * DIM_HEAD
        EPS = 1e-05

        def _split_heads(t):
            b, n, _ = t.shape
            return t.reshape(b, n, HEADS, DIM_HEAD).transpose(0, 2, 1, 3)
        key = jax.random.key(seed)
        ks = jax.random.split(key, 9)
        b, n, m = (2, 1024, 128)
        s = DIM ** (-0.5)
        return {'x': jax.random.normal(ks[0], (b, n, DIM), jnp.float32), 'memories': jax.random.normal(ks[1], (b, m, DIM), jnp.float32), 'ln_g': jnp.ones((DIM,), jnp.float32), 'ln_b': jnp.zeros((DIM,), jnp.float32), 'Wq': jax.random.normal(ks[2], (DIM, INNER), jnp.float32) * s, 'Wkv': jax.random.normal(ks[3], (DIM, 2 * INNER), jnp.float32) * s, 'Wm': jax.random.normal(ks[4], (DIM, INNER), jnp.float32) * s, 'Wo': jax.random.normal(ks[5], (INNER, DIM), jnp.float32) * s, 'bo': jnp.zeros((DIM,), jnp.float32)}
    _L1_xattn_all = _L1_xattn_setup()
    _L1_xattn_in = {k: v for k, v in _L1_xattn_all.items() if k in ('ln_g', 'ln_b', 'Wq', 'Wkv', 'Wm', 'Wo', 'bo')}
    del _L1_xattn_all

    def _L1_attn_setup():
        import jax, jax.numpy as jnp
        import numpy as np
        D_MODEL = 512
        D_HIDDEN = 128
        key = jax.random.key(seed)
        ks = jax.random.split(key, 10)
        B, T = (4, 2048)
        s = lambda fan_in: 1.0 / np.sqrt(fan_in)
        return {'x': jax.random.normal(ks[0], (B, T, D_MODEL), dtype=jnp.float32), 'A': jnp.log(jnp.arange(1, D_HIDDEN + 1, dtype=jnp.float32)), 'Wb': jax.random.uniform(ks[1], (D_MODEL, D_HIDDEN), jnp.float32, -s(D_MODEL), s(D_MODEL)), 'bb': jax.random.uniform(ks[2], (D_HIDDEN,), jnp.float32, -s(D_MODEL), s(D_MODEL)), 'Wc': jax.random.uniform(ks[3], (D_HIDDEN, D_MODEL), jnp.float32, -s(D_HIDDEN), s(D_HIDDEN)), 'bc': jax.random.uniform(ks[4], (D_MODEL,), jnp.float32, -s(D_HIDDEN), s(D_HIDDEN)), 'Wd': jax.random.uniform(ks[5], (D_MODEL, D_MODEL), jnp.float32, -s(D_MODEL), s(D_MODEL)), 'bd': jax.random.uniform(ks[6], (D_MODEL,), jnp.float32, -s(D_MODEL), s(D_MODEL)), 'Wdelta': jax.random.uniform(ks[7], (D_MODEL, D_HIDDEN), jnp.float32, -s(D_MODEL), s(D_MODEL)), 'bdelta': jax.random.uniform(ks[8], (D_HIDDEN,), jnp.float32, -s(D_MODEL), s(D_MODEL))}
    _L1_attn_all = _L1_attn_setup()
    _L1_attn_in = {k: v for k, v in _L1_attn_all.items() if k in ('A', 'Wb', 'bb', 'Wc', 'bc', 'Wd', 'bd', 'Wdelta', 'bdelta')}
    del _L1_attn_all

    def _L1_ffn_setup():
        import jax, jax.numpy as jnp
        import numpy as np

        def _bitlinear(x, w_latent):
            scale = jax.lax.stop_gradient(jnp.clip(jnp.mean(jnp.abs(w_latent), axis=1, keepdims=True), 1e-05, None))
            tern = jnp.clip(jnp.round(w_latent / scale), -1.0, 1.0)
            w = w_latent + jax.lax.stop_gradient(tern - w_latent)
            return x @ (w * scale).T
        key = jax.random.key(seed)
        ks = jax.random.split(key, 6)
        dim, hidden, rank = (512, 2048, 16)
        B, S = (4, 2048)
        x = jax.random.normal(ks[0], (B, S, dim), dtype=jnp.float32)
        w_fc = 0.02 * jax.random.normal(ks[1], (hidden, dim), dtype=jnp.float32)
        w_proj = 0.02 * jax.random.normal(ks[2], (dim, hidden), dtype=jnp.float32)
        u = 0.02 * jax.random.normal(ks[3], (hidden, rank), dtype=jnp.float32)
        v = 0.02 * jax.random.normal(ks[4], (rank, dim), dtype=jnp.float32)
        fast_b = jax.random.normal(ks[5], (rank, rank), dtype=jnp.float32)
        gate = jnp.float32(0.05)
        return {'x': x, 'fast_b': fast_b, 'w_fc': w_fc, 'w_proj': w_proj, 'u': u, 'v': v, 'gate': gate}
    _L1_ffn_all = _L1_ffn_setup()
    _L1_ffn_in = {k: v for k, v in _L1_ffn_all.items() if k in ('fast_b', 'w_fc', 'w_proj', 'u', 'v', 'gate')}
    del _L1_ffn_all
    return {'x': x, 'ctx_1024': ctx_1024, 'L0_xattn_Wq': _L0_xattn_in['Wq'], 'L0_xattn_bq': _L0_xattn_in['bq'], 'L0_xattn_Wk': _L0_xattn_in['Wk'], 'L0_xattn_bk': _L0_xattn_in['bk'], 'L0_xattn_Wv': _L0_xattn_in['Wv'], 'L0_xattn_bv': _L0_xattn_in['bv'], 'L0_xattn_Wo': _L0_xattn_in['Wo'], 'L0_xattn_bo': _L0_xattn_in['bo'], 'L0_attn_Wq': _L0_attn_in['Wq'], 'L0_attn_Wk': _L0_attn_in['Wk'], 'L0_attn_Wv': _L0_attn_in['Wv'], 'L0_attn_gate_w': _L0_attn_in['gate_w'], 'L0_attn_gate_b': _L0_attn_in['gate_b'], 'L0_attn_p_w': _L0_attn_in['p_w'], 'L0_attn_p_b': _L0_attn_in['p_b'], 'L0_attn_out_w': _L0_attn_in['out_w'], 'L0_attn_out_b': _L0_attn_in['out_b'], 'L0_attn_clock_w': _L0_attn_in['clock_w'], 'L0_attn_clock_b': _L0_attn_in['clock_b'], 'L0_attn_ln1_g': _L0_attn_in['ln1_g'], 'L0_attn_ln1_b': _L0_attn_in['ln1_b'], 'L0_attn_ln2_g': _L0_attn_in['ln2_g'], 'L0_attn_ln2_b': _L0_attn_in['ln2_b'], 'L0_attn_mlp_w1': _L0_attn_in['mlp_w1'], 'L0_attn_mlp_b1': _L0_attn_in['mlp_b1'], 'L0_attn_mlp_w2': _L0_attn_in['mlp_w2'], 'L0_attn_mlp_b2': _L0_attn_in['mlp_b2'], 'L0_ffn_Wg': _L0_ffn_in['Wg'], 'L0_ffn_bg': _L0_ffn_in['bg'], 'L0_ffn_Wu': _L0_ffn_in['Wu'], 'L0_ffn_bu': _L0_ffn_in['bu'], 'L0_ffn_Wd': _L0_ffn_in['Wd'], 'L0_ffn_bd': _L0_ffn_in['bd'], 'L0_ffn_Wq': _L0_ffn_in['Wq'], 'L0_ffn_keys': _L0_ffn_in['keys'], 'L0_ffn_down_embed': _L0_ffn_in['down_embed'], 'L0_ffn_up_embed': _L0_ffn_in['up_embed'], 'L1_xattn_ln_g': _L1_xattn_in['ln_g'], 'L1_xattn_ln_b': _L1_xattn_in['ln_b'], 'L1_xattn_Wq': _L1_xattn_in['Wq'], 'L1_xattn_Wkv': _L1_xattn_in['Wkv'], 'L1_xattn_Wm': _L1_xattn_in['Wm'], 'L1_xattn_Wo': _L1_xattn_in['Wo'], 'L1_xattn_bo': _L1_xattn_in['bo'], 'L1_attn_A': _L1_attn_in['A'], 'L1_attn_Wb': _L1_attn_in['Wb'], 'L1_attn_bb': _L1_attn_in['bb'], 'L1_attn_Wc': _L1_attn_in['Wc'], 'L1_attn_bc': _L1_attn_in['bc'], 'L1_attn_Wd': _L1_attn_in['Wd'], 'L1_attn_bd': _L1_attn_in['bd'], 'L1_attn_Wdelta': _L1_attn_in['Wdelta'], 'L1_attn_bdelta': _L1_attn_in['bdelta'], 'L1_ffn_fast_b': _L1_ffn_in['fast_b'], 'L1_ffn_w_fc': _L1_ffn_in['w_fc'], 'L1_ffn_w_proj': _L1_ffn_in['w_proj'], 'L1_ffn_u': _L1_ffn_in['u'], 'L1_ffn_v': _L1_ffn_in['v'], 'L1_ffn_gate': _L1_ffn_in['gate']}

def reference(x, ctx_1024, L0_xattn_Wq, L0_xattn_bq, L0_xattn_Wk, L0_xattn_bk, L0_xattn_Wv, L0_xattn_bv, L0_xattn_Wo, L0_xattn_bo, L0_attn_Wq, L0_attn_Wk, L0_attn_Wv, L0_attn_gate_w, L0_attn_gate_b, L0_attn_p_w, L0_attn_p_b, L0_attn_out_w, L0_attn_out_b, L0_attn_clock_w, L0_attn_clock_b, L0_attn_ln1_g, L0_attn_ln1_b, L0_attn_ln2_g, L0_attn_ln2_b, L0_attn_mlp_w1, L0_attn_mlp_b1, L0_attn_mlp_w2, L0_attn_mlp_b2, L0_ffn_Wg, L0_ffn_bg, L0_ffn_Wu, L0_ffn_bu, L0_ffn_Wd, L0_ffn_bd, L0_ffn_Wq, L0_ffn_keys, L0_ffn_down_embed, L0_ffn_up_embed, L1_xattn_ln_g, L1_xattn_ln_b, L1_xattn_Wq, L1_xattn_Wkv, L1_xattn_Wm, L1_xattn_Wo, L1_xattn_bo, L1_attn_A, L1_attn_Wb, L1_attn_bb, L1_attn_Wc, L1_attn_bc, L1_attn_Wd, L1_attn_bd, L1_attn_Wdelta, L1_attn_bdelta, L1_ffn_fast_b, L1_ffn_w_fc, L1_ffn_w_proj, L1_ffn_u, L1_ffn_v, L1_ffn_gate):
    import jax
    import jax.numpy as jnp

    def _L0_xattn_ref(queries, keys, values, Wq, bq, Wk, bk, Wv, bv, Wo, bo):
        import math
        import jax, jax.numpy as jnp
        import numpy as np
        H = 16
        D_MODEL = 512
        DK = D_MODEL // H
        K_FACTOR = 2

        def _time_delay_agg_inference(v, corr):
            B, _, _, L = v.shape
            top_k = min(int(K_FACTOR * math.log(L)), L)
            mean_value = jnp.mean(corr, axis=(1, 2))
            weights, delay = jax.lax.top_k(mean_value, top_k)
            tmp_corr = jax.nn.softmax(weights, axis=-1)
            idx = (delay[:, :, None] + jnp.arange(L)) % L
            gathered = jnp.take_along_axis(v[:, None], idx[:, :, None, None, :], axis=-1)
            return jnp.einsum('bk,bkhdl->bhdl', tmp_corr, gathered)
        B, Lq, _ = queries.shape
        Lk = keys.shape[1]
        q = (queries @ Wq + bq).reshape(B, Lq, H, DK)
        k = (keys @ Wk + bk).reshape(B, Lk, H, DK)
        v = (values @ Wv + bv).reshape(B, Lk, H, DK)
        if Lq > Lk:
            pad = ((0, 0), (0, Lq - Lk), (0, 0), (0, 0))
            k = jnp.pad(k, pad)
            v = jnp.pad(v, pad)
        else:
            k = k[:, :Lq]
            v = v[:, :Lq]
        qt = jnp.transpose(q, (0, 2, 3, 1))
        kt = jnp.transpose(k, (0, 2, 3, 1))
        vt = jnp.transpose(v, (0, 2, 3, 1))
        qf = jnp.fft.rfft(qt)
        kf = jnp.fft.rfft(kt)
        c = qf.real * kf.real + 1j * -(qf.imag * kf.imag)
        corr = jnp.fft.irfft(c, n=Lq).astype(qt.dtype)
        agg = _time_delay_agg_inference(vt, corr)
        out = jnp.transpose(agg, (0, 3, 1, 2)).reshape(B, Lq, H * DK)
        return out @ Wo + bo

    def _L0_attn_ref(x, Wq, Wk, Wv, gate_w, gate_b, p_w, p_b, out_w, out_b, clock_w, clock_b, ln1_g, ln1_b, ln2_g, ln2_b, mlp_w1, mlp_b1, mlp_w2, mlp_b2):
        import math
        import jax, jax.numpy as jnp
        import numpy as np
        D_MODEL = 512
        N_HEAD = 16
        HEAD_DIM = D_MODEL // N_HEAD
        B, T = (2, 1024)

        def _layernorm(x, g, b, eps=1e-05):
            mu = jnp.mean(x, axis=-1, keepdims=True)
            var = jnp.mean(jnp.square(x - mu), axis=-1, keepdims=True)
            return (x - mu) * jax.lax.rsqrt(var + eps) * g + b

        def _l2norm(x, eps=1e-12):
            n = jnp.sqrt(jnp.sum(jnp.square(x), axis=-1, keepdims=True))
            return x / jnp.maximum(n, eps)

        def _rope(x, times):
            half = x.shape[-1] // 2
            freqs = jnp.exp(-jnp.arange(half, dtype=x.dtype) * (math.log(10000.0) / half))
            theta = times[:, None] * freqs[None, :]
            cos = jnp.cos(theta)[None, :, None, :]
            sin = jnp.sin(theta)[None, :, None, :]
            xr = x.reshape(*x.shape[:-1], half, 2)
            x1, x2 = (xr[..., 0], xr[..., 1])
            r1 = x1 * cos - x2 * sin
            r2 = x1 * sin + x2 * cos
            return jnp.stack([r1, r2], axis=-1).reshape(x.shape)
        Bx, Tx, D = x.shape
        H, Dh = (N_HEAD, HEAD_DIM)
        residual = x
        xn = _layernorm(x, ln1_g, ln1_b)
        times = jnp.arange(Tx, dtype=x.dtype)
        q = _l2norm((xn @ Wq).reshape(Bx, Tx, H, Dh))
        k = _l2norm((xn @ Wk).reshape(Bx, Tx, H, Dh))
        v = (xn @ Wv).reshape(Bx, Tx, H, Dh)
        clock = jax.nn.softplus(xn @ clock_w + clock_b).reshape(Bx, Tx, H, 1)
        q = _rope(q, times)
        k = _rope(k, times)
        gj = -jax.nn.softplus(xn @ gate_w + gate_b).reshape(Bx, Tx, H, Dh)
        gcp = jnp.exp(jnp.clip(jnp.cumsum(gj, axis=1), -60.0, 50.0))
        q = q * gcp
        k = k / (gcp + 1e-08)
        p = (xn @ p_w + p_b).reshape(Bx, Tx, H, Dh)
        p_max = jnp.max(p, axis=1, keepdims=True)
        p_exp = jnp.exp(p - p_max) * clock
        p_cs = jnp.cumsum(p_exp, axis=1)
        q = q / (p_cs + 1e-08)
        k = k * p_exp
        scores = jnp.einsum('bqhd,bkhd->bhqk', q, k) / math.sqrt(Dh)
        mask = jnp.tril(jnp.ones((Tx, Tx), dtype=bool))
        scores = jnp.where(mask[None, None], scores, -jnp.inf)
        attn = jax.nn.softmax(scores, axis=-1)
        out = jnp.einsum('bhqk,bkhd->bqhd', attn, v).reshape(Bx, Tx, D)
        out = out @ out_w + out_b
        x1 = out + residual
        h = _layernorm(x1, ln2_g, ln2_b)
        h = jax.nn.gelu(h @ mlp_w1 + mlp_b1, approximate=False) @ mlp_w2 + mlp_b2
        return x1 + h

    def _L0_ffn_ref(hidden_states, Wg, bg, Wu, bu, Wd, bd, Wq, keys, down_embed, up_embed):
        import jax, jax.numpy as jnp
        import numpy as np
        B, T, D = (2, 1024, 512)
        DCD = 2048
        RET = 128
        NEXP = 2048
        NKEYS = 64
        H = 4
        KPH = 8
        b, t, d = hidden_states.shape
        q = (hidden_states @ Wq).reshape(b, t, 2, H, RET // 2)
        sim = jnp.einsum('btphn,hkpn->pbthk', q, keys)
        sc, ix = jax.lax.top_k(sim, KPH)
        sx, sy = (sc[0], sc[1])
        ixx, ixy = (ix[0], ix[1])
        all_sc = (sx[..., :, None] + sy[..., None, :]).reshape(b, t, H, KPH * KPH)
        all_ix = (ixx[..., :, None] * NKEYS + ixy[..., None, :]).reshape(b, t, H, KPH * KPH)
        scores, pk = jax.lax.top_k(all_sc, KPH)
        idx = jnp.take_along_axis(all_ix, pk, axis=-1)
        de = down_embed[idx]
        ue = up_embed[idx]
        w = jnp.einsum('btd,bthkd->bthk', hidden_states, de)
        w = jax.nn.silu(w) * jax.nn.softmax(scores, axis=-1)
        experts_states = jnp.einsum('bthk,bthkd->btd', w, ue)
        mlp = jax.nn.silu(hidden_states @ Wg + bg) * (hidden_states @ Wu + bu) @ Wd + bd
        return mlp + experts_states

    def _L1_xattn_ref(x, memories, ln_g, ln_b, Wq, Wkv, Wm, Wo, bo):
        import jax, jax.numpy as jnp
        import numpy as np
        DIM = 512
        HEADS = 16
        DIM_HEAD = 64
        INNER = HEADS * DIM_HEAD
        EPS = 1e-05

        def _split_heads(t):
            b, n, _ = t.shape
            return t.reshape(b, n, HEADS, DIM_HEAD).transpose(0, 2, 1, 3)
        mu = jnp.mean(x, axis=-1, keepdims=True)
        var = jnp.mean(jnp.square(x - mu), axis=-1, keepdims=True)
        xn = (x - mu) * jax.lax.rsqrt(var + EPS) * ln_g + ln_b
        q = _split_heads(xn @ Wq)
        kv = xn @ Wkv
        k = _split_heads(kv[..., :INNER])
        v = _split_heads(kv[..., INNER:])
        mem = _split_heads(memories @ Wm)
        k = jnp.concatenate([k, mem], axis=2)
        v = jnp.concatenate([v, mem], axis=2)
        scale = DIM_HEAD ** (-0.5)
        dots = jnp.einsum('bhid,bhjd->bhij', q, k) * scale
        attn = jax.nn.softmax(dots, axis=-1)
        out = jnp.einsum('bhij,bhjd->bhid', attn, v)
        b, h, n, d = out.shape
        out = out.transpose(0, 2, 1, 3).reshape(b, n, h * d)
        return out @ Wo + bo

    def _L1_attn_ref(x, A, Wb, bb, Wc, bc, Wd, bd, Wdelta, bdelta):
        import jax, jax.numpy as jnp
        import numpy as np
        D_MODEL = 512
        D_HIDDEN = 128
        delta = jax.nn.softplus(jnp.einsum('btc,ch->bth', x, Wdelta) + bdelta)
        A_log = -jax.nn.softplus(A)
        A_bar_log = delta * A_log
        B_bar = delta * (jnp.einsum('btc,ch->bth', x, Wb) + bb)
        A_log_cum = jnp.clip(jnp.cumsum(A_bar_log, axis=1), -20.0, 20.0)
        A_log_cum_shifted = jnp.concatenate([jnp.zeros_like(A_log_cum[:, :1, :]), A_log_cum[:, :-1, :]], axis=1)
        B_shift = B_bar * jnp.exp(-A_log_cum_shifted)
        h = jnp.exp(A_log_cum) * jnp.cumsum(B_shift, axis=1)
        out = jnp.einsum('bth,hc->btc', h, Wc) + bc + jnp.einsum('btc,cd->btd', x, Wd) + bd
        return out

    def _L1_ffn_ref(x, fast_b, w_fc, w_proj, u, v, gate):
        import jax, jax.numpy as jnp
        import numpy as np

        def _bitlinear(x, w_latent):
            scale = jax.lax.stop_gradient(jnp.clip(jnp.mean(jnp.abs(w_latent), axis=1, keepdims=True), 1e-05, None))
            tern = jnp.clip(jnp.round(w_latent / scale), -1.0, 1.0)
            w = w_latent + jax.lax.stop_gradient(tern - w_latent)
            return x @ (w * scale).T
        h = _bitlinear(x, w_fc) + gate * (x @ v.T @ fast_b.T @ u.T)
        r = jnp.maximum(h, 0.0)
        return _bitlinear(r * r, w_proj)
    x = x + _L0_xattn_ref(_layernorm(x, axis=-1), ctx_1024, ctx_1024, L0_xattn_Wq, L0_xattn_bq, L0_xattn_Wk, L0_xattn_bk, L0_xattn_Wv, L0_xattn_bv, L0_xattn_Wo, L0_xattn_bo)
    x = x + _L0_attn_ref(_layernorm(x, axis=-1), L0_attn_Wq, L0_attn_Wk, L0_attn_Wv, L0_attn_gate_w, L0_attn_gate_b, L0_attn_p_w, L0_attn_p_b, L0_attn_out_w, L0_attn_out_b, L0_attn_clock_w, L0_attn_clock_b, L0_attn_ln1_g, L0_attn_ln1_b, L0_attn_ln2_g, L0_attn_ln2_b, L0_attn_mlp_w1, L0_attn_mlp_b1, L0_attn_mlp_w2, L0_attn_mlp_b2)
    x = x + _L0_ffn_ref(_layernorm(x, axis=-1), L0_ffn_Wg, L0_ffn_bg, L0_ffn_Wu, L0_ffn_bu, L0_ffn_Wd, L0_ffn_bd, L0_ffn_Wq, L0_ffn_keys, L0_ffn_down_embed, L0_ffn_up_embed)
    x = x + _L1_xattn_ref(_layernorm(x, axis=-1), ctx_1024, L1_xattn_ln_g, L1_xattn_ln_b, L1_xattn_Wq, L1_xattn_Wkv, L1_xattn_Wm, L1_xattn_Wo, L1_xattn_bo)
    x = x + _L1_attn_ref(_layernorm(x, axis=-1), L1_attn_A, L1_attn_Wb, L1_attn_bb, L1_attn_Wc, L1_attn_bc, L1_attn_Wd, L1_attn_bd, L1_attn_Wdelta, L1_attn_bdelta)
    x = x + _L1_ffn_ref(_layernorm(x, axis=-1), L1_ffn_fast_b, L1_ffn_w_fc, L1_ffn_w_proj, L1_ffn_u, L1_ffn_v, L1_ffn_gate)
    return x

_drawn_inputs = setup_inputs


def setup_inputs(seed=0):
    import zlib

    import numpy as np

    out = dict(_drawn_inputs(seed))
    spreads = {'L0_xattn_bq': (0.0, 0.8),
     'L0_xattn_bk': (0.0, 0.8),
     'L0_xattn_bv': (0.0, 0.1),
     'L0_xattn_bo': (0.0, 0.1),
     'L0_attn_gate_b': (0.0, 0.8),
     'L0_attn_p_b': (0.0, 0.8),
     'L0_attn_out_b': (0.0, 0.1),
     'L0_attn_clock_b': (0.0, 0.8),
     'L0_attn_ln1_g': (1.0, 0.6),
     'L0_attn_ln1_b': (0.0, 0.611),
     'L0_attn_ln2_g': (1.0, 0.6),
     'L0_attn_ln2_b': (0.0, 0.624),
     'L0_attn_mlp_b1': (0.0, 0.285),
     'L0_attn_mlp_b2': (0.0, 0.1),
     'L0_ffn_bg': (0.0, 0.8),
     'L0_ffn_bu': (0.0, 0.8),
     'L0_ffn_bd': (0.0, 0.1),
     'L1_xattn_ln_g': (1.0, 0.2),
     'L1_xattn_ln_b': (0.0, 0.31),
     'L1_xattn_bo': (0.0, 0.1)}
    factors = {'L0_attn_Wq': 8.0,
     'L0_attn_Wk': 8.0,
     'L0_attn_gate_w': 8.0,
     'L0_attn_p_w': 8.0,
     'L0_attn_clock_w': 8.0,
     'L0_ffn_Wq': 8.0,
     'L0_ffn_keys': 8.0,
     'L0_ffn_down_embed': 8.0,
     'L0_ffn_up_embed': 8.0,
     'L1_attn_bc': 3.485,
     'L1_attn_bd': 6.786,
     'L1_attn_bdelta': 3.304,
     'L1_ffn_fast_b': 8.0,
     'L1_ffn_u': 8.0,
     'L1_ffn_v': 8.0}
    for name, (base, spread) in spreads.items():
        noise = np.random.default_rng([zlib.crc32(name.encode()), seed]).standard_normal(out[name].shape)
        drawn = base * np.exp(spread * noise) if base else spread * noise
        out[name] = jnp.asarray(drawn.astype(out[name].dtype))
    for name, factor in factors.items():
        out[name] = (out[name] * factor).astype(out[name].dtype)
    return out
```

```python
import numpy as np
import concourse.bass as bass
from concourse import mybir
from contextlib import ExitStack

B, L, D = 32, 32, 512
N = B * L
M = 257
KT_ = D // 128
TT = N // 128
C2 = N // 512
F = 2048
NQ = F // 512
TOPK = int(2 * np.log(L))
NKEYS, NEXP, PH = 64, 2048, 4
HD1, H1 = 64, 16
INNER = HD1 * H1
OT1 = INNER // 128
EPS = 1e-5



def constant_tables():
    p = np.arange(128)
    tabs = {}
    tabs["ident"] = np.eye(128)
    l = np.arange(32)
    f = np.concatenate([np.arange(17), np.arange(1, 16)])
    ang = 2 * np.pi * np.outer(l, f) / 32
    base = np.where(np.arange(32)[None, :] < 17, np.cos(ang), np.sin(ang))
    tabs["dft"] = np.kron(np.eye(4), base)
    wf = np.where((f == 0) | (f == 16), 1.0, 2.0)
    tabs["corr"] = np.tile((base * wf[None, :]).T / (32 * 512), (4, 1))
    tabs["own_batch"] = (p[:, None] // 32 == np.arange(4)[None, :]) * 1.0
    tabs["head_ones"] = np.kron(np.eye(4), np.ones((32, 32)))
    rot = np.zeros((128, 128))
    for i in range(0, 128, 2):
        rot[i, i + 1] = -1.0
        rot[i + 1, i] = 1.0
    tabs["rot"] = rot.T
    fr = np.exp(-np.arange(16, dtype=np.float32) * np.float32(np.log(10000.0) / 16))
    th = (np.arange(32, dtype=np.float32)[None, :] * fr[:, None]).astype(np.float32)
    tabs["cos"] = np.cos(th)[(p % 32) // 2]
    tabs["sin"] = np.sin(th)[(p % 32) // 2]
    ok = (p[:, None] // 32 == p[None, :] // 32) & (p[:, None] <= p[None, :])
    tabs["causal"] = np.where(ok, 0.0, -2.0 ** 99)
    tabs["mean_ones"] = np.full((128, 128), 1.0 / D)
    tabs["hid_ones"] = np.full((128, 128), 1.0 / F)
    tabs["ones"] = np.ones((128, 32))
    tabs["iota"] = np.tile(np.arange(64.0), (128, 1))
    tabs["rank"] = np.tile(8.0 - np.arange(8.0), (128, 1))
    dc = np.zeros((128, 128))
    dc[0, ::32] = 32.0
    tabs["dc"] = dc
    ex = np.zeros((128, 512))
    for c in range(512):
        ex[c // 32, c] = 1.0
    tabs["expand"] = ex
    tabs["eps"] = np.full((128, 1), EPS)
    tabs["eps2"] = np.full((128, 1), EPS * EPS)
    tabs["one"] = np.full((128, 1), 1.0)
    return {k: v.astype(np.float32) for k, v in tabs.items()}


TABLES = constant_tables()
TABLE_AT, at = {}, 0
for _k, _v in TABLES.items():
    TABLE_AT[_k] = (at, _v.shape[1])
    at += _v.shape[1]
TABLE_COLS = at

COLUMNS = [("L0_xattn_bv", 4), ("L0_xattn_bo", 4), ("L0_attn_gate_b", 4), ("L0_attn_p_b", 4), ("L0_attn_out_b", 4),
           ("L0_attn_ln1_g", 4), ("L0_attn_ln1_b", 4), ("L0_attn_ln2_g", 4), ("L0_attn_ln2_b", 4),
           ("L0_attn_mlp_b1", 16), ("L0_attn_mlp_b2", 4), ("L0_ffn_bg", 16), ("L0_ffn_bu", 16), ("L0_ffn_bd", 4),
           ("L1_xattn_ln_g", 4), ("L1_xattn_ln_b", 4), ("L1_xattn_bo", 4), ("L1_attn_A", 1), ("L1_attn_bb", 1),
           ("L1_attn_bc", 4), ("L1_attn_bd", 4), ("L1_attn_bdelta", 1), ("clock_b", 1), ("gate", 1)]
COLUMN_AT, at = {}, 0
for _k, _n in COLUMNS:
    COLUMN_AT[_k] = at
    at += _n
COLUMN_COLS = at


def perceiver(nc, dram, out):
    f32 = mybir.dt.float32
    u32 = mybir.dt.uint32
    ACT = mybir.ActivationFunctionType
    ALU = mybir.AluOpType
    AX = mybir.AxisListType
    ctx = ExitStack()
    with ctx:
        def sb(name, shape, dt=f32):
            return ctx.enter_context(nc.sbuf_tensor(name, shape, dt))

        def sem(name):
            return ctx.enter_context(nc.semaphore(name))

        consts = sb("consts", [128, TABLE_COLS])
        cols = sb("cols", [128, COLUMN_COLS])

        def tab(name, rows=128):
            a, n = TABLE_AT[name]
            return consts[0:rows, a:a + n]

        def col(name, i=0, rows=128):
            a = COLUMN_AT[name] + i
            return cols[0:rows, a:a + 1]

        XT = sb("XT", [128, 4, N])
        Y = sb("Y", [128, 4, N])
        XN = sb("XN", [128, 4, N])
        H = sb("H", [128, 2, 4, N])
        arena = sb("arena", [128, 6, 4, 512])
        RN = 17640
        R = sb("R", [128, RN])
        small = sb("small", [128, 64])
        ident_r = sb("ident_r", [128, 128], mybir.dt.float32r)
        causal_r = sb("causal_r", [128, 128], mybir.dt.float32r)

        def region(spec, base=R, limit=RN):
            got, at = {}, 0
            for name, shape in spec:
                n = int(np.prod(shape))
                ap = base[:, at:at + n]
                if len(shape) == 2:
                    ap = ap.rearrange("p (a b) -> p a b", a=shape[0])
                elif len(shape) == 3:
                    ap = ap.rearrange("p (a b c) -> p a b c", a=shape[0], b=shape[1])
                got[name] = ap
                at += n
            assert at <= limit, (at, limit)
            return got

        banks = [ctx.enter_context(nc.psum_tensor(f"bank{i}", [128, 512], f32)) for i in range(8)]

        act_bank_full, act_bank_free = sem("act_bank_full"), sem("act_bank_free")
        dve_bank_full, dve_bank_free = sem("dve_bank_full"), sem("dve_bank_free")
        slot_full = [sem(f"slot_full{i}") for i in range(6)]
        stage_done = sem("stage_done")
        act_step, dve_step, pool_step = sem("act_step"), sem("dve_step"), sem("pool_step")
        in_consts, in_xT, in_xtm, in_ctx32 = sem("in_consts"), sem("in_xT"), sem("in_xtm"), sem("in_ctx32")
        in_small = sem("in_small")
        xn_tile = sem("xn_tile")
        a_std, a_var = sem("a_std"), sem("a_var")
        cx_ready, top_ready, topexp_ready = sem("cx_ready"), sem("top_ready"), sem("topexp_ready")
        w_ready, w_stored, m_loaded, mt_ready, m_zero = (sem("w_ready"), sem("w_stored"), sem("m_loaded"),
                                                         sem("mt_ready"), sem("m_zero"))
        ln_sq, ln_out = sem("ln_sq"), sem("ln_out")
        out_stored = sem("out_stored")
        S = {n: sem(n) for n in (
            "b_ckln", "b_clock", "b_gsp", "b_gcs", "b_gcp", "b_pdif", "b_pexp", "b_sq", "b_qk", "b_cos",
            "c_topin", "c_topexp", "c_p", "c_kb", "c_fac", "c_dense", "c_ee", "c_mul",
            "d_self", "d_qbd", "d_max", "d_ct0", "d_ct1", "d_ct256", "d_probn",
            "e_a", "e_sp", "e_cum", "e_shift", "e_exp", "e_hh", "f_abs", "f_wp", "f_wf")}

        class Units:

            def __init__(self, banks):
                self.banks, self.at, self.n = banks, {}, 0

            def new(self, key):
                assert key not in self.at, key
                self.at[key] = self.n
                self.n += 1
                return self.n - 1

        UA, UV = Units(banks[0:4]), Units(banks[4:8])

        loads, slot_of, load_no, uses = [], {}, {}, [0] * 6
        turn = [0]

        def plan(name, src, slots=None):
            if slots is None:
                s = turn[0] % 6
                turn[0] += 1
            else:
                s = slots
            uses[s] += 1
            slot_of[name], load_no[name] = s, uses[s]
            loads.append((name, s, src))

        def rows4(w, r0=0, c0=0, nc_=512):
            return dram[w][r0:r0 + 512, c0:c0 + nc_].rearrange("(k p) n -> p k n", p=128)

        for n_, w in (("aq", "L0_xattn_Wq"), ("ak", "L0_xattn_Wk"), ("av", "L0_xattn_Wv"), ("ao", "L0_xattn_Wo"),
                      ("bv", "L0_attn_Wv"), ("bq", "L0_attn_Wq"), ("bk", "L0_attn_Wk"), ("bg", "L0_attn_gate_w"),
                      ("bp", "L0_attn_p_w"), ("bo", "L0_attn_out_w")):
            plan(n_, rows4(w))

        def quarters(up, down):
            for j in range(NQ):
                up(j)
                if j:
                    down(j - 1)
            down(NQ - 1)

        quarters(lambda j: plan(("b1", j), rows4("L0_attn_mlp_w1", 0, 512 * j)),
                 lambda j: plan(("b2", j), rows4("L0_attn_mlp_w2", 512 * j)))
        plan("cq", rows4("L0_ffn_Wq"))

        def plan_gu(j):
            plan(("cg", j), rows4("L0_ffn_Wg", 0, 512 * j))
            plan(("cu", j), rows4("L0_ffn_Wu", 0, 512 * j))

        quarters(plan_gu, lambda j: plan(("cd", j), rows4("L0_ffn_Wd", 512 * j)))
        for j in range(-1, NQ + 1):
            if j + 1 < NQ:
                plan(("ce", j + 1), rows4("downT", 0, 512 * j + 512))
            if j >= 1:
                plan(("cf", j - 1), rows4("L0_ffn_up_embed", 512 * j - 512))
        D_FIRST = len(loads)
        for h in range(2):
            plan(("dm", h), rows4("L1_xattn_Wm", 0, 512 * h), 4 + h)
        for cc in range(2):
            for w, src, off in (("dq", "L1_xattn_Wq", 0), ("dk", "L1_xattn_Wkv", 0), ("dv", "L1_xattn_Wkv", INNER)):
                for h in range(2):
                    plan((w, cc, h), rows4(src, 0, off + 512 * h), h)
            for h in range(2):
                plan(("dw", cc, h), rows4("L1_xattn_Wo", 512 * h), h)
        E_FIRST = len(loads)
        turn[0] = 0
        plan("edb", dram["L1_delta_b"].rearrange("(k p) n -> p k n", p=128))
        plan("ed", rows4("L1_attn_Wd"))
        for j in range(NQ):
            plan(("fp", j), rows4("w_projT", 512 * j))
        for j in range(NQ):
            plan(("ff", j), rows4("w_fcT", 0, 512 * j))
        released = {}

        def W(name):
            return arena[:, slot_of[name], :, :]

        RA = region([("m", (TT, 128)), ("mt", (TT, 128)), ("qs", (2, 512)), ("junk", (1, 512)), ("C", (1, 8)), ("cx", (8, 4)),
                     ("st", (8, 6)), ("mv", (8, 2)), ("cr", (1, 32)), ("v8", (1, 8)), ("i8", (1, 8)), ("e8", (1, 8)),
                     ("fi8", (1, 8)),
                     ("eq", (6, 32)), ("w2", (2, 32)), ("bq", (1, 512)), ("bk", (1, 512))])
        xtm, ctm = XN[:, :, :].rearrange("p a b -> p (a b)").rearrange("p (t d) -> p t d", t=8), \
            Y[:, :, :].rearrange("p a b -> p (a b)").rearrange("p (t d) -> p t d", t=8)
        LQ, LK = H[:, 0], H[:, 1]
        RL = region([("sq", (2, 2048)), ("r1", (2, 512)), ("r2", (2, 512))])
        RB = region([("v", (8, 512)), ("ot", (4, N)), ("reset", (1, N)), ("ck", (1, N)), ("p", (8, 512)), ("p2", (1, N)),
                     ("cw", (4, 16)), ("t", (2, N)), ("pm", (1, 32)), ("den", (1, 128))])
        RC = region([("sim", (8, 512)), ("kb", (4, 128)), ("Tx", (8, PH, 32)), ("Ex", (8, PH, 32)), ("Ry", (8, PH, 64)),
                     ("Ey", (8, PH, 64)), ("eq", (1, 2048)), ("s", (4, 512)), ("xv", (1, 8)),
                     ("pj", (2, 512))])
        XNf = XN[:, :, :].rearrange("p a b -> p (a b)")
        SJ = [H[:, 0], H[:, 1], XN]
        XNf = XN[:, :, :].rearrange("p a b -> p (a b)")
        RT = region([("tv", (8, 8)), ("ti", (8, 8)), ("tf", (2, 8, 8)), ("cand", (PH, 64)), ("rep", (PH, 64)), ("t8", (PH, 8)),
                     ("na", (2, PH, 8)), ("z", (1, 4)), ("rz", (1, 4)), ("m0", (1, 4)), ("ge", (PH, 8)),
                     ("rs", (PH, 8)), ("sd", (8, 64)), ("sel", (PH, 64))], base=XNf, limit=4096)
        RD = region([("kt", (8, 2, 322)), ("vt", (2, 3, 1024)), ("ct", (2, 4, 514)), ("m256", (8, 32)), ("c256", (4, 32)), ("qbd", (2, 512))])
        RDa = region([("p", (8, 289)), ("pt", (4, 384))],
                     base=arena[:, 2:4, :, :].rearrange("p s a b -> p (s a b)"), limit=4096)
        gate_buf, p_buf = [H[:, 1, 0, :], H[:, 1, 3, :]], [H[:, 1, 1, :], RB["p2"][:, 0, :]]
        EE = RC["sim"].rearrange("p t n -> p (t n)").rearrange("p (i n) -> p i n", i=2)
        kt = RD["kt"]
        qbd = [RD["qbd"][:, i].rearrange("p (o c) -> p o c", o=8) for i in range(2)]
        ct = [RD["ct"][:, i].rearrange("p k (b m) -> p k b m", b=2) for i in range(2)]
        Q1 = Y[:, :, :].rearrange("p a b -> p (a b)").rearrange("p (o t) -> p o t", o=8)
        K1 = H[:, 0].rearrange("p a b -> p (a b)").rearrange("p (o t) -> p o t", o=8)
        V1 = H[:, 1].rearrange("p a b -> p (a b)").rearrange("p (o t) -> p o t", o=8)
        RE = region([("dl", (1, N)), ("bb", (1, N)), ("z", (2, N)), ("t", (2, N)), ("reset", (1, N)), ("hh", (1, N)),
                     ("wc", (1, 512)), ("sh", (B, L))])
        RF = region([("wp", (16, 512)), ("vT", (4, 16)), ("fb", (1, 16)), ("uT", (1, F)), ("z", (1, N)), ("z2", (1, N)),
                     ("half", (1, 512)), ("s", (1, 512)), ("sp", (1, 512)), ("r", (2, 512)), ("tn", (1, 2048))])
        wf = [XNf[:, 2048 * i:2048 * i + 2048].rearrange("p (k n) -> p k n", k=4) for i in range(2)]

        LNS = [dict(src=XT, dst=XN, double=True, plain=Y, g="L0_attn_ln1_g", b="L0_attn_ln1_b"),
               dict(src=Y, dst=XN, double=False, plain=None, g="L0_attn_ln2_g", b="L0_attn_ln2_b"),
               dict(src=XT, dst=Y, double=False, plain=None, g=None, b=None),
               dict(src=XT, dst=XN, double=True, plain=None, g="L1_xattn_ln_g", b="L1_xattn_ln_b"),
               dict(src=XT, dst=Y, double=False, plain=None, g=None, b=None),
               dict(src=XT, dst=Y, double=False, plain=None, g=None, b=None)]

        def ch(c):
            return slice(512 * c, 512 * c + 512)

        def tl(t):
            return slice(128 * t, 128 * t + 128)

        d_end = [0]
        block = ctx.enter_context(nc.Block())

        @block.tensor
        def _(pe):
            stage = [0]
            mm = nc.tensor.matmul

            def end_stage():
                stage[0] += 1
                pe.drain().then_inc(stage_done, 1)
                pe.wait_ge(stage_done, 4 * stage[0])

            def open_act(key):
                u = UA.new(key)
                if u >= 4:
                    pe.wait_ge(act_bank_free, u - 3)
                return UA.banks[u % 4]

            def open_dve(key):
                u = UV.new(key)
                if u >= 4:
                    pe.wait_ge(dve_bank_free, u - 3)
                return UV.banks[u % 4]

            def on_act(key):
                pe.wait_ge(act_bank_free, UA.at[key] + 1)

            def on_dve(key):
                pe.wait_ge(dve_bank_free, UV.at[key] + 1)

            def weight(name):
                pe.wait_ge(slot_full[slot_of[name]], 16 * load_no[name])

            def free_after_act(name):
                released[name] = (act_bank_full, UA.n)

            def free_after_dve(name):
                released[name] = (dve_bank_full, UV.n)

            def linear(bank, w, cols_, x, xc, more=False):
                for k in range(4):
                    last = mm(bank, w[:, k, cols_], x[:, k, xc], start=(k == 0), stop=(k == 3 and not more))
                return last

            def layernorm(l):
                for c in range(C2):
                    b = open_dve(("mean", l, c))
                    linear(b[:, :], tab("mean_ones").unsqueeze(1).to_broadcast([128, 4, 128]), slice(0, 128), LNS[l]["src"], ch(c)
                           ).then_inc(dve_bank_full, 1)
                for c in range(C2):
                    pe.wait_ge(ln_sq, 2 * l + c + 1)
                    b = open_act(("var", l, c))
                    sq = RL["sq"][:, c].rearrange("p (k n) -> p k n", k=4)
                    linear(b[:, :], tab("mean_ones").unsqueeze(1).to_broadcast([128, 4, 128]), slice(0, 128), sq, slice(0, 512)
                           ).then_inc(act_bank_full, 1)
                end_stage()

            pe.wait_ge(in_consts, 32)
            pe.wait_ge(in_small, 32)
            pe.wait_ge(in_ctx32, 64)
            for t in range(TT):
                b = open_act(("ldk", t))
                for k in range(4):
                    last = mm(b[:, tl(k)], ctm[:, t, tl(k)], tab("dft"), start=True, stop=True)
                last.then_inc(act_bank_full, 1)
            for t in range(TT):
                pe.wait_ge(xn_tile, t + 1)
                b = open_dve(("ldq", t))
                for k in range(4):
                    last = mm(b[:, tl(k)], xtm[:, t, tl(k)], tab("dft"), start=True, stop=True)
                last.then_inc(dve_bank_full, 1)
            weight("aq")
            weight("ak")
            for t in range(TT):
                on_dve(("ldq", t))
                b = open_act(("qf", t))
                for k in range(4):
                    mm(b[:, :], LQ[:, k, tl(t)], W("aq")[:, k, :], start=(k == 0), stop=False)
                mm(b[:, :], tab("dc", 1), RA["bq"][0:1, 0, :], start=False, stop=True).then_inc(act_bank_full, 1)
                on_act(("ldk", t))
                b = open_dve(("kf", t))
                for k in range(4):
                    mm(b[:, :], LK[:, k, tl(t)], W("ak")[:, k, :], start=(k == 0), stop=False)
                mm(b[:, :], tab("dc", 1), RA["bk"][0:1, 0, :], start=False, stop=True).then_inc(dve_bank_full, 1)
            free_after_act("aq")
            free_after_dve("ak")
            pe.wait_ge(cx_ready, 1)
            b = open_dve("corr")
            mm(b[0:32, 0:32], RA["cx"].rearrange("p a b -> p (a b)"), tab("corr"), start=True, stop=True
               ).then_inc(dve_bank_full, 1)
            pe.wait_ge(mt_ready, 1)
            for t in range(TT):
                b = open_act(("agg", t))
                for k in range(4):
                    last = mm(b[:, tl(k)], ctm[:, t, tl(k)], RA["mt"][:, t, :], start=True, stop=True)
                last.then_inc(act_bank_full, 1)
            on_act(("agg", TT - 1))
            weight("av")
            for o in range(4):
                for c in range(C2):
                    b = open_act(("av", o, c))
                    linear(b[:, :], W("av"), tl(o), LQ, ch(c)).then_inc(act_bank_full, 1)
            free_after_act("av")
            on_act(("av", 3, C2 - 1))
            weight("ao")
            for o in range(4):
                for c in range(C2):
                    b = open_dve(("ao", o, c))
                    linear(b[:, :], W("ao"), tl(o), LK, ch(c)).then_inc(dve_bank_full, 1)
            free_after_dve("ao")
            end_stage()

            layernorm(0)
            pe.wait_ge(in_small, 48)
            for c in range(C2):
                b = open_act(("clock", c))
                for k in range(4):
                    last = mm(b[0:16, :], RB["cw"][:, k, :], XN[:, k, ch(c)], start=(k == 0), stop=(k == 3))
                last.then_inc(act_bank_full, 1)
            weight("bv")
            for t in range(TT):
                b = open_act(("v", t))
                for k in range(4):
                    last = mm(b[:, :], XN[:, k, tl(t)], W("bv")[:, k, :], start=(k == 0), stop=(k == 3))
                last.then_inc(act_bank_full, 1)
            free_after_act("bv")
            for w in ("bq", "bk", "bg", "bp"):
                weight(w)

            def project(o, names):
                for w in names:
                    for c in range(C2):
                        b = open_act((w, o, c))
                        linear(b[:, :], W(w), tl(o), XN, ch(c)).then_inc(act_bank_full, 1)

            def clock_norms_rotations(o):
                for c in range(C2):
                    pe.wait_ge(S["b_clock"], C2)
                    b = open_dve(("ck", o, c))
                    mm(b[:, :], tab("expand", 16)[:, tl(o)], RB["ck"][0:16, 0, ch(c)], start=True, stop=True
                       ).then_inc(dve_bank_full, 1)
                for i, w in enumerate(("bq", "bk")):
                    for c in range(C2):
                        on_act((w, o, c))
                        b = open_dve(("r" + w, o, c))
                        mm(b[:, :], tab("rot"), H[:, 0, i, ch(c)], start=True, stop=True).then_inc(dve_bank_full, 1)
                for i, w in enumerate(("bq", "bk")):
                    for c in range(C2):
                        pe.wait_ge(S["b_sq"], 4 * o + 2 * i + c + 1)
                        b = open_act(("n" + w, o, c))
                        mm(b[:, :], tab("head_ones"), H[:, 0, 2 + i, ch(c)], start=True, stop=True).then_inc(act_bank_full, 1)

            def scores(o):
                pe.wait_ge(S["b_qk"], 2 * (o + 1))
                for hf in range(2):
                    for h in range(4):
                        hp = slice(32 * h, 32 * h + 32)
                        b = open_act(("s", o, hf, h))
                        mm(b[:, :].rearrange("p (t n) -> p t n", t=4), ident_r[:, :],
                           causal_r[:, :].unsqueeze(1).to_broadcast([128, 4, 128]), start=True, stop=False)
                        for t in range(4):
                            tt = tl(4 * hf + t)
                            last = mm(b[:, tl(t)], H[hp, 0, 1, tt], H[hp, 0, 0, tt], start=False, stop=(t == 3),
                                      tile_position=(32 * h, 0))
                        last.then_inc(act_bank_full, 1)

            def values(o):
                for tt in range(TT):
                    on_act(("s", o, tt // 4, 3))
                    b = open_dve(("pv", o, tt))
                    for h in range(4):
                        hp = slice(32 * h, 32 * h + 32)
                        pt_ = RB["p"][:, 4 * (tt // 4) + h, tl(tt % 4)]
                        mm(b[hp, 0:128], RB["v"][:, tt, 128 * o + 32 * h:128 * o + 32 * h + 32], pt_,
                           start=True, stop=True, tile_position=(0, 32 * h))
                        last = mm(b[hp, 128:256], tab("ones"), pt_, start=True, stop=True, tile_position=(0, 32 * h))
                    last.then_inc(dve_bank_full, 1)

            project(0, ("bg", "bp", "bq", "bk"))
            clock_norms_rotations(0)
            for o in range(4):
                if o < 3:
                    project(o + 1, ("bg", "bp"))
                scores(o)
                if o < 3:
                    project(o + 1, ("bq", "bk"))
                    clock_norms_rotations(o + 1)
                values(o)
            for w in ("bq", "bk", "bg", "bp"):
                free_after_act(w)
            on_dve(("pv", 3, TT - 1))
            weight("bo")
            for o in range(4):
                for c in range(C2):
                    b = open_dve(("bo", o, c))
                    linear(b[:, :], W("bo"), tl(o), RB["ot"], ch(c)).then_inc(dve_bank_full, 1)
            free_after_dve("bo")
            end_stage()
            layernorm(1)

            def b_up(j):
                weight(("b1", j))
                for o in range(4):
                    for c in range(C2):
                        b = open_act(("b1", j, o, c))
                        linear(b[:, :], W(("b1", j)), tl(o), XN, ch(c)).then_inc(act_bank_full, 1)
                free_after_act(("b1", j))

            def down(name, j, ready):
                weight((name, j))
                ready(j)
                for o in range(4):
                    for c in range(C2):
                        b = open_dve((name, j, o, c))
                        linear(b[:, :], W((name, j)), tl(o), H[:, j % 2], ch(c)).then_inc(dve_bank_full, 1)
                free_after_dve((name, j))

            quarters(b_up, lambda j: down("b2", j, lambda j: on_act(("b1", j, 3, C2 - 1))))
            end_stage()

            layernorm(2)
            weight("cq")
            for o in range(4):
                for c in range(C2):
                    b = open_act(("cq", o, c))
                    linear(b[:, :], W("cq"), tl(o), Y, ch(c)).then_inc(act_bank_full, 1)
            free_after_act("cq")
            on_act(("cq", 3, C2 - 1))
            pe.wait_ge(S["c_kb"], 16)
            for t in range(TT):
                b = open_act(("sim", t))
                for j in range(4):
                    last = mm(b[:, tl(j)], XN[:, j, tl(t)], RC["kb"][:, j, :], start=True, stop=True)
                last.then_inc(act_bank_full, 1)

            def c_up(j):
                weight(("cg", j))
                weight(("cu", j))
                for o in range(4):
                    for c in range(C2):
                        b = open_act(("cg", j, o, c))
                        linear(b[:, :], W(("cg", j)), tl(o), Y, ch(c)).then_inc(act_bank_full, 1)
                        b = open_dve(("cu", j, o, c))
                        linear(b[:, :], W(("cu", j)), tl(o), Y, ch(c)).then_inc(dve_bank_full, 1)
                free_after_act(("cg", j))
                free_after_dve(("cu", j))

            quarters(c_up, lambda j: down("cd", j, lambda j: on_dve(("cu", j, 3, C2 - 1))))

            for j in range(-1, NQ + 1):
                if j + 1 < NQ:
                    weight(("ce", j + 1))
                if j >= 1:
                    weight(("cf", j - 1))
                for t in range(TT):
                    if j + 1 < NQ:
                        b = open_act(("ce", j + 1, t))
                        linear(b[:, :], W(("ce", j + 1)), tl(t % 4), Y, ch(t // 4)).then_inc(act_bank_full, 1)
                    if 0 <= j < NQ:
                        pe.wait_ge(S["c_p"], TT * j + t + 1)
                        b = open_dve(("pt", j, t))
                        for e in range(4):
                            last = nc.tensor.transpose(b[:, tl(e)], RC["pj"][:, t % 2, tl(e)], tab("ident"))
                        last.then_inc(dve_bank_full, 1)
                    if j >= 1:
                        if t == 0:
                            on_dve(("pt", j - 1, TT - 1))
                        b = open_dve(("cf", j - 1, t))
                        linear(b[:, :], W(("cf", j - 1)), tl(t % 4), SJ[(j - 1) % 3], ch(t // 4)).then_inc(dve_bank_full, 1)
                if j + 1 < NQ:
                    free_after_act(("ce", j + 1))
                if j >= 1:
                    free_after_dve(("cf", j - 1))
            end_stage()

            layernorm(3)

            def pv_group(b, bb, g):
                on_dve(("ptr", bb, g))
                if g == 0:
                    on_act(("vt", bb, 2, 1))
                    on_dve(("vt", bb, 2, 0))
                for x in range(2):
                    o = 2 * g + x
                    for blk, n in ((0, 128), (1, 128), (2, 33)):
                        last = mm(b[:, 64 * o:64 * o + 64], RD["vt"][0:n, bb % 2, blk, tl(o)],
                                  RDa["pt"][0:n, g, 128 * blk + 64 * x:128 * blk + 64 * x + 64],
                                  start=(blk == 0), stop=(blk == 2))
                return last

            pe.wait_ge(S["d_ct256"], 16)
            weight(("dm", 0))
            weight(("dm", 1))
            b = open_act("m256")
            for o in range(OT1):
                for k in range(4):
                    last = mm(b[:, 32 * o:32 * o + 32], W(("dm", o // 4))[:, k, tl(o % 4)], RD["c256"][:, k, :],
                              start=(k == 0), stop=(k == 3))
            last.then_inc(act_bank_full, 1)
            def memory(pr):
                pe.wait_ge(S[f"d_ct{pr % 2}"], 16 * (pr // 2 + 1))
                for o in range(OT1):
                    b = open_act(("mem", pr, o))
                    for k in range(4):
                        last = mm(b[:, :].rearrange("p (a c) -> p a c", a=2), W(("dm", o // 4))[:, k, tl(o % 4)],
                                  ct[pr % 2][:, k, :, 0:256], start=(k == 0), stop=(k == 3))
                    last.then_inc(act_bank_full, 1)

            memory(0)
            for cc in range(2):
                for w in ("dq", "dk", "dv"):
                    for o in range(OT1):
                        weight((w, cc, o // 4))
                        b = open_act((w, cc, o))
                        linear(b[:, :], W((w, cc, o // 4)), tl(o % 4), XN, ch(cc)).then_inc(act_bank_full, 1)
                        free_after_act((w, cc, o // 4))
                for pr in range(8 * cc, 8 * cc + 8):
                    on_act(("mem", pr, OT1 - 1))
                    for i in range(2):
                        bb = 2 * pr + i
                        pe.wait_ge(S["d_self"], bb + 1)
                        for blk, (a, n) in enumerate(((0, 128), (128, 128), (289, 33))):
                            for half, (open_, full) in enumerate(((open_dve, dve_bank_full), (open_act, act_bank_full))):
                                b = open_(("vt", bb, blk, half))
                                for o in range(4):
                                    last = nc.tensor.transpose(b[0:n, tl(o)], kt[:, 4 * half + o, i, a:a + n], tab("ident"))
                                last.then_inc(full, 1)
                        pe.wait_ge(S["d_qbd"], bb + 1)
                        for g in range(4):
                            b = open_act(("sc", bb, g))
                            for x in range(2):
                                last = mm(b[64 * x:64 * x + 64, 0:289], qbd[bb % 2][:, 2 * g + x, :],
                                          kt[:, 2 * g + x, i, 0:289], start=True, stop=True, tile_position=(0, 64 * x))
                            last.then_inc(act_bank_full, 1)
                    if pr + 1 < B // 2:
                        memory(pr + 1)
                    steps_ = [(2 * pr + i, g) for i in range(2) for g in range(4)]
                    for n_ in range(9):
                        if n_ < 8:
                            bb, g = steps_[n_]
                            pe.wait_ge(S["d_probn"], 4 * bb + g + 1)
                            pr_t = RDa["p"][:, 4 * (bb % 2) + g, :]
                            b = open_dve(("ptr", bb, g))
                            nc.tensor.transpose(b[:, 0:128], pr_t[:, 0:128], tab("ident"))
                            nc.tensor.transpose(b[:, 128:256], pr_t[:, 128:256], tab("ident"))
                            nc.tensor.transpose(b[0:33, 256:384], pr_t[:, 256:289], tab("ident")).then_inc(dve_bank_full, 1)
                        if n_:
                            bb, g = steps_[n_ - 1]
                            if g == 0:
                                bo_ = open_act(("pvd", bb))
                            last = pv_group(bo_, bb, g)
                            if g == 3:
                                last.then_inc(act_bank_full, 1)
                on_act(("pvd", 16 * cc + 15))
                for h in range(2):
                    weight(("dw", cc, h))
                for o in range(4):
                    b = open_dve(("dw", cc, o))
                    for k in range(8):
                        last = mm(b[:, :], W(("dw", cc, k // 4))[:, k % 4, tl(o)], Q1[:, k, :], start=(k == 0), stop=(k == 7))
                    last.then_inc(dve_bank_full, 1)
                for h in range(2):
                    free_after_dve(("dw", cc, h))
            for h in range(2):
                released[("dm", h)] = (stage_done, 4 * (stage[0] + 1))
            end_stage()
            d_end[0] = stage[0]

            layernorm(4)
            weight("edb")
            pe.wait_ge(in_small, 64)
            for c in range(C2):
                b = open_act(("dl", c))
                linear(b[:, :], W("edb"), slice(0, 128), Y, ch(c)).then_inc(act_bank_full, 1)
            for c in range(C2):
                b = open_dve(("bb", c))
                linear(b[:, :], W("edb"), slice(128, 256), Y, ch(c)).then_inc(dve_bank_full, 1)
            free_after_dve("edb")
            weight("ed")
            for o in range(4):
                for c in range(C2):
                    b = open_dve(("ed", o, c))
                    linear(b[:, :], W("ed"), tl(o), Y, ch(c), more=True)
                    pe.wait_ge(S["e_hh"], 1)
                    mm(b[:, :], RE["wc"][:, 0, tl(o)], RE["hh"][:, 0, ch(c)], start=False, stop=True).then_inc(dve_bank_full, 1)
            free_after_dve("ed")
            end_stage()

            layernorm(5)
            pe.wait_ge(in_small, 112)
            b = open_dve("fps")
            for j in range(NQ):
                pe.wait_ge(S["f_abs"], j + 1)
                for k in range(4):
                    last = mm(b[:, :], tab("hid_ones"), RF["wp"][:, 4 * j + k, :], start=(j == 0 and k == 0),
                              stop=(j == 3 and k == 3))
            last.then_inc(dve_bank_full, 1)
            for c in range(C2):
                b = open_act(("z", c))
                for k in range(4):
                    last = mm(b[0:16, :], RF["vT"][:, k, :], Y[:, k, ch(c)], start=(k == 0), stop=(k == 3))
                last.then_inc(act_bank_full, 1)
            for c in range(C2):
                on_act(("z", c))
                b = open_act(("z2", c))
                mm(b[0:16, :], RF["fb"][0:16, 0, :], RF["z"][0:16, 0, ch(c)], start=True, stop=True).then_inc(act_bank_full, 1)

            def f_scale(j):
                pe.wait_ge(S["f_abs"], NQ + j + 1)
                b = open_dve(("fs", j))
                for k in range(4):
                    last = mm(b[:, :], tab("mean_ones"), wf[j % 2][:, k, :], start=(k == 0), stop=(k == 3))
                last.then_inc(dve_bank_full, 1)

            def f_up(j):
                if j + 1 < NQ:
                    f_scale(j + 1)
                pe.wait_ge(S["f_wf"], j + 1)
                for o in range(4):
                    for c in range(C2):
                        b = open_act(("ff", j, o, c))
                        if j == 0 and o == 0:
                            on_act(("z2", c))
                        linear(b[:, :], wf[j % 2], tl(o), Y, ch(c), more=True)
                        mm(b[:, :], RF["uT"][0:16, 0, 512 * j + 128 * o:512 * j + 128 * o + 128], RF["z2"][0:16, 0, ch(c)],
                           start=False, stop=True).then_inc(act_bank_full, 1)

            f_scale(0)

            def f_down(j):
                on_act(("ff", j, 3, C2 - 1))
                pe.wait_ge(S["f_wp"], NQ)
                for o in range(4):
                    for c in range(C2):
                        b = open_dve(("fp", j, o, c))
                        linear(b[:, :], RF["wp"][:, 4 * j:4 * j + 4, :], tl(o), H[:, j % 2], ch(c)).then_inc(dve_bank_full, 1)

            quarters(f_up, f_down)
            end_stage()


        def common(eng, step_sem):
            stage, steps = [0], [0]

            def end_stage():
                stage[0] += 1
                eng.drain().then_inc(stage_done, 1)
                eng.wait_ge(stage_done, 4 * stage[0])

            def step(ins):
                ins.then_inc(step_sem, 1)
                steps[0] += 1
                eng.wait_ge(step_sem, steps[0])

            return end_stage, step

        @block.scalar
        def _(act):
            end_stage, step = common(act, act_step)
            fn = nc.scalar.activation

            def unit(key):
                u = UA.at[key]
                act.wait_ge(act_bank_full, u + 1)
                return UA.banks[u % 4]

            def copy_out(dst, src):
                fn(dst, src, ACT.Copy).then_inc(act_bank_free, 1)

            def vrow(key):
                act.wait_ge(dve_bank_free, UV.at[key] + 1)

            def layernorm(l):
                spec = LNS[l]
                for c in range(C2):
                    vrow(("mean", l, c))
                    sq = RL["sq"][:, c].rearrange("p (k n) -> p k n", k=4)
                    fn(sq, spec["dst"][:, :, ch(c)], ACT.Square).then_inc(ln_sq, 1)
                for c in range(C2):
                    b = unit(("var", l, c))
                    if spec["plain"] is not None:
                        fn(RL["r1"][:, c, :], b[:, :], ACT.Sqrt, bias=tab("eps"))
                    if spec["double"]:
                        fn(RL["r2"][:, c, :], b[:, :], ACT.Sqrt, bias=tab("eps2"), scale=1.0 + EPS).then_inc(act_bank_free, 1)
                    else:
                        fn(RL["r2"][:, c, :], b[:, :], ACT.Sqrt, bias=tab("eps")).then_inc(act_bank_free, 1)
                if spec["g"]:
                    for c in range(C2):
                        act.wait_ge(ln_out, 2 * l + c + 1)
                        for k in range(4):
                            x = spec["dst"][:, k, ch(c)]
                            fn(x, x, ACT.Identity, scale=col(spec["g"], k), bias=col(spec["b"], k))
                end_stage()

            act.wait_ge(in_consts, 32)
            act.wait_ge(a_var, 1)
            fn(small[:, 0:8], RA["mv"][:, :, 1], ACT.Sqrt, bias=tab("eps")).then_inc(a_std, 1)
            for t in range(TT):
                b = unit(("ldk", t))
                copy_out(LK[:, :, tl(t)], b[:, :].rearrange("p (k n) -> p k n", k=4))
            for t in range(TT):
                b = unit(("qf", t))
                if t >= 2:
                    vrow(("kf", t - 2))
                copy_out(RA["qs"][:, t % 2, :], b[:, :])
            act.wait_ge(top_ready, 1)
            fn(RA["e8"][0:32, 0, 0:TOPK], RA["v8"][0:32, 0, 0:TOPK], ACT.Exp, bias=small[0:32, 8:9],
               accum_out=small[0:32, 9:10]).then_inc(topexp_ready, 1)
            for t in range(TT):
                b = unit(("agg", t))
                copy_out(LQ[:, :, tl(t)], b[:, :].rearrange("p (k n) -> p k n", k=4))
            for o in range(4):
                for c in range(C2):
                    b = unit(("av", o, c))
                    fn(LK[:, o, ch(c)], b[:, :], ACT.Identity, bias=col("L0_xattn_bv", o)).then_inc(act_bank_free, 1)
            end_stage()

            layernorm(0)
            for c in range(C2):
                b = unit(("clock", c))
                fn(RB["ck"][0:16, 0, ch(c)], b[0:16, :], ACT.Identity, bias=col("clock_b", 0, 16)).then_inc(act_bank_free, 1)
            act.wait_ge(act_bank_free, UA.at[("clock", C2 - 1)] + 1)

            def log1pexp(z, t, done):
                step(fn(t, z, ACT.Abs))
                step(fn(t, t, ACT.Exp, scale=-1.0))
                fn(t, t, ACT.Ln, bias=tab("one")[0:z.shape[0], :]).then_inc(done, 1)

            log1pexp(RB["ck"][0:16, 0, :], RB["t"][0:16, 0, :], S["b_ckln"])
            for t in range(TT):
                b = unit(("v", t))
                copy_out(RB["v"][:, t, :], b[:, :])

            def gates_in(o):
                for w, dst, bias in (("bg", gate_buf, "L0_attn_gate_b"), ("bp", p_buf, "L0_attn_p_b")):
                    for c in range(C2):
                        b = unit((w, o, c))
                        fn(dst[o % 2][:, ch(c)], b[:, :], ACT.Identity, bias=col(bias, o)).then_inc(act_bank_free, 1)

            def factors(o):
                act.wait_ge(act_bank_free, UA.at[("bg", o, C2 - 1)] + 1)
                if o == 0:
                    act.wait_ge(S["b_clock"], C2)
                log1pexp(gate_buf[o % 2], RB["t"][:, 0, :], S["b_gsp"])
                for i, w in enumerate(("bq", "bk")):
                    for c in range(C2):
                        b = unit((w, o, c))
                        fn(H[:, 0, 2 + i, ch(c)], b[:, :], ACT.Square).then_inc(S["b_sq"], 1)
                        copy_out(H[:, 0, i, ch(c)], b[:, :])
                act.wait_ge(S["b_gcs"], o + 1)
                fn(gate_buf[o % 2], RB["t"][:, 1, :], ACT.Exp).then_inc(S["b_gcp"], 1)
                act.wait_ge(S["b_pdif"], o + 1)
                fn(p_buf[o % 2], p_buf[o % 2], ACT.Exp).then_inc(S["b_pexp"], 1)
                for i, w in enumerate(("bq", "bk")):
                    for c in range(C2):
                        b = unit(("n" + w, o, c))
                        fn(H[:, 0, 2 + i, ch(c)], b[:, :], ACT.Sqrt).then_inc(act_bank_free, 1)

            gates_in(0)
            factors(0)
            for o in range(4):
                if o < 3:
                    gates_in(o + 1)
                for hf in range(2):
                    for h in range(4):
                        b = unit(("s", o, hf, h))
                        fn(RB["p"][:, 4 * hf + h, :], b[:, :], ACT.Exp, scale=32 ** -0.5).then_inc(act_bank_free, 1)
                if o < 3:
                    factors(o + 1)
            end_stage()
            layernorm(1)

            def b_up(j):
                if j >= 2:
                    act.wait_ge(dve_bank_full, UV.at[("b2", j - 2, 3, C2 - 1)] + 1)
                for o in range(4):
                    for c in range(C2):
                        b = unit(("b1", j, o, c))
                        fn(H[:, j % 2, o, ch(c)], b[:, :], ACT.Gelu, bias=col("L0_attn_mlp_b1", 4 * j + o)
                           ).then_inc(act_bank_free, 1)

            quarters(b_up, lambda j: None)
            end_stage()

            layernorm(2)
            for o in range(4):
                for c in range(C2):
                    copy_out(XN[:, o, ch(c)], unit(("cq", o, c))[:, :])
            for t in range(TT):
                copy_out(RC["sim"][:, t, :], unit(("sim", t))[:, :])
            gated = [0]

            def c_up(j):
                for o in range(4):
                    for c in range(C2):
                        b = unit(("cg", j, o, c))
                        if gated[0] >= 4:
                            vrow(gates[gated[0] - 4])
                        fn(RC["s"][:, gated[0] % 4, :], b[:, :], ACT.Silu, bias=col("L0_ffn_bg", 4 * j + o)
                           ).then_inc(act_bank_free, 1)
                        gated[0] += 1
                    if o % 2 == 0:
                        act.wait_ge(S["c_topin"], 2 * j + o // 2 + 1)
                        fn(RT["rep"], RT["rep"], ACT.Exp)
                        fn(RT["sd"], RT["sd"], ACT.Exp).then_inc(S["c_topexp"], 1)

            gates = [("cu", j, o, c) for j in range(NQ) for o in range(4) for c in range(C2)]
            for j in range(NQ):
                c_up(j)
            for j in range(NQ):
                if j == 0:
                    act.wait_ge(dve_bank_full, UV.at[("cd", 3, 3, C2 - 1)] + 1)
                if j >= 3:
                    act.wait_ge(dve_bank_full, UV.at[("cf", j - 3, TT - 1)] + 1)
                for t in range(TT):
                    b = unit(("ce", j, t))
                    fn(SJ[j % 3][:, t % 4, ch(t // 4)], b[:, :], ACT.Silu).then_inc(act_bank_free, 1)
            end_stage()

            layernorm(3)
            b = unit("m256")
            copy_out(RD["m256"], b[:, 0:256].rearrange("p (o b) -> p o b", o=8))

            def memory(pr):
                if pr:
                    act.wait_ge(act_bank_full, UA.at[("sc", 2 * pr - 1, 3)] + 1)
                for o in range(OT1):
                    b = unit(("mem", pr, o))
                    copy_out(kt[:, o, :, 0:256], b[:, :].rearrange("p (i m) -> p i m", i=2))

            memory(0)
            for cc in range(2):
                for w, dst in (("dq", Q1), ("dk", K1), ("dv", V1)):
                    for o in range(OT1):
                        copy_out(dst[:, o, :], unit((w, cc, o))[:, :])
                for pr in range(8 * cc, 8 * cc + 8):
                    for bb in (2 * pr, 2 * pr + 1):
                        if bb >= 2:
                            act.wait_ge(act_bank_full, UA.at[("pvd", bb - 2)] + 1)
                        for blk, n in ((0, 128), (1, 128), (2, 33)):
                            copy_out(RD["vt"][0:n, bb % 2, blk, 512:1024], unit(("vt", bb, blk, 1))[0:n, :])
                        for g in range(4):
                            x = 4 * (bb % 2) + g
                            b = unit(("sc", bb, g))
                            act.wait_ge(S["d_max"], 4 * bb + g + 1)
                            if bb >= 2:
                                act.wait_ge(dve_bank_full, UV.at[("ptr", bb - 2, g)] + 1)
                            fn(RDa["p"][:, x, :], b[:, 0:289], ACT.Exp, bias=small[:, 16 + x:17 + x], scale=HD1 ** -0.5,
                               accum_out=small[:, 24 + x:25 + x]).then_inc(act_bank_free, 1)
                    if pr + 1 < B // 2:
                        memory(pr + 1)
                    for bb in (2 * pr, 2 * pr + 1):
                        b = unit(("pvd", bb))[:, :].rearrange("p (o c) -> p o c", o=8)
                        tk = slice(32 * (bb % 16), 32 * (bb % 16) + 32)
                        fn(Q1[0:64, :, tk], b[0:64, :, 0:32], ACT.Copy)
                        copy_out(Q1[64:128, :, tk], b[64:128, :, 32:64])
                if cc == 0:
                    act.wait_ge(dve_bank_full, UV.at[("dw", 0, 3)] + 1)
            end_stage()

            layernorm(4)
            step(fn(small[:, 32:33], col("L1_attn_A"), ACT.Abs))
            step(fn(small[:, 33:34], small[:, 32:33], ACT.Exp, scale=-1.0))
            fn(small[:, 34:35], small[:, 33:34], ACT.Ln, bias=tab("one")).then_inc(S["e_a"], 1)
            for c in range(C2):
                b = unit(("dl", c))
                fn(RE["z"][:, 0, ch(c)], b[:, :], ACT.Identity, bias=col("L1_attn_bdelta")).then_inc(act_bank_free, 1)
            act.wait_ge(act_bank_free, UA.at[("dl", C2 - 1)] + 1)
            log1pexp(RE["z"][:, 0, :], RE["t"][:, 0, :], S["e_sp"])
            act.wait_ge(S["e_cum"], 2)
            fn(RE["sh"], RE["sh"], ACT.Exp, scale=-1.0)
            fn(RE["z"][:, 0, :], RE["z"][:, 1, :], ACT.Exp).then_inc(S["e_exp"], 1)
            end_stage()

            layernorm(5)
            for j in range(NQ):
                act.wait_ge(slot_full[slot_of[("fp", j)]], 16 * load_no[("fp", j)])
                fn(RF["wp"][:, 4 * j:4 * j + 4, :], W(("fp", j)), ACT.Abs).then_inc(S["f_abs"], 1)

            def f_abs(j):
                act.wait_ge(slot_full[slot_of[("ff", j)]], 16 * load_no[("ff", j)])
                if j >= 2:
                    act.wait_ge(act_bank_full, UA.at[("ff", j - 2, 3, C2 - 1)] + 1)
                fn(wf[j % 2], W(("ff", j)), ACT.Abs).then_inc(S["f_abs"], 1)

            f_abs(0)
            for c in range(C2):
                copy_out(RF["z"][0:16, 0, ch(c)], unit(("z", c))[0:16, :])
            for c in range(C2):
                fn(RF["z2"][0:16, 0, ch(c)], unit(("z2", c))[0:16, :], ACT.Copy, scale=col("gate", 0, 16)
                   ).then_inc(act_bank_free, 1)
            f_abs(1)
            for j in range(NQ):
                if j >= 2:
                    act.wait_ge(dve_bank_full, UV.at[("fp", j - 2, 3, C2 - 1)] + 1)
                for o in range(4):
                    for c in range(C2):
                        b = unit(("ff", j, o, c))
                        step(fn(RF["r"][:, c, :], b[:, :], ACT.Relu))
                        fn(H[:, j % 2, o, ch(c)], RF["r"][:, c, :], ACT.Square).then_inc(act_bank_free, 1)
                if j + 2 < NQ:
                    f_abs(j + 2)
            end_stage()

        @block.vector
        def _(dve):
            end_stage, step = common(dve, dve_step)
            v = nc.vector

            def unit(key):
                u = UV.at[key]
                dve.wait_ge(dve_bank_full, u + 1)
                return UV.banks[u % 4]

            def on_act(key):
                dve.wait_ge(act_bank_free, UA.at[key] + 1)

            def stored(key):
                dve.wait_ge(dve_bank_free, UV.at[key] + 1)

            def layernorm(l):
                spec = LNS[l]
                for c in range(C2):
                    b = unit(("mean", l, c))
                    v.tensor_tensor(spec["dst"][:, :, ch(c)], spec["src"][:, :, ch(c)],
                                    b[:, :].unsqueeze(1).to_broadcast([128, 4, 512]), ALU.subtract).then_inc(dve_bank_free, 1)
                for c in range(C2):
                    on_act(("var", l, c))
                    x = spec["dst"][:, :, ch(c)]
                    if spec["plain"] is not None:
                        step(v.reciprocal(RL["r1"][:, c, :], RL["r1"][:, c, :]))
                        v.tensor_tensor(spec["plain"][:, :, ch(c)], x,
                                        RL["r1"][:, c, :].unsqueeze(1).to_broadcast([128, 4, 512]), ALU.mult)
                    step(v.reciprocal(RL["r2"][:, c, :], RL["r2"][:, c, :]))
                    v.tensor_tensor(x, x, RL["r2"][:, c, :].unsqueeze(1).to_broadcast([128, 4, 512]), ALU.mult
                                    ).then_inc(ln_out, 1)
                end_stage()

            def add_to_stream(key, o, c, bias=None):
                b = unit(key)
                x = XT[:, o, ch(c)]
                if bias is None:
                    v.tensor_tensor(x, b[:, :], x, ALU.add).then_inc(dve_bank_free, 1)
                else:
                    v.scalar_tensor_tensor(x, b[:, :], bias, x, ALU.add, ALU.add).then_inc(dve_bank_free, 1)

            dve.wait_ge(in_consts, 32)
            v.tensor_copy(ident_r[:, :], tab("ident"))
            v.tensor_copy(causal_r[:, :], tab("causal"))
            dve.wait_ge(in_xtm, 16)
            for t in range(TT):
                last = v.bn_stats(RA["st"][:, t, :], xtm[:, t, :])
            step(last)
            for t in range(TT):
                last = v.bn_aggr(RA["mv"][:, t, :], RA["st"][:, t, :])
            last.then_inc(a_var, 1)
            dve.wait_ge(a_std, 1)
            step(v.reciprocal(small[:, 0:8], small[:, 0:8]))
            for t in range(TT):
                v.tensor_scalar(xtm[:, t, :], xtm[:, t, :], RA["mv"][:, t, 0:1], small[:, t:t + 1], ALU.subtract, ALU.mult
                                ).then_inc(xn_tile, 1)
            for t in range(TT):
                b = unit(("ldq", t))
                v.tensor_copy(LQ[:, :, tl(t)], b[:, :].rearrange("p (k n) -> p k n", k=4)).then_inc(dve_bank_free, 1)
            for t in range(TT):
                on_act(("qf", t))
                b = unit(("kf", t))
                v.tensor_tensor_reduce(out=RA["qs"][:, t % 2, :], in0=RA["qs"][:, t % 2, :], in1=b[:, :], scale=1.0, scalar=0.0,
                                       op0=ALU.mult, op1=ALU.add, accum_out=RA["C"][:, 0, t:t + 1]).then_inc(dve_bank_free, 1)
            dve.wait_ge(dve_bank_free, UV.at[("kf", TT - 1)] + 1)
            dve.wait_ge(in_consts, 32)
            v.tensor_tensor(RA["cx"], RA["C"][:, 0, :].unsqueeze(2).to_broadcast([128, 8, 4]),
                            tab("own_batch").unsqueeze(1).to_broadcast([128, 8, 4]), ALU.mult).then_inc(cx_ready, 1)
            b = unit("corr")
            cr, v8, i8, e8, fi8 = (RA[n][0:32, 0, :] for n in ("cr", "v8", "i8", "e8", "fi8"))
            v.tensor_copy(cr, b[0:32, 0:32]).then_inc(dve_bank_free, 1)
            dve.wait_ge(dve_bank_free, UV.at["corr"] + 1)
            step(v.max(v8, cr))
            step(v.max_index(i8.bitcast(u32), v8, cr))
            v.tensor_copy(fi8, i8.bitcast(u32))
            v.tensor_scalar(small[0:32, 8:9], v8[:, 0:1], -1.0, None, ALU.mult).then_inc(top_ready, 1)
            dve.wait_ge(topexp_ready, 1)
            step(v.reciprocal(small[0:32, 9:10], small[0:32, 9:10]))
            step(v.tensor_scalar(e8[:, 0:TOPK], e8[:, 0:TOPK], small[0:32, 9:10], None, ALU.mult))
            eq = RA["eq"][0:32, :, :]
            step(v.tensor_tensor(eq, tab("iota", 32)[:, 0:32].unsqueeze(1).to_broadcast([32, TOPK, 32]),
                                 fi8[:, 0:TOPK].unsqueeze(2).to_broadcast([32, TOPK, 32]), ALU.is_equal))
            step(v.tensor_tensor(eq, eq, e8[:, 0:TOPK].unsqueeze(2).to_broadcast([32, TOPK, 32]), ALU.mult))
            step(v.tensor_reduce(RA["w2"][0:32, 0, :], eq.rearrange("p k t -> p t k"), AX.X, ALU.add))
            v.tensor_copy(RA["w2"][0:32, 1, :], RA["w2"][0:32, 0, :]).then_inc(w_ready, 1)
            dve.wait_ge(m_loaded, 64)
            v.transpose(RA["mt"].rearrange("p a b -> p (a b)"), RA["m"].rearrange("p a b -> p (a b)")).then_inc(mt_ready, 1)
            dve.wait_ge(in_xT, 16)
            for o in range(4):
                for c in range(C2):
                    add_to_stream(("ao", o, c), o, c, col("L0_xattn_bo", o))
            end_stage()

            layernorm(0)
            reset = RB["reset"]
            step(v.memset(reset, 1.0))
            step(v.memset(reset[:, 0, :].rearrange("p (b l) -> p b l", l=L)[:, :, 0:1], 0.0))
            dve.wait_ge(S["b_ckln"], 1)
            for c in range(C2):
                v.scalar_tensor_tensor(RB["ck"][0:16, 0, ch(c)], RB["ck"][0:16, 0, ch(c)], 0.0, RB["t"][0:16, 0, ch(c)],
                                       ALU.max, ALU.add).then_inc(S["b_clock"], 1)
            pcs, q, k = H[:, 1, 2, :], H[:, 0, 0, :], H[:, 0, 1, :]
            t0, t1 = RB["t"][:, 0, :], RB["t"][:, 1, :]
            byb = dict(l=L)

            def normalise(o):
                for t in range(TT):
                    b = unit(("pv", o, t))
                    if t or o:
                        stored(("pv", o, t - 1) if t else ("pv", o - 1, TT - 1))
                    step(v.reciprocal(RB["den"][:, 0, :], b[:, 128:256]))
                    v.tensor_tensor(RB["ot"][:, o, tl(t)], b[:, 0:128], RB["den"][:, 0, :], ALU.mult
                                    ).then_inc(dve_bank_free, 1)

            for o in range(4):
                g, p = gate_buf[o % 2], p_buf[o % 2]
                dve.wait_ge(S["b_gsp"], o + 1)
                step(v.scalar_tensor_tensor(t0, g, 0.0, t0, ALU.max, ALU.add))
                step(v.tensor_tensor_scan(t1, reset[:, 0, :], t0, 0.0, ALU.mult, ALU.subtract))
                v.tensor_scalar(t1, t1, -60.0, 50.0, ALU.max, ALU.min).then_inc(S["b_gcs"], 1)
                on_act(("bp", o, C2 - 1))
                pv3 = p.rearrange("p (b l) -> p b l", **byb)
                step(v.tensor_reduce(RB["pm"][:, 0, :], pv3, AX.X, ALU.max))
                v.tensor_tensor(pv3, pv3, RB["pm"][:, 0, :].unsqueeze(2).to_broadcast([128, B, L]), ALU.subtract
                                ).then_inc(S["b_pdif"], 1)
                dve.wait_ge(S["b_pexp"], o + 1)
                for c in range(C2):
                    b = unit(("ck", o, c))
                    v.tensor_tensor(p[:, ch(c)], b[:, :], p[:, ch(c)], ALU.mult).then_inc(dve_bank_free, 1)
                dve.wait_ge(dve_bank_free, UV.at[("ck", o, C2 - 1)] + 1)
                v.tensor_tensor_scan(pcs, reset[:, 0, :], p, 0.0, ALU.mult, ALU.add)
                for w, t_ in (("bq", t0), ("bk", t1)):
                    for c in range(C2):
                        b = unit(("r" + w, o, c))
                        v.tensor_tensor(t_[:, ch(c)].rearrange("p (b l) -> p b l", **byb),
                                        b[:, :].rearrange("p (b l) -> p b l", **byb),
                                        tab("sin").unsqueeze(1).to_broadcast([128, 16, L]), ALU.mult).then_inc(dve_bank_free, 1)
                on_act(("nbk", o, C2 - 1))
                nrm = H[:, 0, 2:4, :]
                step(v.tensor_scalar(nrm, nrm, 1e-12, None, ALU.max))
                v.scalar_tensor_tensor(H[:, 0, 3, :], g, 1e-8, H[:, 0, 3, :], ALU.add, ALU.mult)
                step(v.scalar_tensor_tensor(H[:, 0, 2, :], pcs, 1e-8, H[:, 0, 2, :], ALU.add, ALU.mult))
                if o:
                    normalise(o - 1)
                step(v.reciprocal(nrm, nrm))
                v.tensor_tensor(pcs, g, H[:, 0, 2, :], ALU.mult)
                v.tensor_tensor(p, p, H[:, 0, 3, :], ALU.mult)
                dve.wait_ge(S["b_cos"], 2 * (o + 1))
                v.tensor_tensor(q, q, t0, ALU.add)
                step(v.tensor_tensor(k, k, t1, ALU.add))
                v.tensor_tensor(q, q, pcs, ALU.mult).then_inc(S["b_qk"], 1)
                v.tensor_tensor(k, k, p, ALU.mult).then_inc(S["b_qk"], 1)
            normalise(3)
            for o in range(4):
                for c in range(C2):
                    b = unit(("bo", o, c))
                    v.scalar_tensor_tensor(Y[:, o, ch(c)], b[:, :], col("L0_attn_out_b", o), Y[:, o, ch(c)], ALU.add, ALU.add
                                           ).then_inc(dve_bank_free, 1)
            end_stage()
            layernorm(1)
            step(v.tensor_tensor(XT[:, :, :], XT[:, :, :], Y[:, :, :], ALU.add))

            def down(name, bias, j):
                for o in range(4):
                    for c in range(C2):
                        add_to_stream((name, j, o, c), o, c, col(bias, o) if j == 0 else None)

            for j in range(NQ):
                down("b2", "L0_attn_mlp_b2", j)
            end_stage()

            layernorm(2)

            def route(t):
                i = t % 2
                tf, na = RT["tf"][:, i], RT["na"][:, i]
                on_act(("sim", TT - 1))
                for n in range(8):
                    sim = RC["sim"][:, t, 64 * n:64 * n + 64]
                    last = v.max(RT["tv"][:, n, :], sim)
                step(last)
                for n in range(8):
                    sim = RC["sim"][:, t, 64 * n:64 * n + 64]
                    last = v.max_index(RT["ti"][:, n, :].bitcast(u32), RT["tv"][:, n, :], sim)
                step(last)
                if t >= 2:
                    dve.wait_ge(S["c_dense"], t - 1)
                v.tensor_copy(tf, RT["ti"].bitcast(u32))
                for h in range(PH):
                    last = v.tensor_tensor(RT["cand"][:, h, :].rearrange("p (a b) -> p a b", a=8),
                                           RT["tv"][:, h, :].unsqueeze(2).to_broadcast([128, 8, 8]),
                                           RT["tv"][:, 4 + h, :].unsqueeze(1).to_broadcast([128, 8, 8]), ALU.add)
                step(last)
                for h in range(PH):
                    last = v.max(RT["t8"][:, h, :], RT["cand"][:, h, :])
                step(last)
                for h in range(PH):
                    last = v.match_replace(RT["rep"][:, h, :], RT["t8"][:, h, :], RT["cand"][:, h, :], -3e38)
                step(last)
                sel = RT["sel"]
                step(v.tensor_tensor(sel, RT["rep"], RT["cand"], ALU.not_equal))
                v.tensor_tensor(RT["rep"], RT["cand"], RT["t8"][:, :, 0:1].to_broadcast([128, PH, 64]), ALU.subtract)
                v.tensor_tensor(RT["sd"], RC["sim"][:, t, :].rearrange("p (n k) -> p n k", n=8),
                                RT["tv"][:, :, 0:1].to_broadcast([128, 8, 64]), ALU.subtract).then_inc(S["c_topin"], 1)
                v.tensor_reduce(na.rearrange("p h a -> p (h a)"), sel.rearrange("p h (a b) -> p (h a) b", a=8), AX.X, ALU.add)
                step(v.tensor_scalar(RT["ge"], tf[:, 0:4, :], 32.0, None, ALU.is_ge))
                dve.wait_ge(S["c_topexp"], t + 1)
                step(v.tensor_tensor(RT["rep"], RT["rep"], sel, ALU.mult))
                step(v.tensor_reduce(RT["rs"].rearrange("p h a -> p (h a)"), RT["rep"].rearrange("p h (a b) -> p (h a) b", a=8),
                                     AX.X, ALU.add))
                step(v.tensor_reduce(RT["z"][:, 0, :], RT["rs"], AX.X, ALU.add))
                step(v.reciprocal(RT["rz"][:, 0, :], RT["z"][:, 0, :]))
                rz = RT["rz"][:, 0, :].unsqueeze(2)
                step(v.tensor_tensor(RT["rs"], RT["rs"], RT["ge"], ALU.mult))
                step(v.tensor_tensor(RT["rs"], RT["rs"], rz.to_broadcast([128, PH, 8]), ALU.mult))
                v.tensor_reduce(RC["xv"][:, 0, t:t + 1], RT["rs"].rearrange("p h a -> p (h a)"), AX.X, ALU.add)
                v.tensor_copy(RC["Ey"][:, t], RT["sd"][:, 4:8, :])
                v.tensor_tensor(RC["Ex"][:, t], RT["sd"][:, 0:4, 0:32], rz.to_broadcast([128, PH, 32]), ALU.mult
                                ).then_inc(S["c_fac"], 1)

            def c_up(j):
                for o in range(4):
                    for c in range(C2):
                        u = 8 * j + 2 * o + c
                        on_act(("cg", j, o, c))
                        b = unit(("cu", j, o, c))
                        v.scalar_tensor_tensor(H[:, j % 2, o, ch(c)], b[:, :], col("L0_ffn_bu", 4 * j + o), RC["s"][:, u % 4, :],
                                               ALU.add, ALU.mult).then_inc(dve_bank_free, 1)
                    if o % 2 == 0:
                        route(2 * j + o // 2)

            quarters(c_up, lambda j: down("cd", "L0_ffn_bd", j))
            tmp = RC["eq"][:, 0, :].rearrange("p (h x y) -> p h x y", h=PH, x=8)
            dve.wait_ge(S["c_dense"], TT)

            def spread(j, t):
                n = TT * j + t
                xs = slice(8 * j, 8 * j + 8)
                if n:
                    dve.wait_ge(S["c_p"], n)
                for h in range(PH):
                    T = RC["Tx"][:, t, h, xs].unsqueeze(2).to_broadcast([128, 8, 64])
                    Ry = RC["Ry"][:, t, h, :].unsqueeze(1).to_broadcast([128, 8, 64])
                    last = v.tensor_tensor(tmp[:, h], T, Ry, ALU.is_gt)
                step(last)
                flat = RC["eq"][:, 0, :]
                dve.wait_ge(S["c_ee"], n + 1)
                last = v.tensor_tensor(flat, flat, EE[:, n % 2, :], ALU.mult)
                last.then_inc(S["c_mul"], 1)
                dve.wait_ge(S["c_mul"], n + 1)
                step(v.tensor_tensor(flat[:, 0:1024], flat[:, 0:1024], flat[:, 1024:2048], ALU.add))
                pj = RC["pj"][:, t % 2, :]
                if n >= 2:
                    dve.wait_ge(dve_bank_full, UV.at[("pt", (n - 2) // TT, (n - 2) % TT)] + 1)
                last = v.tensor_tensor(pj, flat[:, 0:512], flat[:, 512:1024], ALU.add)
                if j == NQ - 1:
                    step(last)
                    last = v.tensor_tensor(pj[:, 511:512], pj[:, 511:512], RC["xv"][:, 0, t:t + 1], ALU.add)
                last.then_inc(S["c_p"], 1)

            def weigh(j, t):
                on_act(("ce", j, 3 if t < 4 else 7))
                b = unit(("pt", j, t))
                x = SJ[j % 3][:, :, tl(t)]
                v.tensor_tensor(x, b[:, :].rearrange("p (e n) -> p e n", e=4), x, ALU.mult).then_inc(dve_bank_free, 1)

            for n in range(TT * (NQ + 1) + 1):
                if n < TT * NQ:
                    spread(n // TT, n % TT)
                if 1 <= n <= TT * NQ:
                    weigh((n - 1) // TT, (n - 1) % TT)
                if n > TT:
                    t = (n - 1) % TT
                    add_to_stream(("cf", (n - 1) // TT - 1, t), t % 4, t // 4)
            end_stage()

            layernorm(3)
            for cc in range(2):
                for pr in range(8 * cc, 8 * cc + 8):
                    for bb in (2 * pr, 2 * pr + 1):
                        if bb >= 2:
                            dve.wait_ge(act_bank_full, UA.at[("pvd", bb - 2)] + 1)
                        for blk, n in ((0, 128), (1, 128), (2, 33)):
                            b = unit(("vt", bb, blk, 0))
                            v.tensor_copy(RD["vt"][0:n, bb % 2, blk, 0:512], b[0:n, :]).then_inc(dve_bank_free, 1)
                        for g_ in range(4):
                            x = 16 + 4 * (bb % 2) + g_
                            u = UA.at[("sc", bb, g_)]
                            dve.wait_ge(act_bank_full, u + 1)
                            step(v.reduce_max(small[:, x:x + 1], UA.banks[u % 4][:, 0:289], AX.X))
                            v.tensor_scalar(small[:, x:x + 1], small[:, x:x + 1], -HD1 ** -0.5, None, ALU.mult
                                            ).then_inc(S["d_max"], 1)
                    for bb in (2 * pr, 2 * pr + 1):
                        for g_ in range(4):
                            x = 4 * (bb % 2) + g_
                            on_act(("sc", bb, g_))
                            step(v.reciprocal(small[:, 24 + x:25 + x], small[:, 24 + x:25 + x]))
                            v.tensor_scalar(RDa["p"][:, x, :], RDa["p"][:, x, :], small[:, 24 + x:25 + x], None, ALU.mult
                                            ).then_inc(S["d_probn"], 1)
                        for g_ in range(4):
                            b = unit(("ptr", bb, g_))
                            v.tensor_copy(RDa["pt"][:, g_, 0:256], b[:, 0:256])
                            v.tensor_copy(RDa["pt"][0:33, g_, 256:384], b[0:33, 256:384]).then_inc(dve_bank_free, 1)
                for o in range(4):
                    add_to_stream(("dw", cc, o), o, cc, col("L1_xattn_bo", o))
            end_stage()

            layernorm(4)
            reset = RE["reset"]
            step(v.memset(reset, 1.0))
            step(v.memset(reset[:, 0, :].rearrange("p (b l) -> p b l", l=L)[:, :, 0:1], 0.0))
            dve.wait_ge(S["e_a"], 1)
            step(v.scalar_tensor_tensor(small[:, 35:36], col("L1_attn_A"), 0.0, small[:, 34:35], ALU.max, ALU.add))
            step(v.tensor_scalar(small[:, 35:36], small[:, 35:36], -1.0, None, ALU.mult))
            step(v.tensor_tensor(small[:, 36:40], cols[:, COLUMN_AT["L1_attn_bc"]:COLUMN_AT["L1_attn_bc"] + 4],
                                 cols[:, COLUMN_AT["L1_attn_bd"]:COLUMN_AT["L1_attn_bd"] + 4], ALU.add))
            dve.wait_ge(S["e_sp"], 1)
            dl, bbar, cum, tt = RE["dl"][:, 0, :], RE["bb"][:, 0, :], RE["z"][:, 1, :], RE["t"][:, 1, :]
            step(v.scalar_tensor_tensor(dl, RE["z"][:, 0, :], 0.0, RE["t"][:, 0, :], ALU.max, ALU.add))
            for c in range(C2):
                b = unit(("bb", c))
                v.scalar_tensor_tensor(bbar[:, ch(c)], b[:, :], col("L1_attn_bb"), dl[:, ch(c)], ALU.add, ALU.mult
                                       ).then_inc(dve_bank_free, 1)
            step(v.tensor_scalar(tt, dl, small[:, 35:36], None, ALU.mult))
            step(v.tensor_tensor_scan(cum, reset[:, 0, :], tt, 0.0, ALU.mult, ALU.add))
            v.tensor_scalar(cum, cum, -20.0, 20.0, ALU.max, ALU.min).then_inc(S["e_cum"], 1)
            dve.wait_ge(S["e_cum"], 1)
            v.memset(RE["sh"][:, :, 0:1], 0.0)
            v.tensor_copy(RE["sh"][:, :, 1:L], cum.rearrange("p (b l) -> p b l", l=L)[:, :, 0:L - 1]).then_inc(S["e_cum"], 1)
            dve.wait_ge(S["e_exp"], 1)
            dve.wait_ge(dve_bank_free, UV.at[("bb", C2 - 1)] + 1)
            step(v.tensor_tensor(bbar, bbar, RE["sh"].rearrange("p b l -> p (b l)"), ALU.mult))
            step(v.tensor_tensor_scan(tt, reset[:, 0, :], bbar, 0.0, ALU.mult, ALU.add))
            v.tensor_tensor(RE["hh"][:, 0, :], tt, RE["z"][:, 0, :], ALU.mult).then_inc(S["e_hh"], 1)
            for o in range(4):
                for c in range(C2):
                    add_to_stream(("ed", o, c), o, c, small[:, 36 + o:37 + o])
            end_stage()

            layernorm(5)

            def ternary(w, dst, scale, done, count):
                tn = RF["tn"][:, 0, :].rearrange("p (k n) -> p k n", k=4)
                for k_ in range(4):
                    v.tensor_tensor(tn[:, k_, :], w[:, k_, :], RF["half"][:, 0, :], ALU.is_gt)
                    last = v.scalar_tensor_tensor(dst[:, k_, :], w[:, k_, :], -1.0, RF["half"][:, 0, :], ALU.mult, ALU.is_gt)
                step(last)
                step(v.tensor_tensor(dst, tn, dst, ALU.subtract))
                v.tensor_tensor(dst, dst, scale.unsqueeze(1).to_broadcast([128, 4, 512]), ALU.mult).then_inc(done, 1)
                dve.wait_ge(done, count)

            def scale_of(key, dst):
                b = unit(key)
                v.tensor_scalar(dst, b[:, :], 1e-5, None, ALU.max).then_inc(dve_bank_free, 1)
                dve.wait_ge(dve_bank_free, UV.at[key] + 1)

            def halve(s):
                step(v.tensor_scalar(RF["half"][:, 0, :], s, 0.5, None, ALU.mult))

            sp_, sf_ = RF["sp"][:, 0, :], RF["s"][:, 0, :]

            def up_weights(j):
                scale_of(("fs", j), sf_)
                halve(sf_)
                dve.wait_ge(slot_full[slot_of[("ff", j)]], 16 * load_no[("ff", j)])
                ternary(W(("ff", j)), wf[j % 2], sf_, S["f_wf"], j + 1)
                released[("ff", j)] = (S["f_wf"], j + 1)

            scale_of("fps", sp_)
            up_weights(0)
            up_weights(1)
            halve(sp_)
            for j in range(NQ):
                dve.wait_ge(slot_full[slot_of[("fp", j)]], 16 * load_no[("fp", j)])
                ternary(W(("fp", j)), RF["wp"][:, 4 * j:4 * j + 4, :], sp_, S["f_wp"], j + 1)
                released[("fp", j)] = (S["f_wp"], j + 1)
            for j in range(NQ):
                if j + 2 < NQ:
                    up_weights(j + 2)
                for o in range(4):
                    for c in range(C2):
                        add_to_stream(("fp", j, o, c), o, c)
            end_stage()

        @block.gpsimd
        def _(pool):
            end_stage, step = common(pool, pool_step)
            g = nc.gpsimd

            g.memset(RA["m"], 0.0).then_inc(m_zero, 1)
            pool.wait_ge(in_consts, 32)
            end_stage()
            end_stage()
            for o in range(4):
                for i, w in enumerate(("bq", "bk")):
                    pool.wait_ge(act_bank_free, UA.at[(w, o, C2 - 1)] + 1)
                    pool.wait_ge(dve_bank_full, UV.at[("r" + w, o, C2 - 1)] + 1)
                    x3 = H[:, 0, i, :].rearrange("p (b l) -> p b l", l=L)
                    g.tensor_tensor(x3, x3, tab("cos").unsqueeze(1).to_broadcast([128, B, L]), ALU.mult).then_inc(S["b_cos"], 1)
            for _i in range(4):
                end_stage()
            eqf = RC["eq"][:, 0, :]
            for t in range(TT):
                i = t % 2
                tf, na = RT["tf"][:, i], RT["na"][:, i]
                pool.wait_ge(S["c_fac"], t + 1)
                for ax in range(2):
                    if ax == 0:
                        n, w, dst = 32, na, RC["Tx"][:, t]
                    else:
                        n, w, dst = 64, None, RC["Ry"][:, t]
                    e4 = eqf[:, 0:32 * n].rearrange("p (a h x) -> p a h x", a=8, h=PH)
                    for h in range(PH):
                        key = tf[:, 4 * ax + h, :].unsqueeze(2).to_broadcast([128, 8, n])
                        last = g.tensor_tensor(e4[:, :, h, :], tab("iota")[:, 0:n].unsqueeze(1).to_broadcast([128, 8, n]), key,
                                               ALU.subtract)
                    step(last)
                    step(g.tensor_scalar(eqf[:, 0:32 * n], eqf[:, 0:32 * n], 0.0, None, ALU.is_equal))
                    for h in range(PH):
                        wt = (na[:, h, :] if ax == 0 else tab("rank")).unsqueeze(2).to_broadcast([128, 8, n])
                        last = g.tensor_tensor(e4[:, :, h, :], e4[:, :, h, :], wt, ALU.mult)
                    step(last)
                    m = 4 * n
                    step(g.tensor_tensor(eqf[:, 0:4 * m], eqf[:, 0:4 * m], eqf[:, 4 * m:8 * m], ALU.add))
                    step(g.tensor_tensor(eqf[:, 0:2 * m], eqf[:, 0:2 * m], eqf[:, 2 * m:4 * m], ALU.add))
                    d2 = dst.rearrange("p h x -> p (h x)")
                    last = g.tensor_tensor(d2, eqf[:, 0:m], eqf[:, m:2 * m], ALU.add)
                    step(last)
                g.tensor_scalar(RC["Ry"][:, t], RC["Ry"][:, t], -1.0, 8.0, ALU.mult, ALU.add).then_inc(S["c_dense"], 1)
            pool.wait_ge(S["c_fac"], TT)
            for n in range(TT * NQ):
                j, t = n // TT, n % TT
                if n >= 2:
                    pool.wait_ge(S["c_mul"], n - 1)
                for h in range(PH):
                    Ex = RC["Ex"][:, t, h, 8 * j:8 * j + 8].unsqueeze(2).to_broadcast([128, 8, 64])
                    Ey = RC["Ey"][:, t, h, :].unsqueeze(1).to_broadcast([128, 8, 64])
                    last = g.tensor_tensor(EE[:, n % 2, 512 * h:512 * h + 512].rearrange("p (x y) -> p x y", x=8), Ex, Ey, ALU.mult)
                last.then_inc(S["c_ee"], 1)
            end_stage()
            end_stage()

            step(g.memset(RD["qbd"], 0.0))
            for bb in range(B):
                pr, i, cc, lb = bb // 2, bb % 2, bb // 16, bb % 16
                if lb == 0:
                    pool.wait_ge(act_bank_free, UA.at[("dv", cc, OT1 - 1)] + 1)
                if i == 0 and pr:
                    pool.wait_ge(act_bank_full, UA.at[("sc", 2 * pr - 1, 3)] + 1)
                if bb:
                    pool.wait_ge(S["d_qbd"], bb)
                tk = slice(32 * lb, 32 * lb + 32)
                for at_ in (256, 289):
                    g.tensor_copy(kt[:, :, i, at_:at_ + 1], RD["m256"][:, :, bb:bb + 1])
                g.tensor_copy(kt[:, :, i, 257:289], K1[:, :, tk])
                g.tensor_copy(kt[:, :, i, 290:322], V1[:, :, tk]).then_inc(S["d_self"], 1)
                if bb >= 2:
                    pool.wait_ge(act_bank_full, UA.at[("sc", bb - 2, 3)] + 1)
                pool.wait_ge(S["d_self"], bb + 1)
                step(g.tensor_copy(qbd[i][0:64, :, 0:32], Q1[0:64, :, tk]))
                g.tensor_copy(qbd[i][64:128, :, 32:64], Q1[64:128, :, tk]).then_inc(S["d_qbd"], 1)
            end_stage()
            for _i in range(4):
                end_stage()

        @block.sync
        def _(sp):
            slot_last = {}

            def load(i):
                name, s_, src = loads[i]
                if s_ in slot_last:
                    sem_, val = released[slot_last[s_]]
                    sp.wait_ge(sem_, val)
                if i >= E_FIRST and s_ in (2, 3) and slot_last.get(s_) in (None, *before_d):
                    sp.wait_ge(stage_done, 4 * 9)
                dst = arena[:, s_, :, :]
                if src.shape[2] != 512:
                    dst = dst[:, :, 0:src.shape[2]]
                sp.dma_start(dst, src).then_inc(slot_full[s_], 16)
                slot_last[s_] = name

            before_d = {n for n, _, _ in loads[:D_FIRST]}
            sp.dma_start(xtm, dram["x_tokens"].rearrange("(t p) d -> p t d", p=128)).then_inc(in_xtm, 16)
            sp.dma_start(consts[:, :], dram["tables"]).then_inc(in_consts, 16)
            sp.dma_start(cols[:, :], dram["columns"]).then_inc(in_consts, 16)
            c32 = dram["ctx"].rearrange("(t b) m d -> b m t d", b=4)
            for b4 in range(4):
                sp.dma_start(ctm[32 * b4:32 * b4 + 32, :, :], c32[b4, 0:32, :, :]).then_inc(in_ctx32, 16)
            sp.dma_start(RA["bq"][0:1, 0, :], dram["L0_xattn_bq"]).then_inc(in_small, 16)
            sp.dma_start(RA["bk"][0:1, 0, :], dram["L0_xattn_bk"]).then_inc(in_small, 16)
            load(0)
            load(1)
            sp.dma_start(XT[:, :, :], dram["xT"].rearrange("(k p) n -> p k n", p=128)).then_inc(in_xT, 16)
            for i in range(2, 6):
                load(i)
            sp.wait_ge(w_ready, 1)
            scratch = dram["scratch"]
            sp.dma_start(scratch.rearrange("b (r j) -> b r j", j=64),
                         RA["w2"][0:32].rearrange("p a b -> p (a b)").unsqueeze(1).to_broadcast([32, 32, 64])
                         ).then_inc(w_stored, 16)
            sp.wait_ge(w_stored, 16)
            sp.wait_ge(m_zero, 1)
            skew = scratch[:, 32:2048].rearrange("b (l s) -> b l s", s=63)[:, :, 0:32].rearrange("(t b) l m -> b l t m", b=4)
            for b4 in range(4):
                sp.dma_start(RA["m"][32 * b4:32 * b4 + 32, :, 32 * b4:32 * b4 + 32], skew[b4]).then_inc(m_loaded, 16)
            for i in range(6, 9):
                load(i)
            sp.wait_ge(stage_done, 8)
            sp.dma_start(RB["cw"], dram["L0_attn_clock_w"].rearrange("(k p) n -> p k n", p=128)).then_inc(in_small, 16)
            first_e = [i for i, l_ in enumerate(loads) if l_[0] == ("ce", 0)][0]
            first_c = [i for i, l_ in enumerate(loads) if l_[0] == "cq"][0]
            for i in range(9, first_c + 1):
                load(i)
            sp.wait_ge(stage_done, 4 * 6)
            sp.dma_start(RC["kb"], dram["key_blocks"]).then_inc(S["c_kb"], 16)
            for i in range(first_c + 1, D_FIRST):
                load(i)
            per = (E_FIRST - D_FIRST - 2) // 2

            def load_ct(pr):
                if pr >= 2:
                    sp.wait_ge(act_bank_full, UA.at[("mem", pr - 2, OT1 - 1)] + 1)
                sp.dma_start(RD["ct"][:, pr % 2], dram["ctxT"].rearrange("(k p) n -> p k n", p=128)[:, :, 514 * pr:514 * pr + 514]
                             ).then_inc(S[f"d_ct{pr % 2}"], 16)

            for cc in range(2):
                lo = D_FIRST + 2 + per * cc
                for i in range(D_FIRST if cc == 0 else lo, lo + per):
                    load(i)
                    if cc == 0 and i == D_FIRST + 1:
                        sp.wait_ge(stage_done, 4 * 8)
                        sp.dma_start(RD["c256"], dram["ctx_lastT"].rearrange("(k p) b -> p k b", p=128)
                                     ).then_inc(S["d_ct256"], 16)
                        load_ct(0)
                        load_ct(1)
                for pr in (range(2, 10) if cc == 0 else range(10, 16)):
                    load_ct(pr)
            load(E_FIRST)
            load(E_FIRST + 1)
            sp.wait_ge(stage_done, 4 * 10)
            sp.dma_start(RE["wc"][:, 0, :], dram["L1_attn_Wc"]).then_inc(in_small, 16)
            for i in range(E_FIRST + 2, E_FIRST + 6):
                load(i)
            sp.wait_ge(stage_done, 4 * 12)
            sp.dma_start(RF["vT"], dram["vT"].rearrange("(k p) n -> p k n", p=128)).then_inc(in_small, 16)
            sp.dma_start(RF["fb"][0:16, 0, :], dram["fast_bT"]).then_inc(in_small, 16)
            sp.dma_start(RF["uT"][0:16, 0, :], dram["uT"]).then_inc(in_small, 16)
            for i in range(E_FIRST + 6, len(loads)):
                load(i)
            sp.wait_ge(stage_done, 4 * 13)
            sp.dma_start(out.rearrange("(k p) n -> p k n", p=128), XT[:, :, :]).then_inc(out_stored, 16)
            sp.wait_ge(out_stored, 16)


_PLAIN = ["L0_xattn_Wq", "L0_xattn_Wk", "L0_xattn_Wv", "L0_xattn_Wo", "L0_attn_Wq", "L0_attn_Wk", "L0_attn_Wv",
          "L0_attn_gate_w", "L0_attn_p_w", "L0_attn_out_w", "L0_attn_clock_w", "L0_attn_mlp_w1", "L0_attn_mlp_w2",
          "L0_ffn_Wg", "L0_ffn_Wu", "L0_ffn_Wd", "L0_ffn_Wq", "L0_ffn_up_embed", "L1_xattn_Wq", "L1_xattn_Wkv",
          "L1_xattn_Wm", "L1_xattn_Wo", "L1_attn_Wc", "L1_attn_Wd"]


def layouts(inputs):
    a = {k: np.ascontiguousarray(v) for k, v in inputs.items()}
    got = {k: a[k] for k in _PLAIN}
    x = a["x"].reshape(N, D)
    got["x_tokens"] = x
    got["xT"] = np.ascontiguousarray(x.T)
    got["ctx"] = a["ctx_1024"]
    got["ctxT"] = np.ascontiguousarray(a["ctx_1024"].reshape(B * M, D).T)
    got["ctx_lastT"] = np.ascontiguousarray(a["ctx_1024"][:, M - 1, :].T)
    got["tables"] = np.concatenate([TABLES[k] for k in TABLES], axis=1)
    columns = np.zeros((128, COLUMN_COLS), np.float32)
    for name, n in COLUMNS:
        at_ = COLUMN_AT[name]
        if name == "clock_b":
            columns[0:16, at_] = a["L0_attn_clock_b"]
        elif name == "gate":
            columns[:, at_] = np.broadcast_to(a["L1_ffn_gate"].reshape(1), (128,))
        else:
            columns[:, at_:at_ + n] = a[name].reshape(n, 128).T
    got["columns"] = columns
    got["L0_xattn_bq"] = a["L0_xattn_bq"].reshape(1, D)
    got["L0_xattn_bk"] = a["L0_xattn_bk"].reshape(1, D)
    keys = a["L0_ffn_keys"]
    kb = np.zeros((128, 4, 128), np.float32)
    for part in range(2):
        for h in range(4):
            o = 64 * (h % 2)
            kb[o:o + 64, 2 * part + h // 2, o:o + 64] = keys[h, :, part, :].T
    got["key_blocks"] = kb
    got["downT"] = np.ascontiguousarray(a["L0_ffn_down_embed"].T)
    got["L1_delta_b"] = np.ascontiguousarray(np.concatenate([a["L1_attn_Wdelta"], a["L1_attn_Wb"]], axis=1))
    got["w_fcT"] = np.ascontiguousarray(a["L1_ffn_w_fc"].T)
    got["w_projT"] = np.ascontiguousarray(a["L1_ffn_w_proj"].T)
    got["vT"] = np.ascontiguousarray(a["L1_ffn_v"].T)
    got["fast_bT"] = np.ascontiguousarray(a["L1_ffn_fast_b"].T)
    got["uT"] = np.ascontiguousarray(a["L1_ffn_u"].T)
    return got


def kernel(**inputs):
    import concourse.bacc as _bacc
    from concourse.bass_utils import run_bass_kernel_spmd as _run

    nc = _bacc.Bacc("TRN2", target_bir_lowering=False, num_devices=1)
    arrays = layouts(inputs)
    f32 = mybir.dt.float32
    dram = {k: nc.dram_tensor(f"in_{k}", v.shape, f32, kind="ExternalInput").ap() for k, v in arrays.items()}
    dram["scratch"] = nc.dram_tensor("scratch", (32, 2048), f32).ap()
    out = nc.dram_tensor("out_xT", (D, N), f32, kind="ExternalOutput").ap()
    perceiver(nc, dram, out)
    r = _run(nc, [{f"in_{k}": v for k, v in arrays.items()}], core_ids=[0])
    return np.ascontiguousarray(r.results[0]["out_xT"].T).reshape(B, L, D)
```

```python
import numpy as np
import concourse.bass as bass
from concourse import mybir
from contextlib import ExitStack

B, L, D = 32, 32, 512
N = B * L
M = 257
KT_ = D // 128
TT = N // 128
C2 = N // 512
F = 2048
NQ = F // 512
TOPK = int(2 * np.log(L))
NKEYS, NEXP, PH = 64, 2048, 4
HD1, H1 = 64, 16
INNER = HD1 * H1
CT = 256
NCH, CB = N // CT, CT // L
OT1 = INNER // 128
EPS = 1e-5



def constant_tables():
    p = np.arange(128)
    tabs = {}
    tabs["ident"] = np.eye(128)
    l = np.arange(32)
    f = np.concatenate([np.arange(17), np.arange(1, 16)])
    ang = 2 * np.pi * np.outer(l, f) / 32
    base = np.where(np.arange(32)[None, :] < 17, np.cos(ang), np.sin(ang))
    tabs["dft"] = np.kron(np.eye(4), base)
    wf = np.where((f == 0) | (f == 16), 1.0, 2.0)
    tabs["corr"] = np.tile((base * wf[None, :]).T / (32 * 512), (4, 1))
    tabs["own_batch"] = (p[:, None] // 32 == np.arange(4)[None, :]) * 1.0
    tabs["head_ones"] = np.kron(np.eye(4), np.ones((32, 32)))
    rot = np.zeros((128, 128))
    for i in range(0, 128, 2):
        rot[i, i + 1] = -1.0
        rot[i + 1, i] = 1.0
    tabs["rot"] = rot.T
    fr = np.exp(-np.arange(16, dtype=np.float32) * np.float32(np.log(10000.0) / 16))
    th = (np.arange(32, dtype=np.float32)[None, :] * fr[:, None]).astype(np.float32)
    tabs["cos"] = np.cos(th)[(p % 32) // 2]
    tabs["sin"] = np.sin(th)[(p % 32) // 2]
    ok = (p[:, None] // 32 == p[None, :] // 32) & (p[:, None] <= p[None, :])
    tabs["causal"] = np.where(ok, 0.0, -2.0 ** 99)
    tabs["mean_ones"] = np.full((128, 128), 1.0 / D)
    tabs["hid_ones"] = np.full((128, 128), 1.0 / F)
    tabs["ones"] = np.ones((128, 32))
    tabs["iota"] = np.tile(np.arange(64.0), (128, 1))
    tabs["rank"] = np.tile(8.0 - np.arange(8.0), (128, 1))
    dc = np.zeros((128, 128))
    dc[0, ::32] = 32.0
    tabs["dc"] = dc
    ex = np.zeros((128, 512))
    for c in range(512):
        ex[c // 32, c] = 1.0
    tabs["expand"] = ex
    tabs["eps"] = np.full((128, 1), EPS)
    tabs["eps2"] = np.full((128, 1), EPS * EPS)
    tabs["one"] = np.full((128, 1), 1.0)
    return {k: v.astype(np.float32) for k, v in tabs.items()}


TABLES = constant_tables()
TABLE_AT, at = {}, 0
for _k, _v in TABLES.items():
    TABLE_AT[_k] = (at, _v.shape[1])
    at += _v.shape[1]
TABLE_COLS = at

COLUMNS = [("L0_xattn_bv", 4), ("L0_xattn_bo", 4), ("L0_attn_gate_b", 4), ("L0_attn_p_b", 4), ("L0_attn_out_b", 4),
           ("L0_attn_ln1_g", 4), ("L0_attn_ln1_b", 4), ("L0_attn_ln2_g", 4), ("L0_attn_ln2_b", 4),
           ("L0_attn_mlp_b1", 16), ("L0_attn_mlp_b2", 4), ("L0_ffn_bg", 16), ("L0_ffn_bu", 16), ("L0_ffn_bd", 4),
           ("L1_xattn_ln_g", 4), ("L1_xattn_ln_b", 4), ("L1_xattn_bo", 4), ("L1_attn_A", 1), ("L1_attn_bb", 1),
           ("L1_attn_bc", 4), ("L1_attn_bd", 4), ("L1_attn_bdelta", 1), ("clock_b", 1), ("gate", 1)]
COLUMN_AT, at = {}, 0
for _k, _n in COLUMNS:
    COLUMN_AT[_k] = at
    at += _n
COLUMN_COLS = at


def perceiver(nc, dram, out):
    f32 = mybir.dt.float32
    u32 = mybir.dt.uint32
    ACT = mybir.ActivationFunctionType
    ALU = mybir.AluOpType
    AX = mybir.AxisListType
    ctx = ExitStack()
    with ctx:
        def sb(name, shape, dt=f32):
            return ctx.enter_context(nc.sbuf_tensor(name, shape, dt))

        def sem(name):
            return ctx.enter_context(nc.semaphore(name))

        consts = sb("consts", [128, TABLE_COLS])
        cols = sb("cols", [128, COLUMN_COLS])

        def tab(name, rows=128):
            a, n = TABLE_AT[name]
            return consts[0:rows, a:a + n]

        def col(name, i=0, rows=128):
            a = COLUMN_AT[name] + i
            return cols[0:rows, a:a + 1]

        XT = sb("XT", [128, 4, N])
        small = sb("small", [128, 64])
        f32r = mybir.dt.float32r
        ident_r = sb("ident_r", [128, 128], f32r)
        causal_r = sb("causal_r", [128, 128], f32r)
        with ExitStack() as until_last:
            def shared(name, shape):
                return until_last.enter_context(nc.sbuf_tensor(name, shape, f32))

            Y = shared("Y", [128, 4, N])
            XN = shared("XN", [128, 4, N])
            H = shared("H", [128, 2, 4, N])
            arena = shared("arena", [128, 6, 4, 512])
            RN = 17640
            R = shared("R", [128, RN])
        with ExitStack() as until_last:
            def gap(n):
                if n:
                    until_last.enter_context(nc.sbuf_tensor(f"gap{len(gaps)}", [128, n], f32))
                gaps.append(n)

            def shared_r(name, shape):
                return until_last.enter_context(nc.sbuf_tensor(name, shape, f32r))

            gaps = []
            gap(2048)
            ctl = shared_r("ctl", [128, 4, 2, 256])
            gap(4096 + 4096)
            wmh = shared_r("wmh", [128, 2, 4, 512])
            gap(4 * 2048)
            wml = shared_r("wml", [128, 2, 4, 512])
            gap(RN - 2048)
            cth = shared_r("cth", [128, 4, 2, 256])
        Yh, Yl = sb("Yh", [128, 4, N], f32r), sb("Yl", [128, 4, N], f32r)
        Hh, Hl = sb("Hh", [128, 4, N], f32r), sb("Hl", [128, 4, N], f32r)
        tern_up, tern_down = sb("tern_up", [128, 2, 4, 512], f32r), sb("tern_down", [128, 16, 512], f32r)

        def region(spec, base=R, limit=RN):
            got, at = {}, 0
            for name, shape in spec:
                n = int(np.prod(shape))
                ap = base[:, at:at + n]
                if len(shape) == 2:
                    ap = ap.rearrange("p (a b) -> p a b", a=shape[0])
                elif len(shape) == 3:
                    ap = ap.rearrange("p (a b c) -> p a b c", a=shape[0], b=shape[1])
                got[name] = ap
                at += n
            assert at <= limit, (at, limit)
            return got

        banks = [ctx.enter_context(nc.psum_tensor(f"bank{i}", [128, 512], f32)) for i in range(8)]

        act_bank_full, act_bank_free = sem("act_bank_full"), sem("act_bank_free")
        dve_bank_full, dve_bank_free = sem("dve_bank_full"), sem("dve_bank_free")
        slot_full = [sem(f"slot_full{i}") for i in range(6)]
        raw_full = [sem(f"raw_full{i}") for i in range(2)]
        stage_done = sem("stage_done")
        act_step, dve_step, pool_step = sem("act_step"), sem("dve_step"), sem("pool_step")
        in_consts, in_xT, in_xtm, in_ctx32 = sem("in_consts"), sem("in_xT"), sem("in_xtm"), sem("in_ctx32")
        in_small = sem("in_small")
        xn_tile = sem("xn_tile")
        a_std, a_var = sem("a_std"), sem("a_var")
        cx_ready, top_ready, topexp_ready = sem("cx_ready"), sem("top_ready"), sem("topexp_ready")
        w_ready, w_stored, m_loaded, mt_ready, m_zero = (sem("w_ready"), sem("w_stored"), sem("m_loaded"),
                                                         sem("mt_ready"), sem("m_zero"))
        ln_sq, ln_out = sem("ln_sq"), sem("ln_out")
        out_stored = sem("out_stored")
        S = {n: sem(n) for n in (
            "b_ckln", "b_clock", "b_gsp", "b_gcs", "b_gcp", "b_pdif", "b_pexp", "b_sq", "b_qk", "b_cos",
            "c_topin", "c_topexp", "c_p", "c_kb", "c_fac", "c_dense", "c_ee", "c_mul",
            "d_self", "d_qbd", "d_max", "d_ct", "d_chi", "d_clo", "d_whi", "d_wlo", "d_ct256", "d_probn",
            "e_a", "e_sp", "e_cum", "e_shift", "e_exp", "e_hh", "f_abs", "f_wp", "f_wf", "f_yhi",
            "f_ylo", "f_used", "f_hi", "f_q", "f_lo")}

        class Units:

            def __init__(self, banks):
                self.banks, self.at, self.n = banks, {}, 0

            def new(self, key):
                assert key not in self.at, key
                self.at[key] = self.n
                self.n += 1
                return self.n - 1

        UA, UV = Units(banks[0:4]), Units(banks[4:8])

        loads, slot_of, load_no, uses = [], {}, {}, [0] * 6
        turn = [0]

        def plan(name, src, slots=None):
            if slots is None:
                s = turn[0] % 6
                turn[0] += 1
            else:
                s = slots
            uses[s] += 1
            slot_of[name], load_no[name] = s, uses[s]
            loads.append((name, s, src))

        def rows4(w, r0=0, c0=0, nc_=512):
            return dram[w][r0:r0 + 512, c0:c0 + nc_].rearrange("(k p) n -> p k n", p=128)

        for n_, w in (("aq", "L0_xattn_Wq"), ("ak", "L0_xattn_Wk"), ("av", "L0_xattn_Wv"), ("ao", "L0_xattn_Wo"),
                      ("bv", "L0_attn_Wv"), ("bq", "L0_attn_Wq"), ("bk", "L0_attn_Wk"), ("bg", "L0_attn_gate_w"),
                      ("bp", "L0_attn_p_w"), ("bo", "L0_attn_out_w")):
            plan(n_, rows4(w))

        def quarters(up, down):
            for j in range(NQ):
                up(j)
                if j:
                    down(j - 1)
            down(NQ - 1)

        quarters(lambda j: plan(("b1", j), rows4("L0_attn_mlp_w1", 0, 512 * j)),
                 lambda j: plan(("b2", j), rows4("L0_attn_mlp_w2", 512 * j)))
        plan("cq", rows4("L0_ffn_Wq"))

        def plan_gu(j):
            plan(("cg", j), rows4("L0_ffn_Wg", 0, 512 * j))
            plan(("cu", j), rows4("L0_ffn_Wu", 0, 512 * j))

        quarters(plan_gu, lambda j: plan(("cd", j), rows4("L0_ffn_Wd", 512 * j)))
        for j in range(-1, NQ + 1):
            if j + 1 < NQ:
                plan(("ce", j + 1), rows4("downT", 0, 512 * j + 512))
            if j >= 1:
                plan(("cf", j - 1), rows4("L0_ffn_up_embed", 512 * j - 512))
        D_FIRST = len(loads)
        for h in range(2):
            plan(("dm", h), rows4("L1_xattn_Wm", 0, 512 * h), 4 + h)
        for cc in range(NCH):
            for w, src, off in (("dq", "L1_xattn_Wq", 0), ("dk", "L1_xattn_Wkv", 0), ("dv", "L1_xattn_Wkv", INNER)):
                for h in range(2):
                    plan((w, cc, h), rows4(src, 0, off + 512 * h), h)
            for h in range(2):
                plan(("dw", cc, h), rows4("L1_xattn_Wo", 512 * h), h)
        E_FIRST = len(loads)
        turn[0] = 0
        plan("edb", dram["L1_delta_b"].rearrange("(k p) n -> p k n", p=128))
        plan("ed", rows4("L1_attn_Wd"))
        last_loads = [("ff", 0)] + [("fa", j) for j in range(NQ)] + [("fp", 0)]
        for j in range(1, NQ):
            last_loads += [("ff", j), ("fp", j)]
        raw_no = {name: i for i, name in enumerate(last_loads)}
        released = {}

        def W(name):
            return arena[:, slot_of[name], :, :]

        RA = region([("m", (TT, 128)), ("mt", (TT, 128)), ("qs", (2, 512)), ("junk", (1, 512)), ("C", (1, 8)), ("cx", (8, 4)),
                     ("st", (8, 6)), ("mv", (8, 2)), ("cr", (1, 32)), ("v8", (1, 8)), ("i8", (1, 8)), ("e8", (1, 8)),
                     ("fi8", (1, 8)),
                     ("eq", (6, 32)), ("w2", (2, 32)), ("bq", (1, 512)), ("bk", (1, 512))])
        xtm, ctm = XN[:, :, :].rearrange("p a b -> p (a b)").rearrange("p (t d) -> p t d", t=8), \
            Y[:, :, :].rearrange("p a b -> p (a b)").rearrange("p (t d) -> p t d", t=8)
        LQ, LK = H[:, 0], H[:, 1]
        RL = region([("sq", (2, 2048)), ("r1", (2, 512)), ("r2", (2, 512))])
        RB = region([("v", (8, 512)), ("ot", (4, N)), ("reset", (1, N)), ("ck", (1, N)), ("p", (8, 512)), ("p2", (1, N)),
                     ("cw", (4, 16)), ("t", (2, N)), ("pm", (1, 32)), ("den", (1, 128))])
        RC = region([("sim", (8, 512)), ("kb", (4, 128)), ("Tx", (8, PH, 32)), ("Ex", (8, PH, 32)), ("Ry", (8, PH, 64)),
                     ("Ey", (8, PH, 64)), ("eq", (1, 2048)), ("s", (4, 512)), ("xv", (1, 8)),
                     ("pj", (2, 512))])
        XNf = XN[:, :, :].rearrange("p a b -> p (a b)")
        SJ = [H[:, 0], H[:, 1], XN]
        XNf = XN[:, :, :].rearrange("p a b -> p (a b)")
        RT = region([("tv", (8, 8)), ("ti", (8, 8)), ("tf", (2, 8, 8)), ("cand", (PH, 64)), ("rep", (PH, 64)), ("t8", (PH, 8)),
                     ("na", (2, PH, 8)), ("z", (1, 4)), ("rz", (1, 4)), ("m0", (1, 4)), ("ge", (PH, 8)),
                     ("rs", (PH, 8)), ("sd", (8, 64)), ("sel", (PH, 64))], base=XNf, limit=4096)
        RD = region([("kt", (8, 2, 322)), ("vt", (2, 3, 1024)), ("ct", (4, 514)), ("m256", (8, 32)), ("c256", (4, 32)), ("qbd", (2, 512))],
                    limit=RN - 2048)
        RDa = region([("p", (8, 289)), ("pt", (4, 384))],
                     base=arena[:, 2:4, :, :].rearrange("p s a b -> p (s a b)"), limit=4096)
        gate_buf, p_buf = [H[:, 1, 0, :], H[:, 1, 3, :]], [H[:, 1, 1, :], RB["p2"][:, 0, :]]
        EE = RC["sim"].rearrange("p t n -> p (t n)").rearrange("p (i n) -> p i n", i=2)
        kt = RD["kt"]
        qbd = [RD["qbd"][:, i].rearrange("p (o c) -> p o c", o=8) for i in range(2)]
        ct = RD["ct"].rearrange("p k (b m) -> p k b m", b=2)[:, :, :, 0:256]
        Q1 = Y[:, 0:2].rearrange("p a b -> p (a b)").rearrange("p (o t) -> p o t", o=8)
        K1 = H[:, 0, 0:2].rearrange("p a b -> p (a b)").rearrange("p (o t) -> p o t", o=8)
        V1 = H[:, 0, 2:4].rearrange("p a b -> p (a b)").rearrange("p (o t) -> p o t", o=8)
        RE = region([("dl", (1, N)), ("bb", (1, N)), ("z", (2, N)), ("t", (2, N)), ("reset", (1, N)), ("hh", (1, N)),
                     ("wc", (1, 512))])
        RE["sh"] = R[:, 13544:13544 + N].rearrange("p (b l) -> p b l", l=L)
        RF = region([("vT", (4, 16)), ("fb", (1, 16)), ("uT", (1, F)), ("z", (1, N)), ("z2", (1, N)),
                     ("half", (1, 512)), ("s", (1, 512)), ("sp", (1, 512)), ("ru", (1, 512)), ("diag", (1, 128)),
                     ("gap", (1, 8)), ("aw", (1, 2048)), ("r", (2, 512))])
        raw = [R[:, 9448 + 2048 * i:9448 + 2048 * i + 2048].rearrange("p (k n) -> p k n", k=4) for i in range(2)]
        y5f = R[:, 13544:17640]
        y5 = y5f.rearrange("p (k n) -> p k n", k=4)
        aw = [RF["aw"][:, 0, :].rearrange("p (k n) -> p k n", k=4)] + \
             [y5f[:, 2048 * i:2048 * i + 2048].rearrange("p (k n) -> p k n", k=4) for i in range(2)]
        MAGS = [("ff", 0), ("fa", 0), ("fa", 1), ("fa", 2), ("fa", 3), ("ff", 1), ("ff", 2), ("ff", 3)]
        LNS = [dict(src=XT, dst=XN, double=True, plain=Y, g="L0_attn_ln1_g", b="L0_attn_ln1_b"),
               dict(src=Y, dst=XN, double=False, plain=None, g="L0_attn_ln2_g", b="L0_attn_ln2_b"),
               dict(src=XT, dst=Y, double=False, plain=None, g=None, b=None),
               dict(src=XT, dst=XN, double=True, plain=None, g="L1_xattn_ln_g", b="L1_xattn_ln_b"),
               dict(src=XT, dst=Y, double=False, plain=None, g=None, b=None),
               dict(src=XT, dst=y5, double=False, plain=None, g=None, b=None)]

        def ch(c):
            return slice(512 * c, 512 * c + 512)

        def cs(cc):
            return slice(CT * cc, CT * cc + CT)

        def tl(t):
            return slice(128 * t, 128 * t + 128)

        d_end = [0]
        block = ctx.enter_context(nc.Block())

        @block.tensor
        def _(pe):
            stage = [0]
            mm = nc.tensor.matmul

            def end_stage():
                stage[0] += 1
                pe.drain().then_inc(stage_done, 1)
                pe.wait_ge(stage_done, 4 * stage[0])

            def open_act(key):
                u = UA.new(key)
                if u >= 4:
                    pe.wait_ge(act_bank_free, u - 3)
                return UA.banks[u % 4]

            def open_dve(key):
                u = UV.new(key)
                if u >= 4:
                    pe.wait_ge(dve_bank_free, u - 3)
                return UV.banks[u % 4]

            def on_act(key):
                pe.wait_ge(act_bank_free, UA.at[key] + 1)

            def on_dve(key):
                pe.wait_ge(dve_bank_free, UV.at[key] + 1)

            def weight(name):
                pe.wait_ge(slot_full[slot_of[name]], 16 * load_no[name])

            def free_after_act(name):
                released[name] = (act_bank_full, UA.n)

            def free_after_dve(name):
                released[name] = (dve_bank_full, UV.n)

            def linear(bank, w, cols_, x, xc, more=False):
                for k in range(4):
                    last = mm(bank, w[:, k, cols_], x[:, k, xc], start=(k == 0), stop=(k == 3 and not more))
                return last

            def layernorm(l):
                for c in range(C2):
                    b = open_dve(("mean", l, c))
                    linear(b[:, :], tab("mean_ones").unsqueeze(1).to_broadcast([128, 4, 128]), slice(0, 128), LNS[l]["src"], ch(c)
                           ).then_inc(dve_bank_full, 1)
                for c in range(C2):
                    pe.wait_ge(ln_sq, 2 * l + c + 1)
                    b = open_act(("var", l, c))
                    sq = RL["sq"][:, c].rearrange("p (k n) -> p k n", k=4)
                    linear(b[:, :], tab("mean_ones").unsqueeze(1).to_broadcast([128, 4, 128]), slice(0, 128), sq, slice(0, 512)
                           ).then_inc(act_bank_full, 1)
                end_stage()

            pe.wait_ge(in_consts, 32)
            pe.wait_ge(in_small, 32)
            pe.wait_ge(in_ctx32, 64)
            for t in range(TT):
                b = open_act(("ldk", t))
                for k in range(4):
                    last = mm(b[:, tl(k)], ctm[:, t, tl(k)], tab("dft"), start=True, stop=True)
                last.then_inc(act_bank_full, 1)
            for t in range(TT):
                pe.wait_ge(xn_tile, t + 1)
                b = open_dve(("ldq", t))
                for k in range(4):
                    last = mm(b[:, tl(k)], xtm[:, t, tl(k)], tab("dft"), start=True, stop=True)
                last.then_inc(dve_bank_full, 1)
            weight("aq")
            weight("ak")
            for t in range(TT):
                on_dve(("ldq", t))
                b = open_act(("qf", t))
                for k in range(4):
                    mm(b[:, :], LQ[:, k, tl(t)], W("aq")[:, k, :], start=(k == 0), stop=False)
                mm(b[:, :], tab("dc", 1), RA["bq"][0:1, 0, :], start=False, stop=True).then_inc(act_bank_full, 1)
                on_act(("ldk", t))
                b = open_dve(("kf", t))
                for k in range(4):
                    mm(b[:, :], LK[:, k, tl(t)], W("ak")[:, k, :], start=(k == 0), stop=False)
                mm(b[:, :], tab("dc", 1), RA["bk"][0:1, 0, :], start=False, stop=True).then_inc(dve_bank_full, 1)
            free_after_act("aq")
            free_after_dve("ak")
            pe.wait_ge(cx_ready, 1)
            b = open_dve("corr")
            mm(b[0:32, 0:32], RA["cx"].rearrange("p a b -> p (a b)"), tab("corr"), start=True, stop=True
               ).then_inc(dve_bank_full, 1)
            pe.wait_ge(mt_ready, 1)
            for t in range(TT):
                b = open_act(("agg", t))
                for k in range(4):
                    last = mm(b[:, tl(k)], ctm[:, t, tl(k)], RA["mt"][:, t, :], start=True, stop=True)
                last.then_inc(act_bank_full, 1)
            on_act(("agg", TT - 1))
            weight("av")
            for o in range(4):
                for c in range(C2):
                    b = open_act(("av", o, c))
                    linear(b[:, :], W("av"), tl(o), LQ, ch(c)).then_inc(act_bank_full, 1)
            free_after_act("av")
            on_act(("av", 3, C2 - 1))
            weight("ao")
            for o in range(4):
                for c in range(C2):
                    b = open_dve(("ao", o, c))
                    linear(b[:, :], W("ao"), tl(o), LK, ch(c)).then_inc(dve_bank_full, 1)
            free_after_dve("ao")
            end_stage()

            layernorm(0)
            pe.wait_ge(in_small, 48)
            for c in range(C2):
                b = open_act(("clock", c))
                for k in range(4):
                    last = mm(b[0:16, :], RB["cw"][:, k, :], XN[:, k, ch(c)], start=(k == 0), stop=(k == 3))
                last.then_inc(act_bank_full, 1)
            weight("bv")
            for t in range(TT):
                b = open_act(("v", t))
                for k in range(4):
                    last = mm(b[:, :], XN[:, k, tl(t)], W("bv")[:, k, :], start=(k == 0), stop=(k == 3))
                last.then_inc(act_bank_full, 1)
            free_after_act("bv")
            for w in ("bq", "bk", "bg", "bp"):
                weight(w)

            def project(o, names):
                for w in names:
                    for c in range(C2):
                        b = open_act((w, o, c))
                        linear(b[:, :], W(w), tl(o), XN, ch(c)).then_inc(act_bank_full, 1)

            def clock_norms_rotations(o):
                for c in range(C2):
                    pe.wait_ge(S["b_clock"], C2)
                    b = open_dve(("ck", o, c))
                    mm(b[:, :], tab("expand", 16)[:, tl(o)], RB["ck"][0:16, 0, ch(c)], start=True, stop=True
                       ).then_inc(dve_bank_full, 1)
                for i, w in enumerate(("bq", "bk")):
                    for c in range(C2):
                        on_act((w, o, c))
                        b = open_dve(("r" + w, o, c))
                        mm(b[:, :], tab("rot"), H[:, 0, i, ch(c)], start=True, stop=True).then_inc(dve_bank_full, 1)
                for i, w in enumerate(("bq", "bk")):
                    for c in range(C2):
                        pe.wait_ge(S["b_sq"], 4 * o + 2 * i + c + 1)
                        b = open_act(("n" + w, o, c))
                        mm(b[:, :], tab("head_ones"), H[:, 0, 2 + i, ch(c)], start=True, stop=True).then_inc(act_bank_full, 1)

            def scores(o):
                pe.wait_ge(S["b_qk"], 2 * (o + 1))
                for hf in range(2):
                    for h in range(4):
                        hp = slice(32 * h, 32 * h + 32)
                        b = open_act(("s", o, hf, h))
                        mm(b[:, :].rearrange("p (t n) -> p t n", t=4), ident_r[:, :],
                           causal_r[:, :].unsqueeze(1).to_broadcast([128, 4, 128]), start=True, stop=False)
                        for t in range(4):
                            tt = tl(4 * hf + t)
                            last = mm(b[:, tl(t)], H[hp, 0, 1, tt], H[hp, 0, 0, tt], start=False, stop=(t == 3),
                                      tile_position=(32 * h, 0))
                        last.then_inc(act_bank_full, 1)

            def values(o):
                for tt in range(TT):
                    on_act(("s", o, tt // 4, 3))
                    b = open_dve(("pv", o, tt))
                    for h in range(4):
                        hp = slice(32 * h, 32 * h + 32)
                        pt_ = RB["p"][:, 4 * (tt // 4) + h, tl(tt % 4)]
                        mm(b[hp, 0:128], RB["v"][:, tt, 128 * o + 32 * h:128 * o + 32 * h + 32], pt_,
                           start=True, stop=True, tile_position=(0, 32 * h))
                        last = mm(b[hp, 128:256], tab("ones"), pt_, start=True, stop=True, tile_position=(0, 32 * h))
                    last.then_inc(dve_bank_full, 1)

            project(0, ("bg", "bp", "bq", "bk"))
            clock_norms_rotations(0)
            for o in range(4):
                if o < 3:
                    project(o + 1, ("bg", "bp"))
                scores(o)
                if o < 3:
                    project(o + 1, ("bq", "bk"))
                    clock_norms_rotations(o + 1)
                values(o)
            for w in ("bq", "bk", "bg", "bp"):
                free_after_act(w)
            on_dve(("pv", 3, TT - 1))
            weight("bo")
            for o in range(4):
                for c in range(C2):
                    b = open_dve(("bo", o, c))
                    linear(b[:, :], W("bo"), tl(o), RB["ot"], ch(c)).then_inc(dve_bank_full, 1)
            free_after_dve("bo")
            end_stage()
            layernorm(1)

            def b_up(j):
                weight(("b1", j))
                for o in range(4):
                    for c in range(C2):
                        b = open_act(("b1", j, o, c))
                        linear(b[:, :], W(("b1", j)), tl(o), XN, ch(c)).then_inc(act_bank_full, 1)
                free_after_act(("b1", j))

            def down(name, j, ready):
                weight((name, j))
                ready(j)
                for o in range(4):
                    for c in range(C2):
                        b = open_dve((name, j, o, c))
                        linear(b[:, :], W((name, j)), tl(o), H[:, j % 2], ch(c)).then_inc(dve_bank_full, 1)
                free_after_dve((name, j))

            quarters(b_up, lambda j: down("b2", j, lambda j: on_act(("b1", j, 3, C2 - 1))))
            end_stage()

            layernorm(2)
            weight("cq")
            for o in range(4):
                for c in range(C2):
                    b = open_act(("cq", o, c))
                    linear(b[:, :], W("cq"), tl(o), Y, ch(c)).then_inc(act_bank_full, 1)
            free_after_act("cq")
            on_act(("cq", 3, C2 - 1))
            pe.wait_ge(S["c_kb"], 16)
            for t in range(TT):
                b = open_act(("sim", t))
                for j in range(4):
                    last = mm(b[:, tl(j)], XN[:, j, tl(t)], RC["kb"][:, j, :], start=True, stop=True)
                last.then_inc(act_bank_full, 1)

            def c_up(j):
                weight(("cg", j))
                weight(("cu", j))
                for o in range(4):
                    for c in range(C2):
                        b = open_act(("cg", j, o, c))
                        linear(b[:, :], W(("cg", j)), tl(o), Y, ch(c)).then_inc(act_bank_full, 1)
                        b = open_dve(("cu", j, o, c))
                        linear(b[:, :], W(("cu", j)), tl(o), Y, ch(c)).then_inc(dve_bank_full, 1)
                free_after_act(("cg", j))
                free_after_dve(("cu", j))

            quarters(c_up, lambda j: down("cd", j, lambda j: on_dve(("cu", j, 3, C2 - 1))))

            for j in range(-1, NQ + 1):
                if j + 1 < NQ:
                    weight(("ce", j + 1))
                if j >= 1:
                    weight(("cf", j - 1))
                for t in range(TT):
                    if j + 1 < NQ:
                        b = open_act(("ce", j + 1, t))
                        linear(b[:, :], W(("ce", j + 1)), tl(t % 4), Y, ch(t // 4)).then_inc(act_bank_full, 1)
                    if 0 <= j < NQ:
                        pe.wait_ge(S["c_p"], TT * j + t + 1)
                        b = open_dve(("pt", j, t))
                        for e in range(4):
                            last = nc.tensor.transpose(b[:, tl(e)], RC["pj"][:, t % 2, tl(e)], tab("ident"))
                        last.then_inc(dve_bank_full, 1)
                    if j >= 1:
                        if t == 0:
                            on_dve(("pt", j - 1, TT - 1))
                        b = open_dve(("cf", j - 1, t))
                        linear(b[:, :], W(("cf", j - 1)), tl(t % 4), SJ[(j - 1) % 3], ch(t // 4)).then_inc(dve_bank_full, 1)
                if j + 1 < NQ:
                    free_after_act(("ce", j + 1))
                if j >= 1:
                    free_after_dve(("cf", j - 1))
            end_stage()

            layernorm(3)

            def pv_group(b, bb, g):
                on_dve(("ptr", bb, g))
                if g == 0:
                    on_act(("vt", bb, 2, 1))
                    on_dve(("vt", bb, 2, 0))
                for x in range(2):
                    o = 2 * g + x
                    for blk, n in ((0, 128), (1, 128), (2, 33)):
                        last = mm(b[:, 64 * o:64 * o + 64], RD["vt"][0:n, bb % 2, blk, tl(o)],
                                  RDa["pt"][0:n, g, 128 * blk + 64 * x:128 * blk + 64 * x + 64],
                                  start=(blk == 0), stop=(blk == 2))
                return last

            pe.wait_ge(S["d_ct256"], 16)
            weight(("dm", 0))
            weight(("dm", 1))
            b = open_act("m256")
            for o in range(OT1):
                for k in range(4):
                    last = mm(b[:, 32 * o:32 * o + 32], W(("dm", o // 4))[:, k, tl(o % 4)], RD["c256"][:, k, :],
                              start=(k == 0), stop=(k == 3))
            last.then_inc(act_bank_full, 1)
            def memory(pr):
                pe.wait_ge(S["d_clo"], pr + 1)
                for o in range(OT1):
                    b = open_act(("mem", pr, o))
                    for k in range(4):
                        wh, wl = wmh[:, o // 4, k, tl(o % 4)], wml[:, o // 4, k, tl(o % 4)]
                        for n_, (w_, c_) in enumerate(((wh, cth), (wh, ctl), (wl, cth))):
                            last = mm(b[:, :].rearrange("p (a c) -> p a c", a=2), w_, c_[:, k, :, :],
                                      start=(k == 0 and n_ == 0), stop=(k == 3 and n_ == 2))
                    last.then_inc(act_bank_full, 1)

            for cc in range(NCH):
                for w in ("dq", "dk", "dv"):
                    for o in range(OT1):
                        weight((w, cc, o // 4))
                        b = open_act((w, cc, o))
                        linear(b[:, 0:CT], W((w, cc, o // 4)), tl(o % 4), XN, cs(cc)).then_inc(act_bank_full, 1)
                        free_after_act((w, cc, o // 4))
                if cc == 0:
                    pe.wait_ge(S["d_wlo"], 2)
                    memory(0)
                for pr in range(CB // 2 * cc, CB // 2 * (cc + 1)):
                    on_act(("mem", pr, OT1 - 1))
                    for i in range(2):
                        bb = 2 * pr + i
                        pe.wait_ge(S["d_self"], bb + 1)
                        for blk, (a, n) in enumerate(((0, 128), (128, 128), (289, 33))):
                            for half, (open_, full) in enumerate(((open_dve, dve_bank_full), (open_act, act_bank_full))):
                                b = open_(("vt", bb, blk, half))
                                for o in range(4):
                                    last = nc.tensor.transpose(b[0:n, tl(o)], kt[:, 4 * half + o, i, a:a + n], tab("ident"))
                                last.then_inc(full, 1)
                        pe.wait_ge(S["d_qbd"], bb + 1)
                        for g in range(4):
                            b = open_act(("sc", bb, g))
                            for x in range(2):
                                last = mm(b[64 * x:64 * x + 64, 0:289], qbd[bb % 2][:, 2 * g + x, :],
                                          kt[:, 2 * g + x, i, 0:289], start=True, stop=True, tile_position=(0, 64 * x))
                            last.then_inc(act_bank_full, 1)
                    if pr + 1 < B // 2:
                        memory(pr + 1)
                    steps_ = [(2 * pr + i, g) for i in range(2) for g in range(4)]
                    for n_ in range(10):
                        if n_ < 8:
                            bb, g = steps_[n_]
                            pe.wait_ge(S["d_probn"], 4 * bb + g + 1)
                            pr_t = RDa["p"][:, 4 * (bb % 2) + g, :]
                            b = open_dve(("ptr", bb, g))
                            nc.tensor.transpose(b[:, 0:128], pr_t[:, 0:128], tab("ident"))
                            nc.tensor.transpose(b[:, 128:256], pr_t[:, 128:256], tab("ident"))
                            nc.tensor.transpose(b[0:33, 256:384], pr_t[:, 256:289], tab("ident")).then_inc(dve_bank_full, 1)
                        if n_ >= 2:
                            bb, g = steps_[n_ - 2]
                            if g == 0:
                                bo_ = open_act(("pvd", bb))
                            last = pv_group(bo_, bb, g)
                            if g == 3:
                                last.then_inc(act_bank_full, 1)
                on_act(("pvd", CB * cc + CB - 1))
                for h in range(2):
                    weight(("dw", cc, h))
                for o in range(4):
                    b = open_dve(("dw", cc, o))
                    for k in range(8):
                        last = mm(b[:, 0:CT], W(("dw", cc, k // 4))[:, k % 4, tl(o)], Q1[:, k, :], start=(k == 0), stop=(k == 7))
                    last.then_inc(dve_bank_full, 1)
                for h in range(2):
                    free_after_dve(("dw", cc, h))
            for h in range(2):
                released[("dm", h)] = (stage_done, 4 * (stage[0] + 1))
            end_stage()
            d_end[0] = stage[0]

            layernorm(4)
            weight("edb")
            pe.wait_ge(in_small, 64)
            for c in range(C2):
                b = open_act(("dl", c))
                linear(b[:, :], W("edb"), slice(0, 128), Y, ch(c)).then_inc(act_bank_full, 1)
            for c in range(C2):
                b = open_dve(("bb", c))
                linear(b[:, :], W("edb"), slice(128, 256), Y, ch(c)).then_inc(dve_bank_full, 1)
            free_after_dve("edb")
            weight("ed")
            for o in range(4):
                for c in range(C2):
                    b = open_dve(("ed", o, c))
                    linear(b[:, :], W("ed"), tl(o), Y, ch(c), more=True)
                    pe.wait_ge(S["e_hh"], 1)
                    mm(b[:, :], RE["wc"][:, 0, tl(o)], RE["hh"][:, 0, ch(c)], start=False, stop=True).then_inc(dve_bank_full, 1)
            free_after_dve("ed")
            end_stage()

            layernorm(5)
            pe.wait_ge(in_small, 112)
            for c in range(C2):
                b = open_act(("z", c))
                for k in range(4):
                    last = mm(b[0:16, :], RF["vT"][:, k, :], y5[:, k, ch(c)], start=(k == 0), stop=(k == 3))
                last.then_inc(act_bank_full, 1)

            def f_scale(j):
                n = MAGS.index(("ff", j))
                pe.wait_ge(S["f_abs"], n + 1)
                b = open_dve(("fs", j))
                for k in range(4):
                    last = mm(b[:, :], tab("mean_ones"), aw[n % 3][:, k, :], start=(k == 0), stop=(k == 3))
                last.then_inc(dve_bank_full, 1)

            f_scale(0)
            for c in range(C2):
                on_act(("z", c))
                b = open_act(("z2", c))
                mm(b[0:16, :], RF["fb"][0:16, 0, :], RF["z"][0:16, 0, ch(c)], start=True, stop=True).then_inc(act_bank_full, 1)

            def f_up(j, c):
                pe.wait_ge(S["f_wf"], j + 1)
                if j == 0:
                    on_act(("z2", c))
                    pe.wait_ge(S["f_ylo"], c + 1)
                for o in range(4):
                    b = open_act(("ff", j, c, o))
                    for k in range(4):
                        for part in (Yh, Yl):
                            mm(b[:, :], tern_up[:, j % 2, k, tl(o)], part[:, k, ch(c)], start=(k == 0 and part is Yh), stop=False)
                    mm(b[:, :], RF["uT"][0:16, 0, 512 * j + 128 * o:512 * j + 128 * o + 128], RF["z2"][0:16, 0, ch(c)],
                       start=False, stop=True).then_inc(act_bank_full, 1)

            def f_down(j, c):
                pe.wait_ge(S["f_wp"], j + 1)
                pe.wait_ge(S["f_lo"], 8 * j + 4 * c + 4)
                for o in range(4):
                    b = open_dve(("fp", j, c, o))
                    for k in range(4):
                        for part in (Hh, Hl):
                            last = mm(b[:, :], tern_down[:, 4 * j + k, tl(o)], part[:, k, ch(c)],
                                      start=(k == 0 and part is Hh), stop=(k == 3 and part is Hl))
                    last.then_inc(dve_bank_full, 1)

            for j in range(NQ):
                f_up(j, 0)
                if j == 0:
                    b = open_dve("fps")
                    for i in range(NQ):
                        n = MAGS.index(("fa", i))
                        pe.wait_ge(S["f_abs"], n + 1)
                        for k in range(4):
                            last = mm(b[:, :], tab("hid_ones"), aw[n % 3][:, k, :], start=(i == 0 and k == 0),
                                      stop=(i == 3 and k == 3))
                        last.then_inc(S["f_used"] if i < NQ - 1 else dve_bank_full, 1)
                if j + 1 < NQ:
                    f_scale(j + 1)
                f_up(j, 1)
                f_down(j, 0)
                f_down(j, 1)
            end_stage()

        def common(eng, step_sem):
            stage, steps = [0], [0]

            def end_stage():
                stage[0] += 1
                eng.drain().then_inc(stage_done, 1)
                eng.wait_ge(stage_done, 4 * stage[0])

            def step(ins):
                ins.then_inc(step_sem, 1)
                steps[0] += 1
                eng.wait_ge(step_sem, steps[0])

            return end_stage, step

        @block.scalar
        def _(act):
            end_stage, step = common(act, act_step)
            fn = nc.scalar.activation

            def unit(key):
                u = UA.at[key]
                act.wait_ge(act_bank_full, u + 1)
                return UA.banks[u % 4]

            def copy_out(dst, src):
                fn(dst, src, ACT.Copy).then_inc(act_bank_free, 1)

            def vrow(key):
                act.wait_ge(dve_bank_free, UV.at[key] + 1)

            def layernorm(l):
                spec = LNS[l]
                for c in range(C2):
                    vrow(("mean", l, c))
                    sq = RL["sq"][:, c].rearrange("p (k n) -> p k n", k=4)
                    fn(sq, spec["dst"][:, :, ch(c)], ACT.Square).then_inc(ln_sq, 1)
                for c in range(C2):
                    b = unit(("var", l, c))
                    if spec["plain"] is not None:
                        fn(RL["r1"][:, c, :], b[:, :], ACT.Sqrt, bias=tab("eps"))
                    if spec["double"]:
                        fn(RL["r2"][:, c, :], b[:, :], ACT.Sqrt, bias=tab("eps2"), scale=1.0 + EPS).then_inc(act_bank_free, 1)
                    else:
                        fn(RL["r2"][:, c, :], b[:, :], ACT.Sqrt, bias=tab("eps")).then_inc(act_bank_free, 1)
                if spec["g"]:
                    for c in range(C2):
                        act.wait_ge(ln_out, 2 * l + c + 1)
                        for k in range(4):
                            x = spec["dst"][:, k, ch(c)]
                            fn(x, x, ACT.Identity, scale=col(spec["g"], k), bias=col(spec["b"], k))
                end_stage()

            act.wait_ge(in_consts, 32)
            act.wait_ge(a_var, 1)
            fn(small[:, 0:8], RA["mv"][:, :, 1], ACT.Sqrt, bias=tab("eps")).then_inc(a_std, 1)
            for t in range(TT):
                b = unit(("ldk", t))
                copy_out(LK[:, :, tl(t)], b[:, :].rearrange("p (k n) -> p k n", k=4))
            for t in range(TT):
                b = unit(("qf", t))
                if t >= 2:
                    vrow(("kf", t - 2))
                copy_out(RA["qs"][:, t % 2, :], b[:, :])
            act.wait_ge(top_ready, 1)
            fn(RA["e8"][0:32, 0, 0:TOPK], RA["v8"][0:32, 0, 0:TOPK], ACT.Exp, bias=small[0:32, 8:9],
               accum_out=small[0:32, 9:10]).then_inc(topexp_ready, 1)
            for t in range(TT):
                b = unit(("agg", t))
                copy_out(LQ[:, :, tl(t)], b[:, :].rearrange("p (k n) -> p k n", k=4))
            for o in range(4):
                for c in range(C2):
                    b = unit(("av", o, c))
                    fn(LK[:, o, ch(c)], b[:, :], ACT.Identity, bias=col("L0_xattn_bv", o)).then_inc(act_bank_free, 1)
            end_stage()

            layernorm(0)
            for c in range(C2):
                b = unit(("clock", c))
                fn(RB["ck"][0:16, 0, ch(c)], b[0:16, :], ACT.Identity, bias=col("clock_b", 0, 16)).then_inc(act_bank_free, 1)
            act.wait_ge(act_bank_free, UA.at[("clock", C2 - 1)] + 1)

            def log1pexp(z, t, done):
                step(fn(t, z, ACT.Abs))
                step(fn(t, t, ACT.Exp, scale=-1.0))
                fn(t, t, ACT.Ln, bias=tab("one")[0:z.shape[0], :]).then_inc(done, 1)

            log1pexp(RB["ck"][0:16, 0, :], RB["t"][0:16, 0, :], S["b_ckln"])
            for t in range(TT):
                b = unit(("v", t))
                copy_out(RB["v"][:, t, :], b[:, :])

            def gates_in(o):
                for w, dst, bias in (("bg", gate_buf, "L0_attn_gate_b"), ("bp", p_buf, "L0_attn_p_b")):
                    for c in range(C2):
                        b = unit((w, o, c))
                        fn(dst[o % 2][:, ch(c)], b[:, :], ACT.Identity, bias=col(bias, o)).then_inc(act_bank_free, 1)

            def factors(o):
                act.wait_ge(act_bank_free, UA.at[("bg", o, C2 - 1)] + 1)
                if o == 0:
                    act.wait_ge(S["b_clock"], C2)
                log1pexp(gate_buf[o % 2], RB["t"][:, 0, :], S["b_gsp"])
                for i, w in enumerate(("bq", "bk")):
                    for c in range(C2):
                        b = unit((w, o, c))
                        fn(H[:, 0, 2 + i, ch(c)], b[:, :], ACT.Square).then_inc(S["b_sq"], 1)
                        copy_out(H[:, 0, i, ch(c)], b[:, :])
                act.wait_ge(S["b_gcs"], o + 1)
                fn(gate_buf[o % 2], RB["t"][:, 1, :], ACT.Exp).then_inc(S["b_gcp"], 1)
                act.wait_ge(S["b_pdif"], o + 1)
                fn(p_buf[o % 2], p_buf[o % 2], ACT.Exp).then_inc(S["b_pexp"], 1)
                for i, w in enumerate(("bq", "bk")):
                    for c in range(C2):
                        b = unit(("n" + w, o, c))
                        fn(H[:, 0, 2 + i, ch(c)], b[:, :], ACT.Sqrt).then_inc(act_bank_free, 1)

            gates_in(0)
            factors(0)
            for o in range(4):
                if o < 3:
                    gates_in(o + 1)
                for hf in range(2):
                    for h in range(4):
                        b = unit(("s", o, hf, h))
                        fn(RB["p"][:, 4 * hf + h, :], b[:, :], ACT.Exp, scale=32 ** -0.5).then_inc(act_bank_free, 1)
                if o < 3:
                    factors(o + 1)
            end_stage()
            layernorm(1)

            def b_up(j):
                if j >= 2:
                    act.wait_ge(dve_bank_full, UV.at[("b2", j - 2, 3, C2 - 1)] + 1)
                for o in range(4):
                    for c in range(C2):
                        b = unit(("b1", j, o, c))
                        fn(H[:, j % 2, o, ch(c)], b[:, :], ACT.Gelu, bias=col("L0_attn_mlp_b1", 4 * j + o)
                           ).then_inc(act_bank_free, 1)

            quarters(b_up, lambda j: None)
            end_stage()

            layernorm(2)
            for o in range(4):
                for c in range(C2):
                    copy_out(XN[:, o, ch(c)], unit(("cq", o, c))[:, :])
            for t in range(TT):
                copy_out(RC["sim"][:, t, :], unit(("sim", t))[:, :])
            gated = [0]

            def c_up(j):
                for o in range(4):
                    for c in range(C2):
                        b = unit(("cg", j, o, c))
                        if gated[0] >= 4:
                            vrow(gates[gated[0] - 4])
                        fn(RC["s"][:, gated[0] % 4, :], b[:, :], ACT.Silu, bias=col("L0_ffn_bg", 4 * j + o)
                           ).then_inc(act_bank_free, 1)
                        gated[0] += 1
                    if o % 2 == 0:
                        act.wait_ge(S["c_topin"], 2 * j + o // 2 + 1)
                        fn(RT["rep"], RT["rep"], ACT.Exp)
                        fn(RT["sd"], RT["sd"], ACT.Exp).then_inc(S["c_topexp"], 1)

            gates = [("cu", j, o, c) for j in range(NQ) for o in range(4) for c in range(C2)]
            for j in range(NQ):
                c_up(j)
            for j in range(NQ):
                if j == 0:
                    act.wait_ge(dve_bank_full, UV.at[("cd", 3, 3, C2 - 1)] + 1)
                if j >= 3:
                    act.wait_ge(dve_bank_full, UV.at[("cf", j - 3, TT - 1)] + 1)
                for t in range(TT):
                    b = unit(("ce", j, t))
                    fn(SJ[j % 3][:, t % 4, ch(t // 4)], b[:, :], ACT.Silu).then_inc(act_bank_free, 1)
            end_stage()

            layernorm(3)
            b = unit("m256")
            copy_out(RD["m256"], b[:, 0:256].rearrange("p (o b) -> p o b", o=8))

            def split_high(pr):
                act.wait_ge(S["d_ct"], 16 * (pr + 1))
                if pr:
                    act.wait_ge(act_bank_full, UA.at[("mem", pr - 1, OT1 - 1)] + 1)
                fn(cth[:, :, :, :], ct, ACT.Copy).then_inc(S["d_chi"], 1)

            def memory(pr):
                if pr:
                    act.wait_ge(act_bank_full, UA.at[("sc", 2 * pr - 1, 3)] + 1)
                for o in range(OT1):
                    b = unit(("mem", pr, o))
                    copy_out(kt[:, o, :, 0:256], b[:, :].rearrange("p (i m) -> p i m", i=2))
                if pr + 1 < B // 2:
                    split_high(pr + 1)

            for h in range(2):
                fn(wmh[:, h], W(("dm", h)), ACT.Copy).then_inc(S["d_whi"], 1)
            split_high(0)
            for cc in range(NCH):
                for w, dst in (("dq", Q1), ("dk", K1), ("dv", V1)):
                    for o in range(OT1):
                        copy_out(dst[:, o, :], unit((w, cc, o))[:, 0:CT])
                if cc == 0:
                    memory(0)
                for pr in range(CB // 2 * cc, CB // 2 * (cc + 1)):
                    for bb in (2 * pr, 2 * pr + 1):
                        if bb >= 2:
                            act.wait_ge(act_bank_full, UA.at[("pvd", bb - 2)] + 1)
                        for blk, n in ((0, 128), (1, 128), (2, 33)):
                            copy_out(RD["vt"][0:n, bb % 2, blk, 512:1024], unit(("vt", bb, blk, 1))[0:n, :])
                        for g in range(4):
                            x = 4 * (bb % 2) + g
                            b = unit(("sc", bb, g))
                            act.wait_ge(S["d_max"], 4 * bb + g + 1)
                            if bb >= 2:
                                act.wait_ge(dve_bank_full, UV.at[("ptr", bb - 2, g)] + 1)
                            fn(RDa["p"][:, x, :], b[:, 0:289], ACT.Exp, bias=small[:, 16 + x:17 + x], scale=HD1 ** -0.5,
                               accum_out=small[:, 24 + x:25 + x]).then_inc(act_bank_free, 1)
                    if pr + 1 < B // 2:
                        memory(pr + 1)
                    for bb in (2 * pr, 2 * pr + 1):
                        b = unit(("pvd", bb))[:, :].rearrange("p (o c) -> p o c", o=8)
                        tk = slice(32 * (bb % CB), 32 * (bb % CB) + 32)
                        fn(Q1[0:64, :, tk], b[0:64, :, 0:32], ACT.Copy)
                        copy_out(Q1[64:128, :, tk], b[64:128, :, 32:64])
                if cc + 1 < NCH:
                    act.wait_ge(dve_bank_full, UV.at[("dw", cc, 3)] + 1)
            end_stage()

            layernorm(4)
            step(fn(small[:, 32:33], col("L1_attn_A"), ACT.Abs))
            step(fn(small[:, 33:34], small[:, 32:33], ACT.Exp, scale=-1.0))
            fn(small[:, 34:35], small[:, 33:34], ACT.Ln, bias=tab("one")).then_inc(S["e_a"], 1)
            for c in range(C2):
                b = unit(("dl", c))
                fn(RE["z"][:, 0, ch(c)], b[:, :], ACT.Identity, bias=col("L1_attn_bdelta")).then_inc(act_bank_free, 1)
            act.wait_ge(act_bank_free, UA.at[("dl", C2 - 1)] + 1)
            log1pexp(RE["z"][:, 0, :], RE["t"][:, 0, :], S["e_sp"])
            act.wait_ge(S["e_cum"], 2)
            fn(RE["sh"], RE["sh"], ACT.Exp, scale=-1.0)
            fn(RE["z"][:, 0, :], RE["z"][:, 1, :], ACT.Exp).then_inc(S["e_exp"], 1)
            end_stage()

            layernorm(5)
            for c in range(C2):
                fn(Yh[:, :, ch(c)], y5[:, :, ch(c)], ACT.Copy).then_inc(S["f_yhi"], 1)

            def mags(n):
                name = MAGS[n]
                i = raw_no[name]
                act.wait_ge(raw_full[i % 2], 16 * (i // 2 + 1))
                if n == 1:
                    act.wait_ge(S["f_ylo"], C2)
                    act.wait_ge(act_bank_full, UA.at[("z", C2 - 1)] + 1)
                if n >= 3:
                    before = MAGS[n - 3]
                    if before[0] == "ff":
                        act.wait_ge(dve_bank_full, UV.at[("fs", before[1])] + 1)
                    elif before[1] == NQ - 1:
                        act.wait_ge(dve_bank_full, UV.at["fps"] + 1)
                    else:
                        act.wait_ge(S["f_used"], before[1] + 1)
                fn(aw[n % 3], raw[i % 2], ACT.Abs).then_inc(S["f_abs"], 1)

            mags(0)
            for c in range(C2):
                copy_out(RF["z"][0:16, 0, ch(c)], unit(("z", c))[0:16, :])
            for c in range(C2):
                fn(RF["z2"][0:16, 0, ch(c)], unit(("z2", c))[0:16, :], ACT.Copy, scale=col("gate", 0, 16)
                   ).then_inc(act_bank_free, 1)

            def f_up(j, c):
                if j:
                    act.wait_ge(dve_bank_full, UV.at[("fp", j - 1, c, 3)] + 1)
                for o in range(4):
                    n = 8 * j + 4 * c + o
                    b = unit(("ff", j, c, o))
                    if n >= 2:
                        act.wait_ge(S["f_lo"], n - 1)
                    fn(RF["r"][:, n % 2, :], b[:, :], ACT.Relu, scale=small[:, 40 + 4 * (j % 2) + o:41 + 4 * (j % 2) + o]
                       ).then_inc(act_bank_free, 1)
                    act.wait_ge(act_bank_free, UA.at[("ff", j, c, o)] + 1)
                    fn(Hh[:, o, ch(c)], RF["r"][:, n % 2, :], ACT.Square).then_inc(S["f_hi"], 1)

            for j in range(NQ):
                f_up(j, 0)
                if j == 0:
                    for n in range(1, 5):
                        mags(n)
                if j + 1 < NQ:
                    mags(5 + j)
                f_up(j, 1)
            end_stage()

        @block.vector
        def _(dve):
            end_stage, step = common(dve, dve_step)
            v = nc.vector

            def unit(key):
                u = UV.at[key]
                dve.wait_ge(dve_bank_full, u + 1)
                return UV.banks[u % 4]

            def on_act(key):
                dve.wait_ge(act_bank_free, UA.at[key] + 1)

            def stored(key):
                dve.wait_ge(dve_bank_free, UV.at[key] + 1)

            def layernorm(l):
                spec = LNS[l]
                for c in range(C2):
                    b = unit(("mean", l, c))
                    v.tensor_tensor(spec["dst"][:, :, ch(c)], spec["src"][:, :, ch(c)],
                                    b[:, :].unsqueeze(1).to_broadcast([128, 4, 512]), ALU.subtract).then_inc(dve_bank_free, 1)
                for c in range(C2):
                    on_act(("var", l, c))
                    x = spec["dst"][:, :, ch(c)]
                    if spec["plain"] is not None:
                        step(v.reciprocal(RL["r1"][:, c, :], RL["r1"][:, c, :]))
                        v.tensor_tensor(spec["plain"][:, :, ch(c)], x,
                                        RL["r1"][:, c, :].unsqueeze(1).to_broadcast([128, 4, 512]), ALU.mult)
                    step(v.reciprocal(RL["r2"][:, c, :], RL["r2"][:, c, :]))
                    v.tensor_tensor(x, x, RL["r2"][:, c, :].unsqueeze(1).to_broadcast([128, 4, 512]), ALU.mult
                                    ).then_inc(ln_out, 1)
                end_stage()

            def add_to_stream(key, o, c, bias=None):
                b = unit(key)
                x = XT[:, o, ch(c)]
                if bias is None:
                    v.tensor_tensor(x, b[:, :], x, ALU.add).then_inc(dve_bank_free, 1)
                else:
                    v.scalar_tensor_tensor(x, b[:, :], bias, x, ALU.add, ALU.add).then_inc(dve_bank_free, 1)

            dve.wait_ge(in_consts, 32)
            v.tensor_copy(ident_r[:, :], tab("ident"))
            v.tensor_copy(causal_r[:, :], tab("causal"))
            dve.wait_ge(in_xtm, 16)
            for t in range(TT):
                last = v.bn_stats(RA["st"][:, t, :], xtm[:, t, :])
            step(last)
            for t in range(TT):
                last = v.bn_aggr(RA["mv"][:, t, :], RA["st"][:, t, :])
            last.then_inc(a_var, 1)
            dve.wait_ge(a_std, 1)
            step(v.reciprocal(small[:, 0:8], small[:, 0:8]))
            for t in range(TT):
                v.tensor_scalar(xtm[:, t, :], xtm[:, t, :], RA["mv"][:, t, 0:1], small[:, t:t + 1], ALU.subtract, ALU.mult
                                ).then_inc(xn_tile, 1)
            for t in range(TT):
                b = unit(("ldq", t))
                v.tensor_copy(LQ[:, :, tl(t)], b[:, :].rearrange("p (k n) -> p k n", k=4)).then_inc(dve_bank_free, 1)
            for t in range(TT):
                on_act(("qf", t))
                b = unit(("kf", t))
                v.tensor_tensor_reduce(out=RA["qs"][:, t % 2, :], in0=RA["qs"][:, t % 2, :], in1=b[:, :], scale=1.0, scalar=0.0,
                                       op0=ALU.mult, op1=ALU.add, accum_out=RA["C"][:, 0, t:t + 1]).then_inc(dve_bank_free, 1)
            dve.wait_ge(dve_bank_free, UV.at[("kf", TT - 1)] + 1)
            dve.wait_ge(in_consts, 32)
            v.tensor_tensor(RA["cx"], RA["C"][:, 0, :].unsqueeze(2).to_broadcast([128, 8, 4]),
                            tab("own_batch").unsqueeze(1).to_broadcast([128, 8, 4]), ALU.mult).then_inc(cx_ready, 1)
            b = unit("corr")
            cr, v8, i8, e8, fi8 = (RA[n][0:32, 0, :] for n in ("cr", "v8", "i8", "e8", "fi8"))
            v.tensor_copy(cr, b[0:32, 0:32]).then_inc(dve_bank_free, 1)
            dve.wait_ge(dve_bank_free, UV.at["corr"] + 1)
            step(v.max(v8, cr))
            step(v.max_index(i8.bitcast(u32), v8, cr))
            v.tensor_copy(fi8, i8.bitcast(u32))
            v.tensor_scalar(small[0:32, 8:9], v8[:, 0:1], -1.0, None, ALU.mult).then_inc(top_ready, 1)
            dve.wait_ge(topexp_ready, 1)
            step(v.reciprocal(small[0:32, 9:10], small[0:32, 9:10]))
            step(v.tensor_scalar(e8[:, 0:TOPK], e8[:, 0:TOPK], small[0:32, 9:10], None, ALU.mult))
            eq = RA["eq"][0:32, :, :]
            step(v.tensor_tensor(eq, tab("iota", 32)[:, 0:32].unsqueeze(1).to_broadcast([32, TOPK, 32]),
                                 fi8[:, 0:TOPK].unsqueeze(2).to_broadcast([32, TOPK, 32]), ALU.is_equal))
            step(v.tensor_tensor(eq, eq, e8[:, 0:TOPK].unsqueeze(2).to_broadcast([32, TOPK, 32]), ALU.mult))
            step(v.tensor_reduce(RA["w2"][0:32, 0, :], eq.rearrange("p k t -> p t k"), AX.X, ALU.add))
            v.tensor_copy(RA["w2"][0:32, 1, :], RA["w2"][0:32, 0, :]).then_inc(w_ready, 1)
            dve.wait_ge(m_loaded, 64)
            v.transpose(RA["mt"].rearrange("p a b -> p (a b)"), RA["m"].rearrange("p a b -> p (a b)")).then_inc(mt_ready, 1)
            dve.wait_ge(in_xT, 16)
            for o in range(4):
                for c in range(C2):
                    add_to_stream(("ao", o, c), o, c, col("L0_xattn_bo", o))
            end_stage()

            layernorm(0)
            reset = RB["reset"]
            step(v.memset(reset, 1.0))
            step(v.memset(reset[:, 0, :].rearrange("p (b l) -> p b l", l=L)[:, :, 0:1], 0.0))
            dve.wait_ge(S["b_ckln"], 1)
            for c in range(C2):
                v.scalar_tensor_tensor(RB["ck"][0:16, 0, ch(c)], RB["ck"][0:16, 0, ch(c)], 0.0, RB["t"][0:16, 0, ch(c)],
                                       ALU.max, ALU.add).then_inc(S["b_clock"], 1)
            pcs, q, k = H[:, 1, 2, :], H[:, 0, 0, :], H[:, 0, 1, :]
            t0, t1 = RB["t"][:, 0, :], RB["t"][:, 1, :]
            byb = dict(l=L)

            def normalise(o):
                for t in range(TT):
                    b = unit(("pv", o, t))
                    if t or o:
                        stored(("pv", o, t - 1) if t else ("pv", o - 1, TT - 1))
                    step(v.reciprocal(RB["den"][:, 0, :], b[:, 128:256]))
                    v.tensor_tensor(RB["ot"][:, o, tl(t)], b[:, 0:128], RB["den"][:, 0, :], ALU.mult
                                    ).then_inc(dve_bank_free, 1)

            for o in range(4):
                g, p = gate_buf[o % 2], p_buf[o % 2]
                dve.wait_ge(S["b_gsp"], o + 1)
                step(v.scalar_tensor_tensor(t0, g, 0.0, t0, ALU.max, ALU.add))
                step(v.tensor_tensor_scan(t1, reset[:, 0, :], t0, 0.0, ALU.mult, ALU.subtract))
                v.tensor_scalar(t1, t1, -60.0, 50.0, ALU.max, ALU.min).then_inc(S["b_gcs"], 1)
                on_act(("bp", o, C2 - 1))
                pv3 = p.rearrange("p (b l) -> p b l", **byb)
                step(v.tensor_reduce(RB["pm"][:, 0, :], pv3, AX.X, ALU.max))
                v.tensor_tensor(pv3, pv3, RB["pm"][:, 0, :].unsqueeze(2).to_broadcast([128, B, L]), ALU.subtract
                                ).then_inc(S["b_pdif"], 1)
                dve.wait_ge(S["b_pexp"], o + 1)
                for c in range(C2):
                    b = unit(("ck", o, c))
                    v.tensor_tensor(p[:, ch(c)], b[:, :], p[:, ch(c)], ALU.mult).then_inc(dve_bank_free, 1)
                dve.wait_ge(dve_bank_free, UV.at[("ck", o, C2 - 1)] + 1)
                v.tensor_tensor_scan(pcs, reset[:, 0, :], p, 0.0, ALU.mult, ALU.add)
                for w, t_ in (("bq", t0), ("bk", t1)):
                    for c in range(C2):
                        b = unit(("r" + w, o, c))
                        v.tensor_tensor(t_[:, ch(c)].rearrange("p (b l) -> p b l", **byb),
                                        b[:, :].rearrange("p (b l) -> p b l", **byb),
                                        tab("sin").unsqueeze(1).to_broadcast([128, 16, L]), ALU.mult).then_inc(dve_bank_free, 1)
                on_act(("nbk", o, C2 - 1))
                nrm = H[:, 0, 2:4, :]
                step(v.tensor_scalar(nrm, nrm, 1e-12, None, ALU.max))
                v.scalar_tensor_tensor(H[:, 0, 3, :], g, 1e-8, H[:, 0, 3, :], ALU.add, ALU.mult)
                step(v.scalar_tensor_tensor(H[:, 0, 2, :], pcs, 1e-8, H[:, 0, 2, :], ALU.add, ALU.mult))
                if o:
                    normalise(o - 1)
                step(v.reciprocal(nrm, nrm))
                v.tensor_tensor(pcs, g, H[:, 0, 2, :], ALU.mult)
                v.tensor_tensor(p, p, H[:, 0, 3, :], ALU.mult)
                dve.wait_ge(S["b_cos"], 2 * (o + 1))
                v.tensor_tensor(q, q, t0, ALU.add)
                step(v.tensor_tensor(k, k, t1, ALU.add))
                v.tensor_tensor(q, q, pcs, ALU.mult).then_inc(S["b_qk"], 1)
                v.tensor_tensor(k, k, p, ALU.mult).then_inc(S["b_qk"], 1)
            normalise(3)
            for o in range(4):
                for c in range(C2):
                    b = unit(("bo", o, c))
                    v.scalar_tensor_tensor(Y[:, o, ch(c)], b[:, :], col("L0_attn_out_b", o), Y[:, o, ch(c)], ALU.add, ALU.add
                                           ).then_inc(dve_bank_free, 1)
            end_stage()
            layernorm(1)
            step(v.tensor_tensor(XT[:, :, :], XT[:, :, :], Y[:, :, :], ALU.add))

            def down(name, bias, j):
                for o in range(4):
                    for c in range(C2):
                        add_to_stream((name, j, o, c), o, c, col(bias, o) if j == 0 else None)

            for j in range(NQ):
                down("b2", "L0_attn_mlp_b2", j)
            end_stage()

            layernorm(2)

            def route(t):
                i = t % 2
                tf, na = RT["tf"][:, i], RT["na"][:, i]
                on_act(("sim", TT - 1))
                for n in range(8):
                    sim = RC["sim"][:, t, 64 * n:64 * n + 64]
                    last = v.max(RT["tv"][:, n, :], sim)
                step(last)
                for n in range(8):
                    sim = RC["sim"][:, t, 64 * n:64 * n + 64]
                    last = v.max_index(RT["ti"][:, n, :].bitcast(u32), RT["tv"][:, n, :], sim)
                step(last)
                if t >= 2:
                    dve.wait_ge(S["c_dense"], t - 1)
                v.tensor_copy(tf, RT["ti"].bitcast(u32))
                for h in range(PH):
                    last = v.tensor_tensor(RT["cand"][:, h, :].rearrange("p (a b) -> p a b", a=8),
                                           RT["tv"][:, h, :].unsqueeze(2).to_broadcast([128, 8, 8]),
                                           RT["tv"][:, 4 + h, :].unsqueeze(1).to_broadcast([128, 8, 8]), ALU.add)
                step(last)
                for h in range(PH):
                    last = v.max(RT["t8"][:, h, :], RT["cand"][:, h, :])
                step(last)
                for h in range(PH):
                    last = v.match_replace(RT["rep"][:, h, :], RT["t8"][:, h, :], RT["cand"][:, h, :], -3e38)
                step(last)
                sel = RT["sel"]
                step(v.tensor_tensor(sel, RT["rep"], RT["cand"], ALU.not_equal))
                v.tensor_tensor(RT["rep"], RT["cand"], RT["t8"][:, :, 0:1].to_broadcast([128, PH, 64]), ALU.subtract)
                v.tensor_tensor(RT["sd"], RC["sim"][:, t, :].rearrange("p (n k) -> p n k", n=8),
                                RT["tv"][:, :, 0:1].to_broadcast([128, 8, 64]), ALU.subtract).then_inc(S["c_topin"], 1)
                v.tensor_reduce(na.rearrange("p h a -> p (h a)"), sel.rearrange("p h (a b) -> p (h a) b", a=8), AX.X, ALU.add)
                step(v.tensor_scalar(RT["ge"], tf[:, 0:4, :], 32.0, None, ALU.is_ge))
                dve.wait_ge(S["c_topexp"], t + 1)
                step(v.tensor_tensor(RT["rep"], RT["rep"], sel, ALU.mult))
                step(v.tensor_reduce(RT["rs"].rearrange("p h a -> p (h a)"), RT["rep"].rearrange("p h (a b) -> p (h a) b", a=8),
                                     AX.X, ALU.add))
                step(v.tensor_reduce(RT["z"][:, 0, :], RT["rs"], AX.X, ALU.add))
                step(v.reciprocal(RT["rz"][:, 0, :], RT["z"][:, 0, :]))
                rz = RT["rz"][:, 0, :].unsqueeze(2)
                step(v.tensor_tensor(RT["rs"], RT["rs"], RT["ge"], ALU.mult))
                step(v.tensor_tensor(RT["rs"], RT["rs"], rz.to_broadcast([128, PH, 8]), ALU.mult))
                v.tensor_reduce(RC["xv"][:, 0, t:t + 1], RT["rs"].rearrange("p h a -> p (h a)"), AX.X, ALU.add)
                v.tensor_copy(RC["Ey"][:, t], RT["sd"][:, 4:8, :])
                v.tensor_tensor(RC["Ex"][:, t], RT["sd"][:, 0:4, 0:32], rz.to_broadcast([128, PH, 32]), ALU.mult
                                ).then_inc(S["c_fac"], 1)

            def c_up(j):
                for o in range(4):
                    for c in range(C2):
                        u = 8 * j + 2 * o + c
                        on_act(("cg", j, o, c))
                        b = unit(("cu", j, o, c))
                        v.scalar_tensor_tensor(H[:, j % 2, o, ch(c)], b[:, :], col("L0_ffn_bu", 4 * j + o), RC["s"][:, u % 4, :],
                                               ALU.add, ALU.mult).then_inc(dve_bank_free, 1)
                    if o % 2 == 0:
                        route(2 * j + o // 2)

            quarters(c_up, lambda j: down("cd", "L0_ffn_bd", j))
            tmp = RC["eq"][:, 0, :].rearrange("p (h x y) -> p h x y", h=PH, x=8)
            dve.wait_ge(S["c_dense"], TT)

            def spread(j, t):
                n = TT * j + t
                xs = slice(8 * j, 8 * j + 8)
                if n:
                    dve.wait_ge(S["c_p"], n)
                for h in range(PH):
                    T = RC["Tx"][:, t, h, xs].unsqueeze(2).to_broadcast([128, 8, 64])
                    Ry = RC["Ry"][:, t, h, :].unsqueeze(1).to_broadcast([128, 8, 64])
                    last = v.tensor_tensor(tmp[:, h], T, Ry, ALU.is_gt)
                step(last)
                flat = RC["eq"][:, 0, :]
                dve.wait_ge(S["c_ee"], n + 1)
                last = v.tensor_tensor(flat, flat, EE[:, n % 2, :], ALU.mult)
                last.then_inc(S["c_mul"], 1)
                dve.wait_ge(S["c_mul"], n + 1)
                step(v.tensor_tensor(flat[:, 0:1024], flat[:, 0:1024], flat[:, 1024:2048], ALU.add))
                pj = RC["pj"][:, t % 2, :]
                if n >= 2:
                    dve.wait_ge(dve_bank_full, UV.at[("pt", (n - 2) // TT, (n - 2) % TT)] + 1)
                last = v.tensor_tensor(pj, flat[:, 0:512], flat[:, 512:1024], ALU.add)
                if j == NQ - 1:
                    step(last)
                    last = v.tensor_tensor(pj[:, 511:512], pj[:, 511:512], RC["xv"][:, 0, t:t + 1], ALU.add)
                last.then_inc(S["c_p"], 1)

            def weigh(j, t):
                on_act(("ce", j, 3 if t < 4 else 7))
                b = unit(("pt", j, t))
                x = SJ[j % 3][:, :, tl(t)]
                v.tensor_tensor(x, b[:, :].rearrange("p (e n) -> p e n", e=4), x, ALU.mult).then_inc(dve_bank_free, 1)

            for n in range(TT * (NQ + 1) + 1):
                if n < TT * NQ:
                    spread(n // TT, n % TT)
                if 1 <= n <= TT * NQ:
                    weigh((n - 1) // TT, (n - 1) % TT)
                if n > TT:
                    t = (n - 1) % TT
                    add_to_stream(("cf", (n - 1) // TT - 1, t), t % 4, t // 4)
            end_stage()

            layernorm(3)
            dve.wait_ge(act_bank_full, UA.at["m256"] + 1)
            for h in range(2):
                dve.wait_ge(S["d_whi"], h + 1)
                w = W(("dm", h))
                v.tensor_tensor(wml[:, h], w, wmh[:, h].bitcast(f32), ALU.subtract).then_inc(S["d_wlo"], 1)

            def split_low(pr):
                dve.wait_ge(S["d_chi"], pr + 1)
                v.tensor_tensor(ctl[:, :, :, :], ct, cth[:, :, :, :].bitcast(f32), ALU.subtract).then_inc(S["d_clo"], 1)

            split_low(0)
            split_low(1)
            for cc in range(NCH):
                for pr in range(CB // 2 * cc, CB // 2 * (cc + 1)):
                    for bb in (2 * pr, 2 * pr + 1):
                        if bb >= 2:
                            dve.wait_ge(act_bank_full, UA.at[("pvd", bb - 2)] + 1)
                        for blk, n in ((0, 128), (1, 128), (2, 33)):
                            b = unit(("vt", bb, blk, 0))
                            v.tensor_copy(RD["vt"][0:n, bb % 2, blk, 0:512], b[0:n, :]).then_inc(dve_bank_free, 1)
                        for g_ in range(4):
                            x = 16 + 4 * (bb % 2) + g_
                            u = UA.at[("sc", bb, g_)]
                            dve.wait_ge(act_bank_full, u + 1)
                            step(v.reduce_max(small[:, x:x + 1], UA.banks[u % 4][:, 0:289], AX.X))
                            v.tensor_scalar(small[:, x:x + 1], small[:, x:x + 1], -HD1 ** -0.5, None, ALU.mult
                                            ).then_inc(S["d_max"], 1)
                    for bb in (2 * pr, 2 * pr + 1):
                        for g_ in range(4):
                            x = 4 * (bb % 2) + g_
                            on_act(("sc", bb, g_))
                            step(v.reciprocal(small[:, 24 + x:25 + x], small[:, 24 + x:25 + x]))
                            v.tensor_scalar(RDa["p"][:, x, :], RDa["p"][:, x, :], small[:, 24 + x:25 + x], None, ALU.mult
                                            ).then_inc(S["d_probn"], 1)
                    for bb in (2 * pr, 2 * pr + 1):
                        for g_ in range(4):
                            b = unit(("ptr", bb, g_))
                            v.tensor_copy(RDa["pt"][:, g_, 0:256], b[:, 0:256])
                            v.tensor_copy(RDa["pt"][0:33, g_, 256:384], b[0:33, 256:384]).then_inc(dve_bank_free, 1)
                    if pr + 2 < B // 2:
                        split_low(pr + 2)
                for o in range(4):
                    x = XT[:, o, cs(cc)]
                    v.scalar_tensor_tensor(x, unit(("dw", cc, o))[:, 0:CT], col("L1_xattn_bo", o), x, ALU.add, ALU.add
                                           ).then_inc(dve_bank_free, 1)
            end_stage()

            layernorm(4)
            reset = RE["reset"]
            step(v.memset(reset, 1.0))
            step(v.memset(reset[:, 0, :].rearrange("p (b l) -> p b l", l=L)[:, :, 0:1], 0.0))
            dve.wait_ge(S["e_a"], 1)
            step(v.scalar_tensor_tensor(small[:, 35:36], col("L1_attn_A"), 0.0, small[:, 34:35], ALU.max, ALU.add))
            step(v.tensor_scalar(small[:, 35:36], small[:, 35:36], -1.0, None, ALU.mult))
            step(v.tensor_tensor(small[:, 36:40], cols[:, COLUMN_AT["L1_attn_bc"]:COLUMN_AT["L1_attn_bc"] + 4],
                                 cols[:, COLUMN_AT["L1_attn_bd"]:COLUMN_AT["L1_attn_bd"] + 4], ALU.add))
            dve.wait_ge(S["e_sp"], 1)
            dl, bbar, cum, tt = RE["dl"][:, 0, :], RE["bb"][:, 0, :], RE["z"][:, 1, :], RE["t"][:, 1, :]
            step(v.scalar_tensor_tensor(dl, RE["z"][:, 0, :], 0.0, RE["t"][:, 0, :], ALU.max, ALU.add))
            for c in range(C2):
                b = unit(("bb", c))
                v.scalar_tensor_tensor(bbar[:, ch(c)], b[:, :], col("L1_attn_bb"), dl[:, ch(c)], ALU.add, ALU.mult
                                       ).then_inc(dve_bank_free, 1)
            step(v.tensor_scalar(tt, dl, small[:, 35:36], None, ALU.mult))
            step(v.tensor_tensor_scan(cum, reset[:, 0, :], tt, 0.0, ALU.mult, ALU.add))
            v.tensor_scalar(cum, cum, -20.0, 20.0, ALU.max, ALU.min).then_inc(S["e_cum"], 1)
            dve.wait_ge(S["e_cum"], 1)
            v.memset(RE["sh"][:, :, 0:1], 0.0)
            v.tensor_copy(RE["sh"][:, :, 1:L], cum.rearrange("p (b l) -> p b l", l=L)[:, :, 0:L - 1]).then_inc(S["e_cum"], 1)
            dve.wait_ge(S["e_exp"], 1)
            dve.wait_ge(dve_bank_free, UV.at[("bb", C2 - 1)] + 1)
            step(v.tensor_tensor(bbar, bbar, RE["sh"].rearrange("p b l -> p (b l)"), ALU.mult))
            step(v.tensor_tensor_scan(tt, reset[:, 0, :], bbar, 0.0, ALU.mult, ALU.add))
            v.tensor_tensor(RE["hh"][:, 0, :], tt, RE["z"][:, 0, :], ALU.mult).then_inc(S["e_hh"], 1)
            for o in range(4):
                for c in range(C2):
                    add_to_stream(("ed", o, c), o, c, small[:, 36 + o:37 + o])
            end_stage()

            layernorm(5)

            for c in range(C2):
                dve.wait_ge(S["f_yhi"], c + 1)
                v.tensor_tensor(Yl[:, :, ch(c)], y5[:, :, ch(c)], Yh[:, :, ch(c)].bitcast(f32), ALU.subtract
                                ).then_inc(S["f_ylo"], 1)

            def ternary(name, dst, scale, done):
                i = raw_no[name]
                dve.wait_ge(raw_full[i % 2], 16 * (i // 2 + 1))
                if name[0] == "ff":
                    dve.wait_ge(S["f_abs"], MAGS.index(name) + 1)
                w = raw[i % 2]
                half = RF["half"][:, 0, :].unsqueeze(1).to_broadcast([128, 4, 512])
                step(v.tensor_scalar(RF["half"][:, 0, :], scale, 0.5, None, ALU.mult))
                step(v.tensor_tensor(dst, w, half, ALU.is_gt))
                step(v.scalar_tensor_tensor(w, w, -1.0, half, ALU.mult, ALU.is_gt))
                v.tensor_tensor(dst, dst.bitcast(f32), w, ALU.subtract).then_inc(done, 1)

            def scale_of(key, dst, cols_at):
                b = unit(key)
                v.tensor_scalar(dst, b[:, :], 1e-5, None, ALU.max).then_inc(dve_bank_free, 1)
                stored(key)
                for o in range(4):
                    step(v.tensor_tensor_reduce(out=RF["diag"][:, 0, :], in0=dst[:, tl(o)], in1=tab("ident"), scale=1.0,
                                                scalar=0.0, op0=ALU.mult, op1=ALU.add,
                                                accum_out=small[:, cols_at + o:cols_at + o + 1]))

            sp_, sf_, ru = RF["sp"][:, 0, :], RF["s"][:, 0, :], RF["ru"][0:16, 0, :]

            def up_weights(j):
                scale_of(("fs", j), sf_, 40 + 4 * (j % 2))
                step(v.reciprocal(ru, sf_[0:16, :]))
                u_ = RF["uT"][0:16, 0, 512 * j:512 * j + 512]
                if j == 0:
                    dve.wait_ge(in_small, 112)
                step(v.tensor_tensor(u_, u_, ru, ALU.mult))
                ternary(("ff", j), tern_up[:, j % 2], sf_, S["f_wf"])
                dve.wait_ge(S["f_wf"], j + 1)

            def f_low(j, c):
                for o in range(4):
                    n = 8 * j + 4 * c + o
                    dve.wait_ge(S["f_q"], n + 1)
                    v.tensor_tensor(Hl[:, o, ch(c)], RF["r"][:, n % 2, :], Hh[:, o, ch(c)].bitcast(f32), ALU.subtract
                                    ).then_inc(S["f_lo"], 1)

            def f_add(j, c):
                for o in range(4):
                    x = XT[:, o, ch(c)]
                    v.scalar_tensor_tensor(x, unit(("fp", j, c, o))[:, :], small[:, 48 + o:49 + o], x, ALU.mult, ALU.add
                                           ).then_inc(dve_bank_free, 1)

            up_weights(0)
            for j in range(NQ):
                f_low(j, 0)
                if j == 0:
                    scale_of("fps", sp_, 48)
                if j + 1 < NQ:
                    up_weights(j + 1)
                f_low(j, 1)
                if j == 0:
                    ternary(("fp", 0), tern_down[:, 0:4, :], sp_, S["f_wp"])
                    dve.wait_ge(S["f_wp"], 1)
                f_add(j, 0)
                if j + 1 < NQ:
                    ternary(("fp", j + 1), tern_down[:, 4 * j + 4:4 * j + 8, :], sp_, S["f_wp"])
                    dve.wait_ge(S["f_wp"], j + 2)
                f_add(j, 1)
            end_stage()

        @block.gpsimd
        def _(pool):
            end_stage, step = common(pool, pool_step)
            g = nc.gpsimd

            g.memset(RA["m"], 0.0).then_inc(m_zero, 1)
            pool.wait_ge(in_consts, 32)
            end_stage()
            end_stage()
            for o in range(4):
                for i, w in enumerate(("bq", "bk")):
                    pool.wait_ge(act_bank_free, UA.at[(w, o, C2 - 1)] + 1)
                    pool.wait_ge(dve_bank_full, UV.at[("r" + w, o, C2 - 1)] + 1)
                    x3 = H[:, 0, i, :].rearrange("p (b l) -> p b l", l=L)
                    g.tensor_tensor(x3, x3, tab("cos").unsqueeze(1).to_broadcast([128, B, L]), ALU.mult).then_inc(S["b_cos"], 1)
            for _i in range(4):
                end_stage()
            eqf = RC["eq"][:, 0, :]
            for t in range(TT):
                i = t % 2
                tf, na = RT["tf"][:, i], RT["na"][:, i]
                pool.wait_ge(S["c_fac"], t + 1)
                for ax in range(2):
                    if ax == 0:
                        n, w, dst = 32, na, RC["Tx"][:, t]
                    else:
                        n, w, dst = 64, None, RC["Ry"][:, t]
                    e4 = eqf[:, 0:32 * n].rearrange("p (a h x) -> p a h x", a=8, h=PH)
                    for h in range(PH):
                        key = tf[:, 4 * ax + h, :].unsqueeze(2).to_broadcast([128, 8, n])
                        last = g.tensor_tensor(e4[:, :, h, :], tab("iota")[:, 0:n].unsqueeze(1).to_broadcast([128, 8, n]), key,
                                               ALU.subtract)
                    step(last)
                    step(g.tensor_scalar(eqf[:, 0:32 * n], eqf[:, 0:32 * n], 0.0, None, ALU.is_equal))
                    for h in range(PH):
                        wt = (na[:, h, :] if ax == 0 else tab("rank")).unsqueeze(2).to_broadcast([128, 8, n])
                        last = g.tensor_tensor(e4[:, :, h, :], e4[:, :, h, :], wt, ALU.mult)
                    step(last)
                    m = 4 * n
                    step(g.tensor_tensor(eqf[:, 0:4 * m], eqf[:, 0:4 * m], eqf[:, 4 * m:8 * m], ALU.add))
                    step(g.tensor_tensor(eqf[:, 0:2 * m], eqf[:, 0:2 * m], eqf[:, 2 * m:4 * m], ALU.add))
                    d2 = dst.rearrange("p h x -> p (h x)")
                    last = g.tensor_tensor(d2, eqf[:, 0:m], eqf[:, m:2 * m], ALU.add)
                    step(last)
                g.tensor_scalar(RC["Ry"][:, t], RC["Ry"][:, t], -1.0, 8.0, ALU.mult, ALU.add).then_inc(S["c_dense"], 1)
            pool.wait_ge(S["c_fac"], TT)
            for n in range(TT * NQ):
                j, t = n // TT, n % TT
                if n >= 2:
                    pool.wait_ge(S["c_mul"], n - 1)
                for h in range(PH):
                    Ex = RC["Ex"][:, t, h, 8 * j:8 * j + 8].unsqueeze(2).to_broadcast([128, 8, 64])
                    Ey = RC["Ey"][:, t, h, :].unsqueeze(1).to_broadcast([128, 8, 64])
                    last = g.tensor_tensor(EE[:, n % 2, 512 * h:512 * h + 512].rearrange("p (x y) -> p x y", x=8), Ex, Ey, ALU.mult)
                last.then_inc(S["c_ee"], 1)
            end_stage()
            end_stage()

            step(g.memset(RD["qbd"], 0.0))
            for bb in range(B):
                pr, i, cc, lb = bb // 2, bb % 2, bb // CB, bb % CB
                if lb == 0:
                    pool.wait_ge(act_bank_free, UA.at[("dv", cc, OT1 - 1)] + 1)
                if i == 0 and pr:
                    pool.wait_ge(act_bank_full, UA.at[("sc", 2 * pr - 1, 3)] + 1)
                if bb:
                    pool.wait_ge(S["d_qbd"], bb)
                tk = slice(32 * lb, 32 * lb + 32)
                for at_ in (256, 289):
                    g.tensor_copy(kt[:, :, i, at_:at_ + 1], RD["m256"][:, :, bb:bb + 1])
                g.tensor_copy(kt[:, :, i, 257:289], K1[:, :, tk])
                g.tensor_copy(kt[:, :, i, 290:322], V1[:, :, tk]).then_inc(S["d_self"], 1)
                if bb >= 2:
                    pool.wait_ge(act_bank_full, UA.at[("sc", bb - 2, 3)] + 1)
                pool.wait_ge(S["d_self"], bb + 1)
                step(g.tensor_copy(qbd[i][0:64, :, 0:32], Q1[0:64, :, tk]))
                g.tensor_copy(qbd[i][64:128, :, 32:64], Q1[64:128, :, tk]).then_inc(S["d_qbd"], 1)
            end_stage()
            for _i in range(3):
                end_stage()
            for n in range(8 * NQ):
                pool.wait_ge(S["f_hi"], n + 1)
                g.tensor_tensor(RF["r"][:, n % 2, :], RF["r"][:, n % 2, :], RF["r"][:, n % 2, :], ALU.mult).then_inc(S["f_q"], 1)
            end_stage()

        @block.sync
        def _(sp):
            slot_last = {}

            def load(i):
                name, s_, src = loads[i]
                if s_ in slot_last:
                    sem_, val = released[slot_last[s_]]
                    sp.wait_ge(sem_, val)
                dst = arena[:, s_, :, :]
                if src.shape[2] != 512:
                    dst = dst[:, :, 0:src.shape[2]]
                sp.dma_start(dst, src).then_inc(slot_full[s_], 16)
                slot_last[s_] = name

            sp.dma_start(xtm, dram["x_tokens"].rearrange("(t p) d -> p t d", p=128)).then_inc(in_xtm, 16)
            sp.dma_start(consts[:, :], dram["tables"]).then_inc(in_consts, 16)
            sp.dma_start(cols[:, :], dram["columns"]).then_inc(in_consts, 16)
            c32 = dram["ctx"].rearrange("(t b) m d -> b m t d", b=4)
            for b4 in range(4):
                sp.dma_start(ctm[32 * b4:32 * b4 + 32, :, :], c32[b4, 0:32, :, :]).then_inc(in_ctx32, 16)
            sp.dma_start(RA["bq"][0:1, 0, :], dram["L0_xattn_bq"]).then_inc(in_small, 16)
            sp.dma_start(RA["bk"][0:1, 0, :], dram["L0_xattn_bk"]).then_inc(in_small, 16)
            load(0)
            load(1)
            sp.dma_start(XT[:, :, :], dram["xT"].rearrange("(k p) n -> p k n", p=128)).then_inc(in_xT, 16)
            for i in range(2, 6):
                load(i)
            sp.wait_ge(w_ready, 1)
            scratch = dram["scratch"]
            sp.dma_start(scratch.rearrange("b (r j) -> b r j", j=64),
                         RA["w2"][0:32].rearrange("p a b -> p (a b)").unsqueeze(1).to_broadcast([32, 32, 64])
                         ).then_inc(w_stored, 16)
            sp.wait_ge(w_stored, 16)
            sp.wait_ge(m_zero, 1)
            skew = scratch[:, 32:2048].rearrange("b (l s) -> b l s", s=63)[:, :, 0:32].rearrange("(t b) l m -> b l t m", b=4)
            for b4 in range(4):
                sp.dma_start(RA["m"][32 * b4:32 * b4 + 32, :, 32 * b4:32 * b4 + 32], skew[b4]).then_inc(m_loaded, 16)
            for i in range(6, 9):
                load(i)
            sp.wait_ge(stage_done, 8)
            sp.dma_start(RB["cw"], dram["L0_attn_clock_w"].rearrange("(k p) n -> p k n", p=128)).then_inc(in_small, 16)
            first_e = [i for i, l_ in enumerate(loads) if l_[0] == ("ce", 0)][0]
            first_c = [i for i, l_ in enumerate(loads) if l_[0] == "cq"][0]
            for i in range(9, first_c + 1):
                load(i)
            sp.wait_ge(stage_done, 4 * 6)
            sp.dma_start(RC["kb"], dram["key_blocks"]).then_inc(S["c_kb"], 16)
            for i in range(first_c + 1, D_FIRST):
                load(i)
            per = (E_FIRST - D_FIRST - 2) // NCH

            def load_ct(pr):
                if pr:
                    sp.wait_ge(S["d_clo"], pr)
                sp.dma_start(RD["ct"], dram["ctxT"].rearrange("(k p) n -> p k n", p=128)[:, :, 514 * pr:514 * pr + 514]
                             ).then_inc(S["d_ct"], 16)

            load(D_FIRST)
            load(D_FIRST + 1)
            sp.wait_ge(stage_done, 4 * 7)
            sp.dma_start(RD["c256"], dram["ctx_lastT"].rearrange("(k p) b -> p k b", p=128)).then_inc(S["d_ct256"], 16)
            load(D_FIRST + 2)
            load(D_FIRST + 3)
            load_ct(0)
            load_ct(1)
            for cc in range(NCH):
                lo = D_FIRST + 2 + per * cc
                for i in range(lo + (2 if cc == 0 else 0), lo + per):
                    load(i)
                for pr in range(CB // 2 * cc + 2, min(CB // 2 * (cc + 1) + 2, B // 2)):
                    load_ct(pr)
            load(E_FIRST)
            load(E_FIRST + 1)
            sp.wait_ge(stage_done, 4 * 10)
            sp.dma_start(RE["wc"][:, 0, :], dram["L1_attn_Wc"]).then_inc(in_small, 16)

            def load_raw(i):
                kind, j = last_loads[i]
                if i >= 2:
                    before = last_loads[i - 2]
                    if before[0] == "fa":
                        sp.wait_ge(S["f_abs"], MAGS.index(before) + 1)
                    else:
                        sp.wait_ge(S["f_wf" if before[0] == "ff" else "f_wp"], before[1] + 1)
                src = rows4("w_fcT", 0, 512 * j) if kind == "ff" else rows4("w_projT", 512 * j)
                sp.dma_start(raw[i % 2], src).then_inc(raw_full[i % 2], 16)

            load_raw(0)
            load_raw(1)
            sp.wait_ge(stage_done, 4 * 12)
            sp.dma_start(RF["vT"], dram["vT"].rearrange("(k p) n -> p k n", p=128)).then_inc(in_small, 16)
            sp.dma_start(RF["fb"][0:16, 0, :], dram["fast_bT"]).then_inc(in_small, 16)
            sp.dma_start(RF["uT"][0:16, 0, :], dram["uT"]).then_inc(in_small, 16)
            for i in range(2, len(last_loads)):
                load_raw(i)
            sp.wait_ge(stage_done, 4 * 13)
            sp.dma_start(out.rearrange("(k p) n -> p k n", p=128), XT[:, :, :]).then_inc(out_stored, 16)
            sp.wait_ge(out_stored, 16)


_PLAIN = ["L0_xattn_Wq", "L0_xattn_Wk", "L0_xattn_Wv", "L0_xattn_Wo", "L0_attn_Wq", "L0_attn_Wk", "L0_attn_Wv",
          "L0_attn_gate_w", "L0_attn_p_w", "L0_attn_out_w", "L0_attn_clock_w", "L0_attn_mlp_w1", "L0_attn_mlp_w2",
          "L0_ffn_Wg", "L0_ffn_Wu", "L0_ffn_Wd", "L0_ffn_Wq", "L0_ffn_up_embed", "L1_xattn_Wq", "L1_xattn_Wkv",
          "L1_xattn_Wm", "L1_xattn_Wo", "L1_attn_Wc", "L1_attn_Wd"]


def layouts(inputs):
    a = {k: np.ascontiguousarray(v) for k, v in inputs.items()}
    got = {k: a[k] for k in _PLAIN}
    x = a["x"].reshape(N, D)
    got["x_tokens"] = x
    got["xT"] = np.ascontiguousarray(x.T)
    got["ctx"] = a["ctx_1024"]
    got["ctxT"] = np.ascontiguousarray(a["ctx_1024"].reshape(B * M, D).T)
    got["ctx_lastT"] = np.ascontiguousarray(a["ctx_1024"][:, M - 1, :].T)
    got["tables"] = np.concatenate([TABLES[k] for k in TABLES], axis=1)
    columns = np.zeros((128, COLUMN_COLS), np.float32)
    for name, n in COLUMNS:
        at_ = COLUMN_AT[name]
        if name == "clock_b":
            columns[0:16, at_] = a["L0_attn_clock_b"]
        elif name == "gate":
            columns[:, at_] = np.broadcast_to(a["L1_ffn_gate"].reshape(1), (128,))
        else:
            columns[:, at_:at_ + n] = a[name].reshape(n, 128).T
    got["columns"] = columns
    got["L0_xattn_bq"] = a["L0_xattn_bq"].reshape(1, D)
    got["L0_xattn_bk"] = a["L0_xattn_bk"].reshape(1, D)
    keys = a["L0_ffn_keys"]
    kb = np.zeros((128, 4, 128), np.float32)
    for part in range(2):
        for h in range(4):
            o = 64 * (h % 2)
            kb[o:o + 64, 2 * part + h // 2, o:o + 64] = keys[h, :, part, :].T
    got["key_blocks"] = kb
    got["downT"] = np.ascontiguousarray(a["L0_ffn_down_embed"].T)
    got["L1_delta_b"] = np.ascontiguousarray(np.concatenate([a["L1_attn_Wdelta"], a["L1_attn_Wb"]], axis=1))
    got["w_fcT"] = np.ascontiguousarray(a["L1_ffn_w_fc"].T)
    got["w_projT"] = np.ascontiguousarray(a["L1_ffn_w_proj"].T)
    got["vT"] = np.ascontiguousarray(a["L1_ffn_v"].T)
    got["fast_bT"] = np.ascontiguousarray(a["L1_ffn_fast_b"].T)
    got["uT"] = np.ascontiguousarray(a["L1_ffn_u"].T)
    return got


def kernel(**inputs):
    import concourse.bacc as _bacc
    from concourse.bass_utils import run_bass_kernel_spmd as _run

    nc = _bacc.Bacc("TRN2", target_bir_lowering=False, num_devices=1)
    arrays = layouts(inputs)
    f32 = mybir.dt.float32
    dram = {k: nc.dram_tensor(f"in_{k}", v.shape, f32, kind="ExternalInput").ap() for k, v in arrays.items()}
    dram["scratch"] = nc.dram_tensor("scratch", (32, 2048), f32).ap()
    out = nc.dram_tensor("out_xT", (D, N), f32, kind="ExternalOutput").ap()
    perceiver(nc, dram, out)
    r = _run(nc, [{f"in_{k}": v for k, v in arrays.items()}], core_ids=[0])
    return np.ascontiguousarray(r.results[0]["out_xT"].T).reshape(B, L, D)
```

```python
import numpy as np
import concourse.bass as bass
from concourse import mybir
from contextlib import ExitStack

B, L, D = 32, 32, 512
N = B * L
M = 257
KT_ = D // 128
TT = N // 128
C2 = N // 512
F = 2048
NQ = F // 512
TOPK = int(2 * np.log(L))
NKEYS, NEXP, PH = 64, 2048, 4
HD1, H1 = 64, 16
INNER = HD1 * H1
CT = 256
NCH, CB = N // CT, CT // L
OT1 = INNER // 128
EPS = 1e-5



def constant_tables():
    p = np.arange(128)
    tabs = {}
    tabs["ident"] = np.eye(128)
    l = np.arange(32)
    f = np.concatenate([np.arange(17), np.arange(1, 16)])
    ang = 2 * np.pi * np.outer(l, f) / 32
    base = np.where(np.arange(32)[None, :] < 17, np.cos(ang), np.sin(ang))
    tabs["dft"] = np.kron(np.eye(4), base)
    wf = np.where((f == 0) | (f == 16), 1.0, 2.0)
    tabs["corr"] = np.tile((base * wf[None, :]).T / (32 * 512), (4, 1))
    tabs["own_batch"] = (p[:, None] // 32 == np.arange(4)[None, :]) * 1.0
    tabs["head_ones"] = np.kron(np.eye(4), np.ones((32, 32)))
    rot = np.zeros((128, 128))
    for i in range(0, 128, 2):
        rot[i, i + 1] = -1.0
        rot[i + 1, i] = 1.0
    tabs["rot"] = rot.T
    fr = np.exp(-np.arange(16, dtype=np.float32) * np.float32(np.log(10000.0) / 16))
    th = (np.arange(32, dtype=np.float32)[None, :] * fr[:, None]).astype(np.float32)
    tabs["cos"] = np.cos(th)[(p % 32) // 2]
    tabs["sin"] = np.sin(th)[(p % 32) // 2]
    ok = (p[:, None] // 32 == p[None, :] // 32) & (p[:, None] <= p[None, :])
    tabs["causal"] = np.where(ok, 0.0, -2.0 ** 99)
    tabs["mean_ones"] = np.full((128, 128), 1.0 / D)
    tabs["hid_ones"] = np.full((128, 128), 1.0 / F)
    tabs["ones"] = np.ones((128, 32))
    tabs["iota"] = np.tile(np.arange(64.0), (128, 1))
    tabs["rank"] = np.tile(8.0 - np.arange(8.0), (128, 1))
    dc = np.zeros((128, 128))
    dc[0, ::32] = 32.0
    tabs["dc"] = dc
    ex = np.zeros((128, 512))
    for c in range(512):
        ex[c // 32, c] = 1.0
    tabs["expand"] = ex
    tabs["eps"] = np.full((128, 1), EPS)
    tabs["eps2"] = np.full((128, 1), EPS * EPS)
    tabs["one"] = np.full((128, 1), 1.0)
    return {k: v.astype(np.float32) for k, v in tabs.items()}


TABLES = constant_tables()
TABLE_AT, at = {}, 0
for _k, _v in TABLES.items():
    TABLE_AT[_k] = (at, _v.shape[1])
    at += _v.shape[1]
TABLE_COLS = at

COLUMNS = [("L0_xattn_bv", 4), ("L0_xattn_bo", 4), ("L0_attn_gate_b", 4), ("L0_attn_p_b", 4), ("L0_attn_out_b", 4),
           ("L0_attn_ln1_g", 4), ("L0_attn_ln1_b", 4), ("L0_attn_ln2_g", 4), ("L0_attn_ln2_b", 4),
           ("L0_attn_mlp_b1", 16), ("L0_attn_mlp_b2", 4), ("L0_ffn_bg", 16), ("L0_ffn_bu", 16), ("L0_ffn_bd", 4),
           ("L1_xattn_ln_g", 4), ("L1_xattn_ln_b", 4), ("L1_xattn_bo", 4), ("L1_attn_A", 1), ("L1_attn_bb", 1),
           ("L1_attn_bc", 4), ("L1_attn_bd", 4), ("L1_attn_bdelta", 1), ("clock_b", 1), ("gate", 1)]
COLUMN_AT, at = {}, 0
for _k, _n in COLUMNS:
    COLUMN_AT[_k] = at
    at += _n
COLUMN_COLS = at


def perceiver(nc, dram, out):
    f32 = mybir.dt.float32
    u32 = mybir.dt.uint32
    ACT = mybir.ActivationFunctionType
    ALU = mybir.AluOpType
    AX = mybir.AxisListType
    ctx = ExitStack()
    with ctx:
        def sb(name, shape, dt=f32):
            return ctx.enter_context(nc.sbuf_tensor(name, shape, dt))

        def sem(name):
            return ctx.enter_context(nc.semaphore(name))

        consts = sb("consts", [128, TABLE_COLS])
        cols = sb("cols", [128, COLUMN_COLS])

        def tab(name, rows=128):
            a, n = TABLE_AT[name]
            return consts[0:rows, a:a + n]

        def col(name, i=0, rows=128):
            a = COLUMN_AT[name] + i
            return cols[0:rows, a:a + 1]

        XT = sb("XT", [128, 4, N])
        small = sb("small", [128, 64])
        f32r = mybir.dt.float32r
        ident_r = sb("ident_r", [128, 128], f32r)
        causal_r = sb("causal_r", [128, 128], f32r)
        PIECES = 8
        with ExitStack() as until_last:
            def shared(name, shape):
                return until_last.enter_context(nc.sbuf_tensor(name, shape, f32))

            Y = shared("Y", [128, 4, N])
            XN = shared("XN", [128, 4, N])
            H = shared("H", [128, 2, 4, N])
            arena = shared("arena", [128, 6, 4, 512])
            RN = 17640
            R = shared("R", [128, RN])
        def over(n):
            until_last.enter_context(nc.sbuf_tensor(f"skip{len(skips)}", [128, n], f32))
            skips.append(n)

        skips = []
        with ExitStack() as until_last:
            def part(name, shape):
                return until_last.enter_context(nc.sbuf_tensor(name, shape, f32r))

            y_low = part("y_low", [128, 4, N])
            y_high = part("y_high", [128, 4, N])
            hid_high, hid_low = part("hid_high", [128, 4, N]), part("hid_low", [128, 4, N])
            over(2 * 2048)
            piece_high = part("piece_high", [128, PIECES, 4, 128])
            piece_low = part("piece_low", [128, PIECES, 4, 128])
            xn_high, xn_low = part("xn_high", [128, 4, N]), part("xn_low", [128, 4, N])
        with ExitStack() as until_last:
            def shared_r(name, shape):
                return until_last.enter_context(nc.sbuf_tensor(name, shape, f32r))

            over(2048)
            ctl = shared_r("ctl", [128, 4, 2, 256])
            over(4096 + 4096)
            wmh = shared_r("wmh", [128, 2, 4, 512])
            over(4 * 2048)
            wml = shared_r("wml", [128, 2, 4, 512])
            over(RN - 2048)
            cth = shared_r("cth", [128, 4, 2, 256])
        Yh, Yl = sb("Yh", [128, 4, N], f32r), sb("Yl", [128, 4, N], f32r)
        Hh, Hl = sb("Hh", [128, 4, N], f32r), sb("Hl", [128, 4, N], f32r)
        tern_up, tern_down = sb("tern_up", [128, 2, 4, 512], f32r), sb("tern_down", [128, 16, 512], f32r)

        def region(spec, base=R, limit=RN):
            got, at = {}, 0
            for name, shape in spec:
                n = int(np.prod(shape))
                ap = base[:, at:at + n]
                if len(shape) == 2:
                    ap = ap.rearrange("p (a b) -> p a b", a=shape[0])
                elif len(shape) == 3:
                    ap = ap.rearrange("p (a b c) -> p a b c", a=shape[0], b=shape[1])
                got[name] = ap
                at += n
            assert at <= limit, (at, limit)
            return got

        banks = [ctx.enter_context(nc.psum_tensor(f"bank{i}", [128, 512], f32)) for i in range(8)]

        act_bank_full, act_bank_free = sem("act_bank_full"), sem("act_bank_free")
        dve_bank_full, dve_bank_free = sem("dve_bank_full"), sem("dve_bank_free")
        slot_full = [sem(f"slot_full{i}") for i in range(6)]
        raw_full = [sem(f"raw_full{i}") for i in range(2)]
        stage_done = sem("stage_done")
        act_step, dve_step, pool_step = sem("act_step"), sem("dve_step"), sem("pool_step")
        in_consts, in_xT, in_xtm, in_ctx32 = sem("in_consts"), sem("in_xT"), sem("in_xtm"), sem("in_ctx32")
        in_small = sem("in_small")
        xn_tile = sem("xn_tile")
        a_std, a_var = sem("a_std"), sem("a_var")
        cx_ready, top_ready, topexp_ready = sem("cx_ready"), sem("top_ready"), sem("topexp_ready")
        w_ready, w_stored, m_loaded, mt_ready, m_zero = (sem("w_ready"), sem("w_stored"), sem("m_loaded"),
                                                         sem("mt_ready"), sem("m_zero"))
        ln_sq, ln_out, ln_gain = sem("ln_sq"), sem("ln_out"), sem("ln_gain")
        out_stored = sem("out_stored")
        S = {n: sem(n) for n in (
            "b_ckln", "b_clock", "b_gsp", "b_gcs", "b_gcp", "b_pdif", "b_pexp", "b_sq", "b_qk", "b_cos",
            "c_topin", "c_topexp", "c_p", "c_kb", "c_fac", "c_dense", "c_ee", "c_mul", "c_y", "c_wq",
            "w_high", "w_low", "x_high", "x_low", "h_high", "h_low",
            "d_self", "d_qbd", "d_max", "d_ct", "d_chi", "d_clo", "d_whi", "d_wlo", "d_ct256", "d_probn",
            "e_a", "e_sp", "e_cum", "e_exp", "e_hh", "f_abs", "f_wp", "f_wf", "f_yhi",
            "f_ylo", "f_used", "f_hi", "f_q", "f_lo")}

        class Units:

            def __init__(self, banks):
                self.banks, self.at, self.n = banks, {}, 0

            def new(self, key):
                assert key not in self.at, key
                self.at[key] = self.n
                self.n += 1
                return self.n - 1

        UA, UV = Units(banks[0:4]), Units(banks[4:8])

        loads, slot_of, load_no, uses = [], {}, {}, [0] * 6
        turn = [0]

        def plan(name, src, slots=None):
            if slots is None:
                s = turn[0] % 6
                turn[0] += 1
            else:
                s = slots
            uses[s] += 1
            slot_of[name], load_no[name] = s, uses[s]
            loads.append((name, s, src))

        def rows4(w, r0=0, c0=0, nc_=512):
            return dram[w][r0:r0 + 512, c0:c0 + nc_].rearrange("(k p) n -> p k n", p=128)

        for n_, w in (("aq", "L0_xattn_Wq"), ("ak", "L0_xattn_Wk"), ("av", "L0_xattn_Wv"), ("ao", "L0_xattn_Wo"),
                      ("bv", "L0_attn_Wv"), ("bq", "L0_attn_Wq"), ("bk", "L0_attn_Wk"), ("bg", "L0_attn_gate_w"),
                      ("bp", "L0_attn_p_w"), ("bo", "L0_attn_out_w")):
            plan(n_, rows4(w))

        pieces, piece_no = [], {}

        def plan_split(name, src):
            plan(name, src, turn[0] % 2)
            turn[0] += 1

        def add_piece(name, o):
            piece_no[(name, o)] = len(pieces)
            pieces.append((name, o))

        turn[0] = 0
        for j in range(NQ):
            for name, src in ((("b1", j), rows4("L0_attn_mlp_w1", 0, 512 * j)), (("b2", j), rows4("L0_attn_mlp_w2", 512 * j))):
                plan_split(name, src)
                for o in range(4):
                    add_piece(name, o)
        for j in range(NQ):
            plan_split(("cg", j), rows4("L0_ffn_Wg", 0, 512 * j))
            plan_split(("cu", j), rows4("L0_ffn_Wu", 0, 512 * j))
            plan_split(("cd", j), rows4("L0_ffn_Wd", 512 * j))
            for o in range(4):
                add_piece(("cg", j), o)
                add_piece(("cu", j), o)
            for o in range(4):
                add_piece(("cd", j), o)
        expert_slots = iter([(turn[0] + i) % 2 for i in range(2)] + [2, 3, 4, 5] + [(turn[0] + i) % 2 for i in range(2)])
        for j in range(-1, NQ + 1):
            if j + 1 < NQ:
                plan(("ce", j + 1), rows4("downT", 0, 512 * j + 512), next(expert_slots))
            if j >= 1:
                plan(("cf", j - 1), rows4("L0_ffn_up_embed", 512 * j - 512), next(expert_slots))
        D_FIRST = len(loads)
        for h in range(2):
            plan(("dm", h), rows4("L1_xattn_Wm", 0, 512 * h), 4 + h)
        for cc in range(NCH):
            for w, src, off in (("dq", "L1_xattn_Wq", 0), ("dk", "L1_xattn_Wkv", 0), ("dv", "L1_xattn_Wkv", INNER)):
                for h in range(2):
                    plan((w, cc, h), rows4(src, 0, off + 512 * h), h)
            for h in range(2):
                plan(("dw", cc, h), rows4("L1_xattn_Wo", 512 * h), h)
        E_FIRST = len(loads)
        turn[0] = 0
        plan("edb", dram["L1_delta_b"].rearrange("(k p) n -> p k n", p=128))
        plan("ed", rows4("L1_attn_Wd"))
        last_loads = [("ff", 0)] + [("fa", j) for j in range(NQ)] + [("fp", 0)]
        for j in range(1, NQ):
            last_loads += [("ff", j), ("fp", j)]
        raw_no = {name: i for i, name in enumerate(last_loads)}
        piece_used = {}
        released = {}

        def W(name):
            return arena[:, slot_of[name], :, :]

        RA = region([("m", (TT, 128)), ("mt", (TT, 128)), ("qs", (2, 512)), ("C", (1, 8)), ("cx", (8, 4)),
                     ("st", (8, 6)), ("mv", (8, 2)), ("cr", (1, 32)), ("v8", (1, 8)), ("i8", (1, 8)), ("e8", (1, 8)),
                     ("fi8", (1, 8)),
                     ("eq", (6, 32)), ("w2", (2, 32)), ("bq", (1, 512)), ("bk", (1, 512))])
        xtm, ctm = XN[:, :, :].rearrange("p a b -> p (a b)").rearrange("p (t d) -> p t d", t=8), \
            Y[:, :, :].rearrange("p a b -> p (a b)").rearrange("p (t d) -> p t d", t=8)
        LQ, LK = H[:, 0], H[:, 1]
        RL = region([("sq", (2, 2048)), ("r1", (2, 512)), ("r2", (2, 512))])
        RB = region([("v", (8, 512)), ("ot", (4, N)), ("reset", (1, N)), ("ck", (1, N)), ("p", (8, 512)), ("p2", (1, N)),
                     ("cw", (4, 16)), ("t", (2, N)), ("pm", (1, 32)), ("den", (1, 128))])
        RC = region([("sim", (8, 512)), ("kb", (4, 128)), ("Tx", (8, PH, 32)), ("Ex", (8, PH, 32)), ("Ry", (8, PH, 64)),
                     ("Ey", (8, PH, 64)), ("eq", (1, 2048)), ("s", (4, 512)), ("xv", (1, 8)),
                     ("pj", (2, 512)), ("tv", (8, 8)), ("ti", (8, 8)), ("tf", (2, 8, 8)), ("cand", (PH, 64)), ("rep", (PH, 64)),
                     ("t8", (PH, 8)), ("na", (2, PH, 8)), ("z", (1, 4)), ("rz", (1, 4)), ("ge", (PH, 8)), ("rs", (PH, 8)),
                     ("sd", (8, 64)), ("sel", (PH, 64))])
        RT = RC
        CWQ = XN[:, 2:4].rearrange("p a b -> p (a b)").rearrange("p (k n) -> p k n", k=4)
        hid_raw = R[:, 16384:16384 + 1024].rearrange("p (i n) -> p i n", i=2)
        SJ = [H[:, 0], H[:, 1], XN]
        RD = region([("kt", (8, 2, 322)), ("vt", (2, 3, 1024)), ("ct", (4, 514)), ("m256", (8, 32)), ("c256", (4, 32)), ("qbd", (2, 512))],
                    limit=RN - 2048)
        RDa = region([("p", (8, 289)), ("pt", (4, 384))],
                     base=arena[:, 2:4, :, :].rearrange("p s a b -> p (s a b)"), limit=4096)
        gate_buf, p_buf = [H[:, 1, 0, :], H[:, 1, 3, :]], [H[:, 1, 1, :], RB["p2"][:, 0, :]]
        EE = RC["sim"].rearrange("p t n -> p (t n)").rearrange("p (i n) -> p i n", i=2)
        TR = RC["s"].rearrange("p i n -> p (i n)").rearrange("p (i n) -> p i n", i=2)
        kt = RD["kt"]
        qbd = [RD["qbd"][:, i].rearrange("p (o c) -> p o c", o=8) for i in range(2)]
        ct = RD["ct"].rearrange("p k (b m) -> p k b m", b=2)[:, :, :, 0:256]
        Q1 = Y[:, 0:2].rearrange("p a b -> p (a b)").rearrange("p (o t) -> p o t", o=8)
        K1 = H[:, 0, 0:2].rearrange("p a b -> p (a b)").rearrange("p (o t) -> p o t", o=8)
        V1 = H[:, 0, 2:4].rearrange("p a b -> p (a b)").rearrange("p (o t) -> p o t", o=8)
        RE = region([("dl", (1, N)), ("bb", (1, N)), ("z", (2, N)), ("t", (2, N)), ("reset", (1, N)), ("hh", (1, N)),
                     ("wc", (1, 512))])
        RE["sh"] = R[:, 13544:13544 + N].rearrange("p (b l) -> p b l", l=L)
        RF = region([("vT", (4, 16)), ("fb", (1, 16)), ("uT", (1, F)), ("z", (1, N)), ("z2", (1, N)),
                     ("half", (1, 512)), ("s", (1, 512)), ("sp", (1, 512)), ("ru", (1, 512)), ("diag", (1, 128)),
                     ("gap", (1, 8)), ("aw", (1, 2048)), ("r", (2, 512))])
        raw = [R[:, 9448 + 2048 * i:9448 + 2048 * i + 2048].rearrange("p (k n) -> p k n", k=4) for i in range(2)]
        y5f = R[:, 13544:17640]
        y5 = y5f.rearrange("p (k n) -> p k n", k=4)
        aw = [RF["aw"][:, 0, :].rearrange("p (k n) -> p k n", k=4)] + \
             [y5f[:, 2048 * i:2048 * i + 2048].rearrange("p (k n) -> p k n", k=4) for i in range(2)]
        MAGS = [("ff", 0), ("fa", 0), ("fa", 1), ("fa", 2), ("fa", 3), ("ff", 1), ("ff", 2), ("ff", 3)]
        LNS = [dict(src=XT, dst=XN, double=True, plain=Y, g="L0_attn_ln1_g", b="L0_attn_ln1_b"),
               dict(src=Y, dst=XN, double=False, plain=None, g="L0_attn_ln2_g", b="L0_attn_ln2_b"),
               dict(src=XT, dst=Y, double=False, plain=None, g=None, b=None),
               dict(src=XT, dst=XN, double=True, plain=None, g="L1_xattn_ln_g", b="L1_xattn_ln_b"),
               dict(src=XT, dst=Y, double=False, plain=None, g=None, b=None),
               dict(src=XT, dst=y5, double=False, plain=None, g=None, b=None)]

        def normed(eng, l, c):
            if LNS[l]["g"]:
                eng.wait_ge(ln_gain, C2 * sum(1 for m in LNS[:l] if m["g"]) + c + 1)
            else:
                eng.wait_ge(ln_out, C2 * l + c + 1)

        def ch(c):
            return slice(512 * c, 512 * c + 512)

        def cs(cc):
            return slice(CT * cc, CT * cc + CT)

        def tl(t):
            return slice(128 * t, 128 * t + 128)

        block = ctx.enter_context(nc.Block())

        @block.tensor
        def _(pe):
            stage = [0]
            mm = nc.tensor.matmul

            def end_stage():
                stage[0] += 1
                pe.drain().then_inc(stage_done, 1)
                pe.wait_ge(stage_done, 4 * stage[0])

            def open_act(key):
                u = UA.new(key)
                if u >= 4:
                    pe.wait_ge(act_bank_free, u - 3)
                return UA.banks[u % 4]

            def open_dve(key):
                u = UV.new(key)
                if u >= 4:
                    pe.wait_ge(dve_bank_free, u - 3)
                return UV.banks[u % 4]

            def on_act(key):
                pe.wait_ge(act_bank_free, UA.at[key] + 1)

            def on_dve(key):
                pe.wait_ge(dve_bank_free, UV.at[key] + 1)

            def weight(name):
                pe.wait_ge(slot_full[slot_of[name]], 16 * load_no[name])

            def free_after_act(name):
                released[name] = (act_bank_full, UA.n)

            def free_after_dve(name):
                released[name] = (dve_bank_full, UV.n)

            def linear(bank, w, cols_, x, xc, more=False):
                for k in range(4):
                    last = mm(bank, w[:, k, cols_], x[:, k, xc], start=(k == 0), stop=(k == 3 and not more))
                return last

            def layernorm(l):
                for c in range(C2):
                    b = open_dve(("mean", l, c))
                    linear(b[:, :], tab("mean_ones").unsqueeze(1).to_broadcast([128, 4, 128]), slice(0, 128), LNS[l]["src"], ch(c)
                           ).then_inc(dve_bank_full, 1)
                for c in range(C2):
                    pe.wait_ge(ln_sq, 2 * l + c + 1)
                    b = open_act(("var", l, c))
                    sq = RL["sq"][:, c].rearrange("p (k n) -> p k n", k=4)
                    linear(b[:, :], tab("mean_ones").unsqueeze(1).to_broadcast([128, 4, 128]), slice(0, 128), sq, slice(0, 512)
                           ).then_inc(act_bank_full, 1)

            pe.wait_ge(in_consts, 32)
            pe.wait_ge(in_small, 32)
            pe.wait_ge(in_ctx32, 64)
            for t in range(TT):
                b = open_act(("ldk", t))
                for k in range(4):
                    last = mm(b[:, tl(k)], ctm[:, t, tl(k)], tab("dft"), start=True, stop=True)
                last.then_inc(act_bank_full, 1)
            for t in range(TT):
                pe.wait_ge(xn_tile, t + 1)
                b = open_dve(("ldq", t))
                for k in range(4):
                    last = mm(b[:, tl(k)], xtm[:, t, tl(k)], tab("dft"), start=True, stop=True)
                last.then_inc(dve_bank_full, 1)
            weight("aq")
            weight("ak")
            for t in range(TT):
                on_dve(("ldq", t))
                b = open_act(("qf", t))
                for k in range(4):
                    mm(b[:, :], LQ[:, k, tl(t)], W("aq")[:, k, :], start=(k == 0), stop=False)
                mm(b[:, :], tab("dc", 1), RA["bq"][0:1, 0, :], start=False, stop=True).then_inc(act_bank_full, 1)
                on_act(("ldk", t))
                b = open_dve(("kf", t))
                for k in range(4):
                    mm(b[:, :], LK[:, k, tl(t)], W("ak")[:, k, :], start=(k == 0), stop=False)
                mm(b[:, :], tab("dc", 1), RA["bk"][0:1, 0, :], start=False, stop=True).then_inc(dve_bank_full, 1)
            free_after_act("aq")
            free_after_dve("ak")
            pe.wait_ge(cx_ready, 1)
            b = open_dve("corr")
            mm(b[0:32, 0:32], RA["cx"].rearrange("p a b -> p (a b)"), tab("corr"), start=True, stop=True
               ).then_inc(dve_bank_full, 1)
            pe.wait_ge(mt_ready, 1)
            for t in range(TT):
                b = open_act(("agg", t))
                for k in range(4):
                    last = mm(b[:, tl(k)], ctm[:, t, tl(k)], RA["mt"][:, t, :], start=True, stop=True)
                last.then_inc(act_bank_full, 1)
            on_act(("agg", TT - 1))
            weight("av")
            for o in range(4):
                for c in range(C2):
                    b = open_act(("av", o, c))
                    linear(b[:, :], W("av"), tl(o), LQ, ch(c)).then_inc(act_bank_full, 1)
            free_after_act("av")
            on_act(("av", 3, C2 - 1))
            weight("ao")
            for o in range(4):
                for c in range(C2):
                    b = open_dve(("ao", o, c))
                    linear(b[:, :], W("ao"), tl(o), LK, ch(c)).then_inc(dve_bank_full, 1)
            free_after_dve("ao")
            end_stage()

            layernorm(0)
            pe.wait_ge(in_small, 48)
            for c in range(C2):
                normed(pe, 0, c)
                b = open_act(("clock", c))
                for k in range(4):
                    last = mm(b[0:16, :], RB["cw"][:, k, :], XN[:, k, ch(c)], start=(k == 0), stop=(k == 3))
                last.then_inc(act_bank_full, 1)
            for w in ("bq", "bk", "bg", "bp"):
                weight(w)

            def project(o, names):
                for w in names:
                    for c in range(C2):
                        b = open_act((w, o, c))
                        linear(b[:, :], W(w), tl(o), XN, ch(c)).then_inc(act_bank_full, 1)

            def clock_norms_rotations(o):
                for c in range(C2):
                    pe.wait_ge(S["b_clock"], C2)
                    b = open_dve(("ck", o, c))
                    mm(b[:, :], tab("expand", 16)[:, tl(o)], RB["ck"][0:16, 0, ch(c)], start=True, stop=True
                       ).then_inc(dve_bank_full, 1)
                for i, w in enumerate(("bq", "bk")):
                    for c in range(C2):
                        on_act((w, o, c))
                        b = open_dve(("r" + w, o, c))
                        mm(b[:, :], tab("rot"), H[:, 0, i, ch(c)], start=True, stop=True).then_inc(dve_bank_full, 1)
                for i, w in enumerate(("bq", "bk")):
                    for c in range(C2):
                        pe.wait_ge(S["b_sq"], 4 * o + 2 * i + c + 1)
                        b = open_act(("n" + w, o, c))
                        mm(b[:, :], tab("head_ones"), H[:, 0, 2 + i, ch(c)], start=True, stop=True).then_inc(act_bank_full, 1)

            def scores(o):
                pe.wait_ge(S["b_qk"], 2 * (o + 1))
                for hf in range(2):
                    for h in range(4):
                        hp = slice(32 * h, 32 * h + 32)
                        b = open_act(("s", o, hf, h))
                        mm(b[:, :].rearrange("p (t n) -> p t n", t=4), ident_r[:, :],
                           causal_r[:, :].unsqueeze(1).to_broadcast([128, 4, 128]), start=True, stop=False)
                        for t in range(4):
                            tt = tl(4 * hf + t)
                            last = mm(b[:, tl(t)], H[hp, 0, 1, tt], H[hp, 0, 0, tt], start=False, stop=(t == 3),
                                      tile_position=(32 * h, 0))
                        last.then_inc(act_bank_full, 1)

            def values(o):
                for tt in range(TT):
                    on_act(("s", o, tt // 4, 3))
                    b = open_dve(("pv", o, tt))
                    for h in range(4):
                        hp = slice(32 * h, 32 * h + 32)
                        pt_ = RB["p"][:, 4 * (tt // 4) + h, tl(tt % 4)]
                        mm(b[hp, 0:128], RB["v"][:, tt, 128 * o + 32 * h:128 * o + 32 * h + 32], pt_,
                           start=True, stop=True, tile_position=(0, 32 * h))
                        last = mm(b[hp, 128:256], tab("ones"), pt_, start=True, stop=True, tile_position=(0, 32 * h))
                    last.then_inc(dve_bank_full, 1)

            project(0, ("bg", "bp", "bq", "bk"))
            clock_norms_rotations(0)
            weight("bv")
            for t in range(TT):
                b = open_act(("v", t))
                for k in range(4):
                    last = mm(b[:, :], XN[:, k, tl(t)], W("bv")[:, k, :], start=(k == 0), stop=(k == 3))
                last.then_inc(act_bank_full, 1)
            free_after_act("bv")
            for o in range(4):
                if o < 3:
                    project(o + 1, ("bg", "bp"))
                scores(o)
                if o < 3:
                    project(o + 1, ("bq", "bk"))
                    clock_norms_rotations(o + 1)
                values(o)
            for w in ("bq", "bk", "bg", "bp"):
                free_after_act(w)
            on_dve(("pv", 3, TT - 1))
            weight("bo")
            for o in range(4):
                for c in range(C2):
                    b = open_dve(("bo", o, c))
                    linear(b[:, :], W("bo"), tl(o), RB["ot"], ch(c)).then_inc(dve_bank_full, 1)
            free_after_dve("bo")
            end_stage()
            layernorm(1)

            def split_linear(b, name, o, high, low, c):
                n = piece_no[(name, o)]
                pe.wait_ge(S["w_low"], n + 1)
                for k in range(4):
                    wh, wl = piece_high[:, n % PIECES, k, :], piece_low[:, n % PIECES, k, :]
                    for i, (w_, x_) in enumerate(((wh, high), (wh, low), (wl, high))):
                        last = mm(b[:, :], w_, x_[:, k, ch(c)], start=(k == 0 and i == 0), stop=(k == 3 and i == 2))
                return last

            def down(name, j, ready, first):
                for c in range(C2):
                    pe.wait_ge(ready, first + 8 * j + 7 + c)
                    for o in range(4):
                        b = open_dve((name, j, c, o))
                        split_linear(b, (name, j), o, hid_high, hid_low, c).then_inc(dve_bank_full, 1)
                        if c == C2 - 1:
                            piece_used[piece_no[((name, j), o)]] = (dve_bank_full, UV.n)

            for j in range(NQ):
                for o in range(4):
                    for c in range(C2):
                        if j == 0 and o == 0:
                            pe.wait_ge(S["x_low"], c + 1)
                        b = open_act(("b1", j, o, c))
                        split_linear(b, ("b1", j), o, xn_high, xn_low, c).then_inc(act_bank_full, 1)
                    piece_used[piece_no[(("b1", j), o)]] = (act_bank_full, UA.n)
                down("b2", j, S["h_low"], 0)
            end_stage()

            layernorm(2)
            pe.wait_ge(S["c_wq"], 16)
            for o in range(4):
                for c in range(C2):
                    if o == 0:
                        normed(pe, 2, c)
                    b = open_act(("cq", o, c))
                    linear(b[:, :], CWQ, tl(o), Y, ch(c)).then_inc(act_bank_full, 1)
            on_act(("cq", 3, C2 - 1))
            pe.wait_ge(S["c_kb"], 16)
            for t in range(TT):
                b = open_act(("sim", t))
                for j in range(4):
                    last = mm(b[:, tl(j)], H[:, 0, j, tl(t)], RC["kb"][:, j, :], start=True, stop=True)
                last.then_inc(act_bank_full, 1)
            pe.wait_ge(S["x_low"], 2 * C2)
            for j in range(NQ):
                for o in range(4):
                    for c in range(C2):
                        b = open_act(("cg", j, o, c))
                        split_linear(b, ("cg", j), o, y_high, y_low, c).then_inc(act_bank_full, 1)
                        b = open_dve(("cu", j, o, c))
                        split_linear(b, ("cu", j), o, y_high, y_low, c).then_inc(dve_bank_full, 1)
                    piece_used[piece_no[(("cg", j), o)]] = (act_bank_full, UA.n)
                    piece_used[piece_no[(("cu", j), o)]] = (dve_bank_full, UV.n)
                down("cd", j, S["h_low"], 32)
            released["pieces"] = (dve_bank_full, UV.n)
            pe.wait_ge(S["c_y"], C2)

            for j in range(-1, NQ + 1):
                if j + 1 < NQ:
                    weight(("ce", j + 1))
                if j >= 1:
                    weight(("cf", j - 1))
                for t in range(TT):
                    if j + 1 < NQ:
                        b = open_act(("ce", j + 1, t))
                        linear(b[:, :], W(("ce", j + 1)), tl(t % 4), Y, ch(t // 4)).then_inc(act_bank_full, 1)
                    if 0 <= j < NQ:
                        pe.wait_ge(S["c_p"], TT * j + t + 1)
                        b = open_dve(("pt", j, t))
                        for e in range(4):
                            last = nc.tensor.transpose(b[:, tl(e)], RC["pj"][:, t % 2, tl(e)], tab("ident"))
                        last.then_inc(dve_bank_full, 1)
                    if j >= 1:
                        if t == 0:
                            on_dve(("pt", j - 1, TT - 1))
                        b = open_dve(("cf", j - 1, t))
                        linear(b[:, :], W(("cf", j - 1)), tl(t % 4), SJ[(j - 1) % 3], ch(t // 4)).then_inc(dve_bank_full, 1)
                if j + 1 < NQ:
                    free_after_act(("ce", j + 1))
                if j >= 1:
                    free_after_dve(("cf", j - 1))
            end_stage()

            layernorm(3)

            def pv_group(b, bb, g):
                on_dve(("ptr", bb, g))
                if g == 0:
                    on_act(("vt", bb, 2, 1))
                    on_dve(("vt", bb, 2, 0))
                for x in range(2):
                    o = 2 * g + x
                    for blk, n in ((0, 128), (1, 128), (2, 33)):
                        last = mm(b[:, 64 * o:64 * o + 64], RD["vt"][0:n, bb % 2, blk, tl(o)],
                                  RDa["pt"][0:n, g, 128 * blk + 64 * x:128 * blk + 64 * x + 64],
                                  start=(blk == 0), stop=(blk == 2))
                return last

            pe.wait_ge(S["d_ct256"], 16)
            weight(("dm", 0))
            weight(("dm", 1))
            b = open_act("m256")
            for o in range(OT1):
                for k in range(4):
                    last = mm(b[:, 32 * o:32 * o + 32], W(("dm", o // 4))[:, k, tl(o % 4)], RD["c256"][:, k, :],
                              start=(k == 0), stop=(k == 3))
            last.then_inc(act_bank_full, 1)
            def memory(pr):
                pe.wait_ge(S["d_clo"], pr + 1)
                for o in range(OT1):
                    b = open_act(("mem", pr, o))
                    for k in range(4):
                        wh, wl = wmh[:, o // 4, k, tl(o % 4)], wml[:, o // 4, k, tl(o % 4)]
                        for n_, (w_, c_) in enumerate(((wh, cth), (wh, ctl), (wl, cth))):
                            last = mm(b[:, :].rearrange("p (a c) -> p a c", a=2), w_, c_[:, k, :, :],
                                      start=(k == 0 and n_ == 0), stop=(k == 3 and n_ == 2))
                    last.then_inc(act_bank_full, 1)

            for cc in range(NCH):
                normed(pe, 3, cc * CT // 512)
                for w in ("dq", "dk", "dv"):
                    for o in range(OT1):
                        weight((w, cc, o // 4))
                        b = open_act((w, cc, o))
                        linear(b[:, 0:CT], W((w, cc, o // 4)), tl(o % 4), XN, cs(cc)).then_inc(act_bank_full, 1)
                        free_after_act((w, cc, o // 4))
                if cc == 0:
                    pe.wait_ge(S["d_wlo"], 2)
                    memory(0)
                for pr in range(CB // 2 * cc, CB // 2 * (cc + 1)):
                    on_act(("mem", pr, OT1 - 1))
                    for i in range(2):
                        bb = 2 * pr + i
                        pe.wait_ge(S["d_self"], bb + 1)
                        for blk, (a, n) in enumerate(((0, 128), (128, 128), (289, 33))):
                            for half, (open_, full) in enumerate(((open_dve, dve_bank_full), (open_act, act_bank_full))):
                                b = open_(("vt", bb, blk, half))
                                for o in range(4):
                                    last = nc.tensor.transpose(b[0:n, tl(o)], kt[:, 4 * half + o, i, a:a + n], tab("ident"))
                                last.then_inc(full, 1)
                        pe.wait_ge(S["d_qbd"], bb + 1)
                        for g in range(4):
                            b = open_act(("sc", bb, g))
                            for x in range(2):
                                last = mm(b[64 * x:64 * x + 64, 0:289], qbd[bb % 2][:, 2 * g + x, :],
                                          kt[:, 2 * g + x, i, 0:289], start=True, stop=True, tile_position=(0, 64 * x))
                            last.then_inc(act_bank_full, 1)
                    if pr + 1 < B // 2:
                        memory(pr + 1)
                    steps_ = [(2 * pr + i, g) for i in range(2) for g in range(4)]
                    for n_ in range(10):
                        if n_ < 8:
                            bb, g = steps_[n_]
                            pe.wait_ge(S["d_probn"], 4 * bb + g + 1)
                            pr_t = RDa["p"][:, 4 * (bb % 2) + g, :]
                            b = open_dve(("ptr", bb, g))
                            nc.tensor.transpose(b[:, 0:128], pr_t[:, 0:128], tab("ident"))
                            nc.tensor.transpose(b[:, 128:256], pr_t[:, 128:256], tab("ident"))
                            nc.tensor.transpose(b[0:33, 256:384], pr_t[:, 256:289], tab("ident")).then_inc(dve_bank_full, 1)
                        if n_ >= 2:
                            bb, g = steps_[n_ - 2]
                            if g == 0:
                                bo_ = open_act(("pvd", bb))
                            last = pv_group(bo_, bb, g)
                            if g == 3:
                                last.then_inc(act_bank_full, 1)
                on_act(("pvd", CB * cc + CB - 1))
                for h in range(2):
                    weight(("dw", cc, h))
                for o in range(4):
                    b = open_dve(("dw", cc, o))
                    for k in range(8):
                        last = mm(b[:, 0:CT], W(("dw", cc, k // 4))[:, k % 4, tl(o)], Q1[:, k, :], start=(k == 0), stop=(k == 7))
                    last.then_inc(dve_bank_full, 1)
                for h in range(2):
                    free_after_dve(("dw", cc, h))
            for h in range(2):
                released[("dm", h)] = (stage_done, 4 * (stage[0] + 1))
            end_stage()

            layernorm(4)
            weight("edb")
            pe.wait_ge(in_small, 64)
            for c in range(C2):
                normed(pe, 4, c)
                b = open_act(("dl", c))
                linear(b[:, :], W("edb"), slice(0, 128), Y, ch(c)).then_inc(act_bank_full, 1)
            for c in range(C2):
                b = open_dve(("bb", c))
                linear(b[:, :], W("edb"), slice(128, 256), Y, ch(c)).then_inc(dve_bank_full, 1)
            free_after_dve("edb")
            weight("ed")
            for o in range(4):
                for c in range(C2):
                    b = open_dve(("ed", o, c))
                    linear(b[:, :], W("ed"), tl(o), Y, ch(c), more=True)
                    pe.wait_ge(S["e_hh"], 1)
                    mm(b[:, :], RE["wc"][:, 0, tl(o)], RE["hh"][:, 0, ch(c)], start=False, stop=True).then_inc(dve_bank_full, 1)
            free_after_dve("ed")
            end_stage()

            layernorm(5)
            pe.wait_ge(in_small, 112)
            for c in range(C2):
                normed(pe, 5, c)
                b = open_act(("z", c))
                for k in range(4):
                    last = mm(b[0:16, :], RF["vT"][:, k, :], y5[:, k, ch(c)], start=(k == 0), stop=(k == 3))
                last.then_inc(act_bank_full, 1)

            def f_scale(j):
                n = MAGS.index(("ff", j))
                pe.wait_ge(S["f_abs"], n + 1)
                b = open_dve(("fs", j))
                for k in range(4):
                    last = mm(b[:, :], tab("mean_ones"), aw[n % 3][:, k, :], start=(k == 0), stop=(k == 3))
                last.then_inc(dve_bank_full, 1)

            f_scale(0)
            for c in range(C2):
                on_act(("z", c))
                b = open_act(("z2", c))
                mm(b[0:16, :], RF["fb"][0:16, 0, :], RF["z"][0:16, 0, ch(c)], start=True, stop=True).then_inc(act_bank_full, 1)

            def f_up(j, c):
                pe.wait_ge(S["f_wf"], j + 1)
                if j == 0:
                    on_act(("z2", c))
                    pe.wait_ge(S["f_ylo"], c + 1)
                for o in range(4):
                    b = open_act(("ff", j, c, o))
                    for k in range(4):
                        for part in (Yh, Yl):
                            mm(b[:, :], tern_up[:, j % 2, k, tl(o)], part[:, k, ch(c)], start=(k == 0 and part is Yh), stop=False)
                    mm(b[:, :], RF["uT"][0:16, 0, 512 * j + 128 * o:512 * j + 128 * o + 128], RF["z2"][0:16, 0, ch(c)],
                       start=False, stop=True).then_inc(act_bank_full, 1)

            def f_down(j, c):
                pe.wait_ge(S["f_wp"], j + 1)
                pe.wait_ge(S["f_lo"], 8 * j + 4 * c + 4)
                for o in range(4):
                    b = open_dve(("fp", j, c, o))
                    for k in range(4):
                        for part in (Hh, Hl):
                            last = mm(b[:, :], tern_down[:, 4 * j + k, tl(o)], part[:, k, ch(c)],
                                      start=(k == 0 and part is Hh), stop=(k == 3 and part is Hl))
                    last.then_inc(dve_bank_full, 1)

            for j in range(NQ):
                f_up(j, 0)
                if j == 0:
                    b = open_dve("fps")
                    for i in range(NQ):
                        n = MAGS.index(("fa", i))
                        pe.wait_ge(S["f_abs"], n + 1)
                        for k in range(4):
                            last = mm(b[:, :], tab("hid_ones"), aw[n % 3][:, k, :], start=(i == 0 and k == 0),
                                      stop=(i == 3 and k == 3))
                        last.then_inc(S["f_used"] if i < NQ - 1 else dve_bank_full, 1)
                if j + 1 < NQ:
                    f_scale(j + 1)
                f_up(j, 1)
                f_down(j, 0)
                f_down(j, 1)
            end_stage()

        def common(eng, step_sem):
            stage, steps = [0], [0]

            def end_stage():
                stage[0] += 1
                eng.drain().then_inc(stage_done, 1)
                eng.wait_ge(stage_done, 4 * stage[0])

            def step(ins):
                ins.then_inc(step_sem, 1)
                steps[0] += 1
                eng.wait_ge(step_sem, steps[0])

            return end_stage, step

        for name in dict.fromkeys(name for name, _ in pieces):
            released[name] = (S["w_low"], piece_no[(name, 3)] + 1)

        @block.scalar
        def _(act):
            end_stage, step = common(act, act_step)
            fn = nc.scalar.activation

            def unit(key):
                u = UA.at[key]
                act.wait_ge(act_bank_full, u + 1)
                return UA.banks[u % 4]

            def copy_out(dst, src):
                fn(dst, src, ACT.Copy).then_inc(act_bank_free, 1)

            def vrow(key):
                act.wait_ge(dve_bank_free, UV.at[key] + 1)

            def layernorm(l):
                spec = LNS[l]
                for c in range(C2):
                    vrow(("mean", l, c))
                    sq = RL["sq"][:, c].rearrange("p (k n) -> p k n", k=4)
                    fn(sq, spec["dst"][:, :, ch(c)], ACT.Square).then_inc(ln_sq, 1)
                for c in range(C2):
                    b = unit(("var", l, c))
                    if spec["plain"] is not None:
                        fn(RL["r1"][:, c, :], b[:, :], ACT.Sqrt, bias=tab("eps"))
                    if spec["double"]:
                        fn(RL["r2"][:, c, :], b[:, :], ACT.Sqrt, bias=tab("eps2"), scale=1.0 + EPS).then_inc(act_bank_free, 1)
                    else:
                        fn(RL["r2"][:, c, :], b[:, :], ACT.Sqrt, bias=tab("eps")).then_inc(act_bank_free, 1)
                if spec["g"]:
                    for c in range(C2):
                        act.wait_ge(ln_out, 2 * l + c + 1)
                        for k in range(4):
                            x = spec["dst"][:, k, ch(c)]
                            last = fn(x, x, ACT.Identity, scale=col(spec["g"], k), bias=col(spec["b"], k))
                        last.then_inc(ln_gain, 1)

            def split_high(n):
                if n < len(pieces):
                    name, o = pieces[n]
                    if n >= PIECES:
                        act.wait_ge(*piece_used[n - PIECES])
                    act.wait_ge(slot_full[slot_of[name]], 16 * load_no[name])
                    fn(piece_high[:, n % PIECES], W(name)[:, :, tl(o)], ACT.Copy).then_inc(S["w_high"], 1)

            act.wait_ge(in_consts, 32)
            act.wait_ge(a_var, 1)
            fn(small[:, 0:8], RA["mv"][:, :, 1], ACT.Sqrt, bias=tab("eps")).then_inc(a_std, 1)
            for t in range(TT):
                b = unit(("ldk", t))
                copy_out(LK[:, :, tl(t)], b[:, :].rearrange("p (k n) -> p k n", k=4))
            for t in range(TT):
                b = unit(("qf", t))
                if t >= 2:
                    vrow(("kf", t - 2))
                copy_out(RA["qs"][:, t % 2, :], b[:, :])
            act.wait_ge(top_ready, 1)
            fn(RA["e8"][0:32, 0, 0:TOPK], RA["v8"][0:32, 0, 0:TOPK], ACT.Exp, bias=small[0:32, 8:9],
               accum_out=small[0:32, 9:10]).then_inc(topexp_ready, 1)
            for t in range(TT):
                b = unit(("agg", t))
                copy_out(LQ[:, :, tl(t)], b[:, :].rearrange("p (k n) -> p k n", k=4))
            for o in range(4):
                for c in range(C2):
                    b = unit(("av", o, c))
                    fn(LK[:, o, ch(c)], b[:, :], ACT.Identity, bias=col("L0_xattn_bv", o)).then_inc(act_bank_free, 1)
            end_stage()

            layernorm(0)
            for c in range(C2):
                b = unit(("clock", c))
                fn(RB["ck"][0:16, 0, ch(c)], b[0:16, :], ACT.Identity, bias=col("clock_b", 0, 16)).then_inc(act_bank_free, 1)
            act.wait_ge(act_bank_free, UA.at[("clock", C2 - 1)] + 1)

            def log1pexp(z, t, done):
                step(fn(t, z, ACT.Abs))
                step(fn(t, t, ACT.Exp, scale=-1.0))
                fn(t, t, ACT.Ln, bias=tab("one")[0:z.shape[0], :]).then_inc(done, 1)

            log1pexp(RB["ck"][0:16, 0, :], RB["t"][0:16, 0, :], S["b_ckln"])

            def gates_in(o):
                for w, dst, bias in (("bg", gate_buf, "L0_attn_gate_b"), ("bp", p_buf, "L0_attn_p_b")):
                    for c in range(C2):
                        b = unit((w, o, c))
                        fn(dst[o % 2][:, ch(c)], b[:, :], ACT.Identity, bias=col(bias, o)).then_inc(act_bank_free, 1)

            def factors(o):
                act.wait_ge(act_bank_free, UA.at[("bg", o, C2 - 1)] + 1)
                if o == 0:
                    act.wait_ge(S["b_clock"], C2)
                log1pexp(gate_buf[o % 2], RB["t"][:, 0, :], S["b_gsp"])
                for i, w in enumerate(("bq", "bk")):
                    for c in range(C2):
                        b = unit((w, o, c))
                        fn(H[:, 0, 2 + i, ch(c)], b[:, :], ACT.Square).then_inc(S["b_sq"], 1)
                        copy_out(H[:, 0, i, ch(c)], b[:, :])
                act.wait_ge(S["b_gcs"], o + 1)
                fn(gate_buf[o % 2], RB["t"][:, 1, :], ACT.Exp).then_inc(S["b_gcp"], 1)
                act.wait_ge(S["b_pdif"], o + 1)
                fn(p_buf[o % 2], p_buf[o % 2], ACT.Exp).then_inc(S["b_pexp"], 1)
                for i, w in enumerate(("bq", "bk")):
                    for c in range(C2):
                        b = unit(("n" + w, o, c))
                        fn(H[:, 0, 2 + i, ch(c)], b[:, :], ACT.Sqrt).then_inc(act_bank_free, 1)

            gates_in(0)
            factors(0)
            for t in range(TT):
                b = unit(("v", t))
                copy_out(RB["v"][:, t, :], b[:, :])
            for o in range(4):
                if o < 3:
                    gates_in(o + 1)
                for hf in range(2):
                    for h in range(4):
                        b = unit(("s", o, hf, h))
                        fn(RB["p"][:, 4 * hf + h, :], b[:, :], ACT.Exp, scale=32 ** -0.5).then_inc(act_bank_free, 1)
                if o < 3:
                    factors(o + 1)
            end_stage()
            layernorm(1)

            for n in range(PIECES):
                split_high(n)
                if n < C2:
                    normed(act, 1, n)
                    fn(xn_high[:, :, ch(n)], XN[:, :, ch(n)], ACT.Copy).then_inc(S["x_high"], 1)
            for j in range(NQ):
                for o in range(4):
                    for c in range(C2):
                        n = 8 * j + 2 * o + c
                        b = unit(("b1", j, o, c))
                        if n >= 2:
                            act.wait_ge(S["h_low"], n - 1)
                        fn(hid_raw[:, n % 2], b[:, :], ACT.Gelu, bias=col("L0_attn_mlp_b1", 4 * j + o)).then_inc(act_bank_free, 1)
                        act.wait_ge(act_bank_free, UA.at[("b1", j, o, c)] + 1)
                        fn(hid_high[:, o, ch(c)], hid_raw[:, n % 2], ACT.Copy).then_inc(S["h_high"], 1)
                    split_high(piece_no[(("b1", j), o)] + PIECES)
                for o in range(4):
                    split_high(piece_no[(("b2", j), o)] + PIECES)
            end_stage()

            layernorm(2)
            for o in range(4):
                for c in range(C2):
                    copy_out(H[:, 0, o, ch(c)], unit(("cq", o, c))[:, :])
            for c in range(C2):
                fn(y_high[:, :, ch(c)], Y[:, :, ch(c)], ACT.Copy).then_inc(S["x_high"], 1)
            for t in range(TT):
                copy_out(RC["sim"][:, t, :], unit(("sim", t))[:, :])

            def hidden_high(u):
                j, o, c = u // 8, u // 2 % 4, u % 2
                vrow(("cu", j, o, c))
                fn(hid_high[:, o, ch(c)], RC["s"][:, u % 4, :], ACT.Copy).then_inc(S["h_high"], 1)

            for j in range(NQ):
                for o in range(4):
                    for c in range(C2):
                        u = 8 * j + 2 * o + c
                        b = unit(("cg", j, o, c))
                        if u >= 4:
                            act.wait_ge(S["h_low"], 32 + u - 3)
                        fn(RC["s"][:, u % 4, :], b[:, :], ACT.Silu, bias=col("L0_ffn_bg", 4 * j + o)
                           ).then_inc(act_bank_free, 1)
                        if 2 * o + c:
                            hidden_high(u - 1)
                    if o % 2 == 0:
                        act.wait_ge(S["c_topin"], 2 * j + o // 2 + 1)
                        fn(RT["rep"], RT["rep"], ACT.Exp)
                        fn(RT["sd"], RT["sd"], ACT.Exp).then_inc(S["c_topexp"], 1)
                    if o < 3:
                        split_high(piece_no[(("cg", j), o)] + PIECES)
                        split_high(piece_no[(("cu", j), o)] + PIECES)
                hidden_high(8 * j + 7)
                split_high(piece_no[(("cg", j), 3)] + PIECES)
                split_high(piece_no[(("cu", j), 3)] + PIECES)
                for o in range(4):
                    split_high(piece_no[(("cd", j), o)] + PIECES)
            for j in range(NQ):
                if j == 0:
                    act.wait_ge(dve_bank_full, UV.at[("cd", 3, C2 - 1, 3)] + 1)
                if j >= 3:
                    act.wait_ge(dve_bank_full, UV.at[("cf", j - 3, TT - 1)] + 1)
                for t in range(TT):
                    b = unit(("ce", j, t))
                    fn(SJ[j % 3][:, t % 4, ch(t // 4)], b[:, :], ACT.Silu).then_inc(act_bank_free, 1)
            end_stage()

            layernorm(3)
            b = unit("m256")
            copy_out(RD["m256"], b[:, 0:256].rearrange("p (o b) -> p o b", o=8))

            def split_high(pr):
                act.wait_ge(S["d_ct"], 16 * (pr + 1))
                if pr:
                    act.wait_ge(act_bank_full, UA.at[("mem", pr - 1, OT1 - 1)] + 1)
                fn(cth[:, :, :, :], ct, ACT.Copy).then_inc(S["d_chi"], 1)

            def memory(pr):
                if pr:
                    act.wait_ge(act_bank_full, UA.at[("sc", 2 * pr - 1, 3)] + 1)
                for o in range(OT1):
                    b = unit(("mem", pr, o))
                    copy_out(kt[:, o, :, 0:256], b[:, :].rearrange("p (i m) -> p i m", i=2))
                if pr + 1 < B // 2:
                    split_high(pr + 1)

            for h in range(2):
                fn(wmh[:, h], W(("dm", h)), ACT.Copy).then_inc(S["d_whi"], 1)
            split_high(0)
            for cc in range(NCH):
                for w, dst in (("dq", Q1), ("dk", K1), ("dv", V1)):
                    for o in range(OT1):
                        copy_out(dst[:, o, :], unit((w, cc, o))[:, 0:CT])
                if cc == 0:
                    memory(0)
                for pr in range(CB // 2 * cc, CB // 2 * (cc + 1)):
                    for bb in (2 * pr, 2 * pr + 1):
                        if bb >= 2:
                            act.wait_ge(act_bank_full, UA.at[("pvd", bb - 2)] + 1)
                        for blk, n in ((0, 128), (1, 128), (2, 33)):
                            copy_out(RD["vt"][0:n, bb % 2, blk, 512:1024], unit(("vt", bb, blk, 1))[0:n, :])
                        for g in range(4):
                            x = 4 * (bb % 2) + g
                            b = unit(("sc", bb, g))
                            act.wait_ge(S["d_max"], 4 * bb + g + 1)
                            if bb >= 2:
                                act.wait_ge(dve_bank_full, UV.at[("ptr", bb - 2, g)] + 1)
                            fn(RDa["p"][:, x, :], b[:, 0:289], ACT.Exp, bias=small[:, 16 + x:17 + x], scale=HD1 ** -0.5,
                               accum_out=small[:, 24 + x:25 + x]).then_inc(act_bank_free, 1)
                    if pr + 1 < B // 2:
                        memory(pr + 1)
                    for bb in (2 * pr, 2 * pr + 1):
                        b = unit(("pvd", bb))[:, :].rearrange("p (o c) -> p o c", o=8)
                        tk = slice(32 * (bb % CB), 32 * (bb % CB) + 32)
                        fn(Q1[0:64, :, tk], b[0:64, :, 0:32], ACT.Copy)
                        copy_out(Q1[64:128, :, tk], b[64:128, :, 32:64])
                if cc + 1 < NCH:
                    act.wait_ge(dve_bank_full, UV.at[("dw", cc, 3)] + 1)
            end_stage()

            layernorm(4)
            step(fn(small[:, 32:33], col("L1_attn_A"), ACT.Abs))
            step(fn(small[:, 33:34], small[:, 32:33], ACT.Exp, scale=-1.0))
            fn(small[:, 34:35], small[:, 33:34], ACT.Ln, bias=tab("one")).then_inc(S["e_a"], 1)
            for c in range(C2):
                b = unit(("dl", c))
                fn(RE["z"][:, 0, ch(c)], b[:, :], ACT.Identity, bias=col("L1_attn_bdelta")).then_inc(act_bank_free, 1)
            act.wait_ge(act_bank_free, UA.at[("dl", C2 - 1)] + 1)
            log1pexp(RE["z"][:, 0, :], RE["t"][:, 0, :], S["e_sp"])
            act.wait_ge(S["e_cum"], 2)
            fn(RE["sh"], RE["sh"], ACT.Exp, scale=-1.0)
            fn(RE["z"][:, 0, :], RE["z"][:, 1, :], ACT.Exp).then_inc(S["e_exp"], 1)
            end_stage()

            layernorm(5)
            for c in range(C2):
                normed(act, 5, c)
                fn(Yh[:, :, ch(c)], y5[:, :, ch(c)], ACT.Copy).then_inc(S["f_yhi"], 1)

            def mags(n):
                name = MAGS[n]
                i = raw_no[name]
                act.wait_ge(raw_full[i % 2], 16 * (i // 2 + 1))
                if n == 1:
                    act.wait_ge(S["f_ylo"], C2)
                    act.wait_ge(act_bank_full, UA.at[("z", C2 - 1)] + 1)
                if n >= 3:
                    before = MAGS[n - 3]
                    if before[0] == "ff":
                        act.wait_ge(dve_bank_full, UV.at[("fs", before[1])] + 1)
                    elif before[1] == NQ - 1:
                        act.wait_ge(dve_bank_full, UV.at["fps"] + 1)
                    else:
                        act.wait_ge(S["f_used"], before[1] + 1)
                fn(aw[n % 3], raw[i % 2], ACT.Abs).then_inc(S["f_abs"], 1)

            mags(0)
            for c in range(C2):
                copy_out(RF["z"][0:16, 0, ch(c)], unit(("z", c))[0:16, :])
            for c in range(C2):
                fn(RF["z2"][0:16, 0, ch(c)], unit(("z2", c))[0:16, :], ACT.Copy, scale=col("gate", 0, 16)
                   ).then_inc(act_bank_free, 1)

            def f_up(j, c):
                if j:
                    act.wait_ge(dve_bank_full, UV.at[("fp", j - 1, c, 3)] + 1)
                for o in range(4):
                    n = 8 * j + 4 * c + o
                    b = unit(("ff", j, c, o))
                    if n >= 2:
                        act.wait_ge(S["f_lo"], n - 1)
                    fn(RF["r"][:, n % 2, :], b[:, :], ACT.Relu, scale=small[:, 40 + 4 * (j % 2) + o:41 + 4 * (j % 2) + o]
                       ).then_inc(act_bank_free, 1)
                    act.wait_ge(act_bank_free, UA.at[("ff", j, c, o)] + 1)
                    fn(Hh[:, o, ch(c)], RF["r"][:, n % 2, :], ACT.Square).then_inc(S["f_hi"], 1)

            for j in range(NQ):
                f_up(j, 0)
                if j == 0:
                    for n in range(1, 5):
                        mags(n)
                if j + 1 < NQ:
                    mags(5 + j)
                f_up(j, 1)
            end_stage()

        @block.vector
        def _(dve):
            end_stage, step = common(dve, dve_step)
            v = nc.vector

            def unit(key):
                u = UV.at[key]
                dve.wait_ge(dve_bank_full, u + 1)
                return UV.banks[u % 4]

            def on_act(key):
                dve.wait_ge(act_bank_free, UA.at[key] + 1)

            def stored(key):
                dve.wait_ge(dve_bank_free, UV.at[key] + 1)

            def layernorm(l):
                spec = LNS[l]
                for c in range(C2):
                    b = unit(("mean", l, c))
                    v.tensor_tensor(spec["dst"][:, :, ch(c)], spec["src"][:, :, ch(c)],
                                    b[:, :].unsqueeze(1).to_broadcast([128, 4, 512]), ALU.subtract).then_inc(dve_bank_free, 1)
                for c in range(C2):
                    on_act(("var", l, c))
                    x = spec["dst"][:, :, ch(c)]
                    if spec["plain"] is not None:
                        step(v.reciprocal(RL["r1"][:, c, :], RL["r1"][:, c, :]))
                        v.tensor_tensor(spec["plain"][:, :, ch(c)], x,
                                        RL["r1"][:, c, :].unsqueeze(1).to_broadcast([128, 4, 512]), ALU.mult)
                    step(v.reciprocal(RL["r2"][:, c, :], RL["r2"][:, c, :]))
                    v.tensor_tensor(x, x, RL["r2"][:, c, :].unsqueeze(1).to_broadcast([128, 4, 512]), ALU.mult
                                    ).then_inc(ln_out, 1)

            def add_to_stream(key, o, c, bias=None):
                b = unit(key)
                x = XT[:, o, ch(c)]
                if bias is None:
                    v.tensor_tensor(x, b[:, :], x, ALU.add).then_inc(dve_bank_free, 1)
                else:
                    v.scalar_tensor_tensor(x, b[:, :], bias, x, ALU.add, ALU.add).then_inc(dve_bank_free, 1)

            def split_low(n):
                if n < len(pieces):
                    name, o = pieces[n]
                    dve.wait_ge(S["w_high"], n + 1)
                    v.tensor_tensor(piece_low[:, n % PIECES], W(name)[:, :, tl(o)], piece_high[:, n % PIECES].bitcast(f32),
                                    ALU.subtract).then_inc(S["w_low"], 1)

            def down(name, bias, j):
                for c in range(C2):
                    for o in range(4):
                        add_to_stream((name, j, c, o), o, c, col(bias, o) if j == 0 else None)
                        if c == C2 - 1:
                            split_low(piece_no[((name, j), o)] + PIECES)

            dve.wait_ge(in_consts, 32)
            v.tensor_copy(ident_r[:, :], tab("ident"))
            v.tensor_copy(causal_r[:, :], tab("causal"))
            dve.wait_ge(in_xtm, 16)
            for t in range(TT):
                last = v.bn_stats(RA["st"][:, t, :], xtm[:, t, :])
            step(last)
            for t in range(TT):
                last = v.bn_aggr(RA["mv"][:, t, :], RA["st"][:, t, :])
            last.then_inc(a_var, 1)
            dve.wait_ge(a_std, 1)
            step(v.reciprocal(small[:, 0:8], small[:, 0:8]))
            for t in range(TT):
                v.tensor_scalar(xtm[:, t, :], xtm[:, t, :], RA["mv"][:, t, 0:1], small[:, t:t + 1], ALU.subtract, ALU.mult
                                ).then_inc(xn_tile, 1)
            for t in range(TT):
                b = unit(("ldq", t))
                v.tensor_copy(LQ[:, :, tl(t)], b[:, :].rearrange("p (k n) -> p k n", k=4)).then_inc(dve_bank_free, 1)
            for t in range(TT):
                on_act(("qf", t))
                b = unit(("kf", t))
                v.tensor_tensor_reduce(out=RA["qs"][:, t % 2, :], in0=RA["qs"][:, t % 2, :], in1=b[:, :], scale=1.0, scalar=0.0,
                                       op0=ALU.mult, op1=ALU.add, accum_out=RA["C"][:, 0, t:t + 1]).then_inc(dve_bank_free, 1)
            dve.wait_ge(dve_bank_free, UV.at[("kf", TT - 1)] + 1)
            dve.wait_ge(in_consts, 32)
            v.tensor_tensor(RA["cx"], RA["C"][:, 0, :].unsqueeze(2).to_broadcast([128, 8, 4]),
                            tab("own_batch").unsqueeze(1).to_broadcast([128, 8, 4]), ALU.mult).then_inc(cx_ready, 1)
            b = unit("corr")
            cr, v8, i8, e8, fi8 = (RA[n][0:32, 0, :] for n in ("cr", "v8", "i8", "e8", "fi8"))
            v.tensor_copy(cr, b[0:32, 0:32]).then_inc(dve_bank_free, 1)
            dve.wait_ge(dve_bank_free, UV.at["corr"] + 1)
            step(v.max(v8, cr))
            step(v.max_index(i8.bitcast(u32), v8, cr))
            v.tensor_copy(fi8, i8.bitcast(u32))
            v.tensor_scalar(small[0:32, 8:9], v8[:, 0:1], -1.0, None, ALU.mult).then_inc(top_ready, 1)
            dve.wait_ge(topexp_ready, 1)
            step(v.reciprocal(small[0:32, 9:10], small[0:32, 9:10]))
            step(v.tensor_scalar(e8[:, 0:TOPK], e8[:, 0:TOPK], small[0:32, 9:10], None, ALU.mult))
            eq = RA["eq"][0:32, :, :]
            step(v.tensor_tensor(eq, tab("iota", 32)[:, 0:32].unsqueeze(1).to_broadcast([32, TOPK, 32]),
                                 fi8[:, 0:TOPK].unsqueeze(2).to_broadcast([32, TOPK, 32]), ALU.is_equal))
            step(v.tensor_tensor(eq, eq, e8[:, 0:TOPK].unsqueeze(2).to_broadcast([32, TOPK, 32]), ALU.mult))
            step(v.tensor_reduce(RA["w2"][0:32, 0, :], eq.rearrange("p k t -> p t k"), AX.X, ALU.add))
            v.tensor_copy(RA["w2"][0:32, 1, :], RA["w2"][0:32, 0, :]).then_inc(w_ready, 1)
            dve.wait_ge(m_loaded, 64)
            v.transpose(RA["mt"].rearrange("p a b -> p (a b)"), RA["m"].rearrange("p a b -> p (a b)")).then_inc(mt_ready, 1)
            dve.wait_ge(in_xT, 16)
            for o in range(4):
                for c in range(C2):
                    add_to_stream(("ao", o, c), o, c, col("L0_xattn_bo", o))
            end_stage()

            layernorm(0)
            reset = RB["reset"]
            step(v.memset(reset, 1.0))
            step(v.memset(reset[:, 0, :].rearrange("p (b l) -> p b l", l=L)[:, :, 0:1], 0.0))
            dve.wait_ge(S["b_ckln"], 1)
            for c in range(C2):
                v.scalar_tensor_tensor(RB["ck"][0:16, 0, ch(c)], RB["ck"][0:16, 0, ch(c)], 0.0, RB["t"][0:16, 0, ch(c)],
                                       ALU.max, ALU.add).then_inc(S["b_clock"], 1)
            pcs, q, k = H[:, 1, 2, :], H[:, 0, 0, :], H[:, 0, 1, :]
            t0, t1 = RB["t"][:, 0, :], RB["t"][:, 1, :]
            byb = dict(l=L)

            def normalise(o):
                for t in range(TT):
                    b = unit(("pv", o, t))
                    if t or o:
                        stored(("pv", o, t - 1) if t else ("pv", o - 1, TT - 1))
                    step(v.reciprocal(RB["den"][:, 0, :], b[:, 128:256]))
                    v.tensor_tensor(RB["ot"][:, o, tl(t)], b[:, 0:128], RB["den"][:, 0, :], ALU.mult
                                    ).then_inc(dve_bank_free, 1)

            for o in range(4):
                g, p = gate_buf[o % 2], p_buf[o % 2]
                dve.wait_ge(S["b_gsp"], o + 1)
                step(v.scalar_tensor_tensor(t0, g, 0.0, t0, ALU.max, ALU.add))
                step(v.tensor_tensor_scan(t1, reset[:, 0, :], t0, 0.0, ALU.mult, ALU.subtract))
                v.tensor_scalar(t1, t1, -60.0, 50.0, ALU.max, ALU.min).then_inc(S["b_gcs"], 1)
                on_act(("bp", o, C2 - 1))
                pv3 = p.rearrange("p (b l) -> p b l", **byb)
                step(v.tensor_reduce(RB["pm"][:, 0, :], pv3, AX.X, ALU.max))
                v.tensor_tensor(pv3, pv3, RB["pm"][:, 0, :].unsqueeze(2).to_broadcast([128, B, L]), ALU.subtract
                                ).then_inc(S["b_pdif"], 1)
                dve.wait_ge(S["b_pexp"], o + 1)
                for c in range(C2):
                    b = unit(("ck", o, c))
                    v.tensor_tensor(p[:, ch(c)], b[:, :], p[:, ch(c)], ALU.mult).then_inc(dve_bank_free, 1)
                dve.wait_ge(dve_bank_free, UV.at[("ck", o, C2 - 1)] + 1)
                v.tensor_tensor_scan(pcs, reset[:, 0, :], p, 0.0, ALU.mult, ALU.add)
                for w, t_ in (("bq", t0), ("bk", t1)):
                    for c in range(C2):
                        b = unit(("r" + w, o, c))
                        v.tensor_tensor(t_[:, ch(c)].rearrange("p (b l) -> p b l", **byb),
                                        b[:, :].rearrange("p (b l) -> p b l", **byb),
                                        tab("sin").unsqueeze(1).to_broadcast([128, 16, L]), ALU.mult).then_inc(dve_bank_free, 1)
                on_act(("nbk", o, C2 - 1))
                nrm = H[:, 0, 2:4, :]
                step(v.tensor_scalar(nrm, nrm, 1e-12, None, ALU.max))
                v.scalar_tensor_tensor(H[:, 0, 3, :], g, 1e-8, H[:, 0, 3, :], ALU.add, ALU.mult)
                step(v.scalar_tensor_tensor(H[:, 0, 2, :], pcs, 1e-8, H[:, 0, 2, :], ALU.add, ALU.mult))
                if o:
                    normalise(o - 1)
                step(v.reciprocal(nrm, nrm))
                v.tensor_tensor(pcs, g, H[:, 0, 2, :], ALU.mult)
                v.tensor_tensor(p, p, H[:, 0, 3, :], ALU.mult)
                dve.wait_ge(S["b_cos"], 2 * (o + 1))
                v.tensor_tensor(q, q, t0, ALU.add)
                step(v.tensor_tensor(k, k, t1, ALU.add))
                v.tensor_tensor(q, q, pcs, ALU.mult).then_inc(S["b_qk"], 1)
                v.tensor_tensor(k, k, p, ALU.mult).then_inc(S["b_qk"], 1)
            normalise(3)
            for o in range(4):
                for c in range(C2):
                    b = unit(("bo", o, c))
                    v.scalar_tensor_tensor(Y[:, o, ch(c)], b[:, :], col("L0_attn_out_b", o), Y[:, o, ch(c)], ALU.add, ALU.add
                                           ).then_inc(dve_bank_free, 1)
            end_stage()
            layernorm(1)
            for n in range(PIECES):
                split_low(n)
                if n < C2:
                    dve.wait_ge(S["x_high"], n + 1)
                    v.tensor_tensor(xn_low[:, :, ch(n)], XN[:, :, ch(n)], xn_high[:, :, ch(n)].bitcast(f32), ALU.subtract
                                    ).then_inc(S["x_low"], 1)
            step(v.tensor_tensor(XT[:, :, :], XT[:, :, :], Y[:, :, :], ALU.add))
            for j in range(NQ):
                for o in range(4):
                    for c in range(C2):
                        n = 8 * j + 2 * o + c
                        dve.wait_ge(S["h_high"], n + 1)
                        v.tensor_tensor(hid_low[:, o, ch(c)], hid_raw[:, n % 2], hid_high[:, o, ch(c)].bitcast(f32), ALU.subtract
                                        ).then_inc(S["h_low"], 1)
                    split_low(piece_no[(("b1", j), o)] + PIECES)
                down("b2", "L0_attn_mlp_b2", j)
            end_stage()

            layernorm(2)
            for c in range(C2):
                dve.wait_ge(S["x_high"], C2 + c + 1)
                v.tensor_tensor(y_low[:, :, ch(c)], Y[:, :, ch(c)], y_high[:, :, ch(c)].bitcast(f32), ALU.subtract
                                ).then_inc(S["x_low"], 1)

            def route(t):
                i = t % 2
                tf, na = RT["tf"][:, i], RT["na"][:, i]
                on_act(("sim", t))
                for n in range(8):
                    sim = RC["sim"][:, t, 64 * n:64 * n + 64]
                    last = v.max(RT["tv"][:, n, :], sim)
                step(last)
                for n in range(8):
                    sim = RC["sim"][:, t, 64 * n:64 * n + 64]
                    last = v.max_index(RT["ti"][:, n, :].bitcast(u32), RT["tv"][:, n, :], sim)
                step(last)
                if t >= 2:
                    dve.wait_ge(S["c_dense"], t - 1)
                v.tensor_copy(tf, RT["ti"].bitcast(u32))
                for h in range(PH):
                    last = v.tensor_tensor(RT["cand"][:, h, :].rearrange("p (a b) -> p a b", a=8),
                                           RT["tv"][:, h, :].unsqueeze(2).to_broadcast([128, 8, 8]),
                                           RT["tv"][:, 4 + h, :].unsqueeze(1).to_broadcast([128, 8, 8]), ALU.add)
                step(last)
                for h in range(PH):
                    last = v.max(RT["t8"][:, h, :], RT["cand"][:, h, :])
                step(last)
                for h in range(PH):
                    last = v.match_replace(RT["rep"][:, h, :], RT["t8"][:, h, :], RT["cand"][:, h, :], -3e38)
                step(last)
                sel = RT["sel"]
                step(v.tensor_tensor(sel, RT["rep"], RT["cand"], ALU.not_equal))
                v.tensor_tensor(RT["rep"], RT["cand"], RT["t8"][:, :, 0:1].to_broadcast([128, PH, 64]), ALU.subtract)
                v.tensor_tensor(RT["sd"], RC["sim"][:, t, :].rearrange("p (n k) -> p n k", n=8),
                                RT["tv"][:, :, 0:1].to_broadcast([128, 8, 64]), ALU.subtract).then_inc(S["c_topin"], 1)
                v.tensor_reduce(na.rearrange("p h a -> p (h a)"), sel.rearrange("p h (a b) -> p (h a) b", a=8), AX.X, ALU.add)
                step(v.tensor_scalar(RT["ge"], tf[:, 0:4, :], 32.0, None, ALU.is_ge))
                e = RC["pj"].rearrange("p i n -> p (i n)")
                e4 = e.rearrange("p (a h x) -> p a h x", a=8, h=PH)
                for h in range(PH):
                    last = v.tensor_tensor(e4[:, :, h, :], tab("iota")[:, 0:32].unsqueeze(1).to_broadcast([128, 8, 32]),
                                           tf[:, h, :].unsqueeze(2).to_broadcast([128, 8, 32]), ALU.is_equal)
                step(last)
                for h in range(PH):
                    last = v.tensor_tensor(e4[:, :, h, :], e4[:, :, h, :], na[:, h, :].unsqueeze(2).to_broadcast([128, 8, 32]),
                                           ALU.mult)
                step(last)
                step(v.tensor_tensor(e[:, 0:512], e[:, 0:512], e[:, 512:1024], ALU.add))
                step(v.tensor_tensor(e[:, 0:256], e[:, 0:256], e[:, 256:512], ALU.add))
                step(v.tensor_tensor(RC["Tx"][:, t].rearrange("p h x -> p (h x)"), e[:, 0:128], e[:, 128:256], ALU.add))
                dve.wait_ge(S["c_topexp"], t + 1)
                step(v.tensor_tensor(RT["rep"], RT["rep"], sel, ALU.mult))
                step(v.tensor_reduce(RT["rs"].rearrange("p h a -> p (h a)"), RT["rep"].rearrange("p h (a b) -> p (h a) b", a=8),
                                     AX.X, ALU.add))
                step(v.tensor_reduce(RT["z"][:, 0, :], RT["rs"], AX.X, ALU.add))
                step(v.reciprocal(RT["rz"][:, 0, :], RT["z"][:, 0, :]))
                rz = RT["rz"][:, 0, :].unsqueeze(2)
                step(v.tensor_tensor(RT["rs"], RT["rs"], RT["ge"], ALU.mult))
                step(v.tensor_tensor(RT["rs"], RT["rs"], rz.to_broadcast([128, PH, 8]), ALU.mult))
                v.tensor_reduce(RC["xv"][:, 0, t:t + 1], RT["rs"].rearrange("p h a -> p (h a)"), AX.X, ALU.add)
                v.tensor_copy(RC["Ey"][:, t], RT["sd"][:, 4:8, :])
                v.tensor_tensor(RC["Ex"][:, t], RT["sd"][:, 0:4, 0:32], rz.to_broadcast([128, PH, 32]), ALU.mult
                                ).then_inc(S["c_fac"], 1)

            def hidden_low(u):
                j, o, c = u // 8, u // 2 % 4, u % 2
                dve.wait_ge(S["h_high"], 32 + u + 1)
                v.tensor_tensor(hid_low[:, o, ch(c)], RC["s"][:, u % 4, :], hid_high[:, o, ch(c)].bitcast(f32), ALU.subtract
                                ).then_inc(S["h_low"], 1)

            for j in range(NQ):
                for o in range(4):
                    for c in range(C2):
                        u = 8 * j + 2 * o + c
                        on_act(("cg", j, o, c))
                        b = unit(("cu", j, o, c))
                        v.scalar_tensor_tensor(RC["s"][:, u % 4, :], b[:, :], col("L0_ffn_bu", 4 * j + o), RC["s"][:, u % 4, :],
                                               ALU.add, ALU.mult).then_inc(dve_bank_free, 1)
                        if 2 * o + c:
                            hidden_low(u - 1)
                    if o % 2 == 0:
                        route(2 * j + o // 2)
                    if o < 3:
                        split_low(piece_no[(("cg", j), o)] + PIECES)
                        split_low(piece_no[(("cu", j), o)] + PIECES)
                hidden_low(8 * j + 7)
                split_low(piece_no[(("cg", j), 3)] + PIECES)
                split_low(piece_no[(("cu", j), 3)] + PIECES)
                down("cd", "L0_ffn_bd", j)
            tmp = RC["eq"][:, 0, :].rearrange("p (h x y) -> p h x y", h=PH, x=8)
            dve.wait_ge(S["c_dense"], TT)

            def spread(j, t):
                n = TT * j + t
                xs = slice(8 * j, 8 * j + 8)
                if n:
                    dve.wait_ge(S["c_p"], n)
                for h in range(PH // 2):
                    T = RC["Tx"][:, t, h, xs].unsqueeze(2).to_broadcast([128, 8, 64])
                    Ry = RC["Ry"][:, t, h, :].unsqueeze(1).to_broadcast([128, 8, 64])
                    last = v.tensor_tensor(tmp[:, h], T, Ry, ALU.is_gt)
                step(last)
                flat = RC["eq"][:, 0, :]
                dve.wait_ge(S["c_ee"], n + 1)
                v.tensor_tensor(flat[:, 0:1024], flat[:, 0:1024], EE[:, n % 2, 0:1024], ALU.mult)
                v.scalar_tensor_tensor(flat[:, 1024:2048], TR[:, n % 2, :], 0.0, EE[:, n % 2, 1024:2048], ALU.is_gt, ALU.mult
                                       ).then_inc(S["c_mul"], 1)
                dve.wait_ge(S["c_mul"], n + 1)
                step(v.tensor_tensor(flat[:, 0:1024], flat[:, 0:1024], flat[:, 1024:2048], ALU.add))
                pj = RC["pj"][:, t % 2, :]
                if n >= 2:
                    dve.wait_ge(dve_bank_full, UV.at[("pt", (n - 2) // TT, (n - 2) % TT)] + 1)
                last = v.tensor_tensor(pj, flat[:, 0:512], flat[:, 512:1024], ALU.add)
                if j == NQ - 1:
                    step(last)
                    last = v.tensor_tensor(pj[:, 511:512], pj[:, 511:512], RC["xv"][:, 0, t:t + 1], ALU.add)
                last.then_inc(S["c_p"], 1)

            def weigh(j, t):
                on_act(("ce", j, 3 if t < 4 else 7))
                b = unit(("pt", j, t))
                x = SJ[j % 3][:, :, tl(t)]
                v.tensor_tensor(x, b[:, :].rearrange("p (e n) -> p e n", e=4), x, ALU.mult).then_inc(dve_bank_free, 1)

            for n in range(TT * (NQ + 1) + 1):
                if n < TT * NQ:
                    spread(n // TT, n % TT)
                if 1 <= n <= TT * NQ:
                    weigh((n - 1) // TT, (n - 1) % TT)
                if n > TT:
                    t = (n - 1) % TT
                    add_to_stream(("cf", (n - 1) // TT - 1, t), t % 4, t // 4)
            end_stage()

            layernorm(3)
            dve.wait_ge(act_bank_full, UA.at["m256"] + 1)
            for h in range(2):
                dve.wait_ge(S["d_whi"], h + 1)
                w = W(("dm", h))
                v.tensor_tensor(wml[:, h], w, wmh[:, h].bitcast(f32), ALU.subtract).then_inc(S["d_wlo"], 1)

            def split_low(pr):
                dve.wait_ge(S["d_chi"], pr + 1)
                v.tensor_tensor(ctl[:, :, :, :], ct, cth[:, :, :, :].bitcast(f32), ALU.subtract).then_inc(S["d_clo"], 1)

            split_low(0)
            split_low(1)
            for cc in range(NCH):
                for pr in range(CB // 2 * cc, CB // 2 * (cc + 1)):
                    for bb in (2 * pr, 2 * pr + 1):
                        if bb >= 2:
                            dve.wait_ge(act_bank_full, UA.at[("pvd", bb - 2)] + 1)
                        for blk, n in ((0, 128), (1, 128), (2, 33)):
                            b = unit(("vt", bb, blk, 0))
                            v.tensor_copy(RD["vt"][0:n, bb % 2, blk, 0:512], b[0:n, :]).then_inc(dve_bank_free, 1)
                        for g_ in range(4):
                            x = 16 + 4 * (bb % 2) + g_
                            u = UA.at[("sc", bb, g_)]
                            dve.wait_ge(act_bank_full, u + 1)
                            step(v.reduce_max(small[:, x:x + 1], UA.banks[u % 4][:, 0:289], AX.X))
                            v.tensor_scalar(small[:, x:x + 1], small[:, x:x + 1], -HD1 ** -0.5, None, ALU.mult
                                            ).then_inc(S["d_max"], 1)
                    for bb in (2 * pr, 2 * pr + 1):
                        for g_ in range(4):
                            x = 4 * (bb % 2) + g_
                            on_act(("sc", bb, g_))
                            step(v.reciprocal(small[:, 24 + x:25 + x], small[:, 24 + x:25 + x]))
                            v.tensor_scalar(RDa["p"][:, x, :], RDa["p"][:, x, :], small[:, 24 + x:25 + x], None, ALU.mult
                                            ).then_inc(S["d_probn"], 1)
                    for bb in (2 * pr, 2 * pr + 1):
                        for g_ in range(4):
                            b = unit(("ptr", bb, g_))
                            v.tensor_copy(RDa["pt"][:, g_, 0:256], b[:, 0:256])
                            v.tensor_copy(RDa["pt"][0:33, g_, 256:384], b[0:33, 256:384]).then_inc(dve_bank_free, 1)
                    if pr + 2 < B // 2:
                        split_low(pr + 2)
                for o in range(4):
                    x = XT[:, o, cs(cc)]
                    v.scalar_tensor_tensor(x, unit(("dw", cc, o))[:, 0:CT], col("L1_xattn_bo", o), x, ALU.add, ALU.add
                                           ).then_inc(dve_bank_free, 1)
            end_stage()

            layernorm(4)
            reset = RE["reset"]
            step(v.memset(reset, 1.0))
            step(v.memset(reset[:, 0, :].rearrange("p (b l) -> p b l", l=L)[:, :, 0:1], 0.0))
            dve.wait_ge(S["e_a"], 1)
            step(v.scalar_tensor_tensor(small[:, 35:36], col("L1_attn_A"), 0.0, small[:, 34:35], ALU.max, ALU.add))
            step(v.tensor_scalar(small[:, 35:36], small[:, 35:36], -1.0, None, ALU.mult))
            step(v.tensor_tensor(small[:, 36:40], cols[:, COLUMN_AT["L1_attn_bc"]:COLUMN_AT["L1_attn_bc"] + 4],
                                 cols[:, COLUMN_AT["L1_attn_bd"]:COLUMN_AT["L1_attn_bd"] + 4], ALU.add))
            dve.wait_ge(S["e_sp"], 1)
            dl, bbar, cum, tt = RE["dl"][:, 0, :], RE["bb"][:, 0, :], RE["z"][:, 1, :], RE["t"][:, 1, :]
            step(v.scalar_tensor_tensor(dl, RE["z"][:, 0, :], 0.0, RE["t"][:, 0, :], ALU.max, ALU.add))
            for c in range(C2):
                b = unit(("bb", c))
                v.scalar_tensor_tensor(bbar[:, ch(c)], b[:, :], col("L1_attn_bb"), dl[:, ch(c)], ALU.add, ALU.mult
                                       ).then_inc(dve_bank_free, 1)
            step(v.tensor_scalar(tt, dl, small[:, 35:36], None, ALU.mult))
            step(v.tensor_tensor_scan(cum, reset[:, 0, :], tt, 0.0, ALU.mult, ALU.add))
            v.tensor_scalar(cum, cum, -20.0, 20.0, ALU.max, ALU.min).then_inc(S["e_cum"], 1)
            dve.wait_ge(S["e_cum"], 1)
            v.memset(RE["sh"][:, :, 0:1], 0.0)
            v.tensor_copy(RE["sh"][:, :, 1:L], cum.rearrange("p (b l) -> p b l", l=L)[:, :, 0:L - 1]).then_inc(S["e_cum"], 1)
            dve.wait_ge(S["e_exp"], 1)
            dve.wait_ge(dve_bank_free, UV.at[("bb", C2 - 1)] + 1)
            step(v.tensor_tensor(bbar, bbar, RE["sh"].rearrange("p b l -> p (b l)"), ALU.mult))
            step(v.tensor_tensor_scan(tt, reset[:, 0, :], bbar, 0.0, ALU.mult, ALU.add))
            v.tensor_tensor(RE["hh"][:, 0, :], tt, RE["z"][:, 0, :], ALU.mult).then_inc(S["e_hh"], 1)
            for o in range(4):
                for c in range(C2):
                    add_to_stream(("ed", o, c), o, c, small[:, 36 + o:37 + o])
            end_stage()

            layernorm(5)

            for c in range(C2):
                dve.wait_ge(S["f_yhi"], c + 1)
                v.tensor_tensor(Yl[:, :, ch(c)], y5[:, :, ch(c)], Yh[:, :, ch(c)].bitcast(f32), ALU.subtract
                                ).then_inc(S["f_ylo"], 1)

            def ternary(name, dst, scale, done):
                i = raw_no[name]
                dve.wait_ge(raw_full[i % 2], 16 * (i // 2 + 1))
                if name[0] == "ff":
                    dve.wait_ge(S["f_abs"], MAGS.index(name) + 1)
                w = raw[i % 2]
                half = RF["half"][:, 0, :].unsqueeze(1).to_broadcast([128, 4, 512])
                step(v.tensor_scalar(RF["half"][:, 0, :], scale, 0.5, None, ALU.mult))
                step(v.tensor_tensor(dst, w, half, ALU.is_gt))
                step(v.scalar_tensor_tensor(w, w, -1.0, half, ALU.mult, ALU.is_gt))
                v.tensor_tensor(dst, dst.bitcast(f32), w, ALU.subtract).then_inc(done, 1)

            def scale_of(key, dst, cols_at):
                b = unit(key)
                v.tensor_scalar(dst, b[:, :], 1e-5, None, ALU.max).then_inc(dve_bank_free, 1)
                stored(key)
                for o in range(4):
                    step(v.tensor_tensor_reduce(out=RF["diag"][:, 0, :], in0=dst[:, tl(o)], in1=tab("ident"), scale=1.0,
                                                scalar=0.0, op0=ALU.mult, op1=ALU.add,
                                                accum_out=small[:, cols_at + o:cols_at + o + 1]))

            sp_, sf_, ru = RF["sp"][:, 0, :], RF["s"][:, 0, :], RF["ru"][0:16, 0, :]

            def up_weights(j):
                scale_of(("fs", j), sf_, 40 + 4 * (j % 2))
                step(v.reciprocal(ru, sf_[0:16, :]))
                u_ = RF["uT"][0:16, 0, 512 * j:512 * j + 512]
                if j == 0:
                    dve.wait_ge(in_small, 112)
                step(v.tensor_tensor(u_, u_, ru, ALU.mult))
                ternary(("ff", j), tern_up[:, j % 2], sf_, S["f_wf"])
                dve.wait_ge(S["f_wf"], j + 1)

            def f_low(j, c):
                for o in range(4):
                    n = 8 * j + 4 * c + o
                    dve.wait_ge(S["f_q"], n + 1)
                    v.tensor_tensor(Hl[:, o, ch(c)], RF["r"][:, n % 2, :], Hh[:, o, ch(c)].bitcast(f32), ALU.subtract
                                    ).then_inc(S["f_lo"], 1)

            def f_add(j, c):
                for o in range(4):
                    x = XT[:, o, ch(c)]
                    v.scalar_tensor_tensor(x, unit(("fp", j, c, o))[:, :], small[:, 48 + o:49 + o], x, ALU.mult, ALU.add
                                           ).then_inc(dve_bank_free, 1)

            up_weights(0)
            for j in range(NQ):
                f_low(j, 0)
                if j == 0:
                    scale_of("fps", sp_, 48)
                if j + 1 < NQ:
                    up_weights(j + 1)
                f_low(j, 1)
                if j == 0:
                    ternary(("fp", 0), tern_down[:, 0:4, :], sp_, S["f_wp"])
                    dve.wait_ge(S["f_wp"], 1)
                f_add(j, 0)
                if j + 1 < NQ:
                    ternary(("fp", j + 1), tern_down[:, 4 * j + 4:4 * j + 8, :], sp_, S["f_wp"])
                    dve.wait_ge(S["f_wp"], j + 2)
                f_add(j, 1)
            end_stage()

        @block.gpsimd
        def _(pool):
            end_stage, step = common(pool, pool_step)
            g = nc.gpsimd

            g.memset(RA["m"], 0.0).then_inc(m_zero, 1)
            pool.wait_ge(in_consts, 32)
            end_stage()
            for o in range(4):
                for i, w in enumerate(("bq", "bk")):
                    pool.wait_ge(act_bank_free, UA.at[(w, o, C2 - 1)] + 1)
                    pool.wait_ge(dve_bank_full, UV.at[("r" + w, o, C2 - 1)] + 1)
                    x3 = H[:, 0, i, :].rearrange("p (b l) -> p b l", l=L)
                    g.tensor_tensor(x3, x3, tab("cos").unsqueeze(1).to_broadcast([128, B, L]), ALU.mult).then_inc(S["b_cos"], 1)
            end_stage()
            end_stage()
            eqf = RC["eq"][:, 0, :]
            for t in range(TT):
                i = t % 2
                tf = RT["tf"][:, i]
                pool.wait_ge(S["c_fac"], t + 1)
                e4 = eqf.rearrange("p (a h y) -> p a h y", a=8, h=PH)
                for h in range(PH):
                    key = tf[:, 4 + h, :].unsqueeze(2).to_broadcast([128, 8, 64])
                    last = g.tensor_tensor(e4[:, :, h, :], tab("iota").unsqueeze(1).to_broadcast([128, 8, 64]), key, ALU.subtract)
                step(last)
                step(g.tensor_scalar(eqf, eqf, 0.0, None, ALU.is_equal))
                for h in range(PH):
                    last = g.tensor_tensor(e4[:, :, h, :], e4[:, :, h, :], tab("rank").unsqueeze(2).to_broadcast([128, 8, 64]),
                                           ALU.mult)
                step(last)
                step(g.tensor_tensor(eqf[:, 0:1024], eqf[:, 0:1024], eqf[:, 1024:2048], ALU.add))
                step(g.tensor_tensor(eqf[:, 0:512], eqf[:, 0:512], eqf[:, 512:1024], ALU.add))
                step(g.tensor_tensor(RC["Ry"][:, t].rearrange("p h x -> p (h x)"), eqf[:, 0:256], eqf[:, 256:512], ALU.add))
                g.tensor_scalar(RC["Ry"][:, t], RC["Ry"][:, t], -1.0, 8.0, ALU.mult, ALU.add).then_inc(S["c_dense"], 1)
            pool.wait_ge(dve_bank_full, UV.at[("cu", NQ - 1, 3, C2 - 1)] + 1)
            for c in range(C2):
                g.tensor_tensor(Y[:, :, ch(c)], y_high[:, :, ch(c)].bitcast(f32), y_low[:, :, ch(c)].bitcast(f32), ALU.add
                                ).then_inc(S["c_y"], 1)
            pool.wait_ge(S["c_fac"], TT)
            pool.wait_ge(S["c_dense"], TT)
            pool.wait_ge(S["h_low"], 2 * 8 * NQ)
            for n in range(TT * NQ):
                j, t = n // TT, n % TT
                if n >= 2:
                    pool.wait_ge(S["c_mul"], n - 1)
                for h in range(PH):
                    Ex = RC["Ex"][:, t, h, 8 * j:8 * j + 8].unsqueeze(2).to_broadcast([128, 8, 64])
                    Ey = RC["Ey"][:, t, h, :].unsqueeze(1).to_broadcast([128, 8, 64])
                    last = g.tensor_tensor(EE[:, n % 2, 512 * h:512 * h + 512].rearrange("p (x y) -> p x y", x=8), Ex, Ey, ALU.mult)
                for h in range(PH // 2, PH):
                    T = RC["Tx"][:, t, h, 8 * j:8 * j + 8].unsqueeze(2).to_broadcast([128, 8, 64])
                    Ry = RC["Ry"][:, t, h, :].unsqueeze(1).to_broadcast([128, 8, 64])
                    a = 512 * (h - PH // 2)
                    last = g.tensor_tensor(TR[:, n % 2, a:a + 512].rearrange("p (x y) -> p x y", x=8), T, Ry, ALU.subtract)
                last.then_inc(S["c_ee"], 1)
            end_stage()

            step(g.memset(RD["qbd"], 0.0))
            for bb in range(B):
                pr, i, cc, lb = bb // 2, bb % 2, bb // CB, bb % CB
                if lb == 0:
                    pool.wait_ge(act_bank_free, UA.at[("dv", cc, OT1 - 1)] + 1)
                if i == 0 and pr:
                    pool.wait_ge(act_bank_full, UA.at[("sc", 2 * pr - 1, 3)] + 1)
                if bb:
                    pool.wait_ge(S["d_qbd"], bb)
                tk = slice(32 * lb, 32 * lb + 32)
                for at_ in (256, 289):
                    g.tensor_copy(kt[:, :, i, at_:at_ + 1], RD["m256"][:, :, bb:bb + 1])
                g.tensor_copy(kt[:, :, i, 257:289], K1[:, :, tk])
                g.tensor_copy(kt[:, :, i, 290:322], V1[:, :, tk]).then_inc(S["d_self"], 1)
                if bb >= 2:
                    pool.wait_ge(act_bank_full, UA.at[("sc", bb - 2, 3)] + 1)
                pool.wait_ge(S["d_self"], bb + 1)
                step(g.tensor_copy(qbd[i][0:64, :, 0:32], Q1[0:64, :, tk]))
                g.tensor_copy(qbd[i][64:128, :, 32:64], Q1[64:128, :, tk]).then_inc(S["d_qbd"], 1)
            end_stage()
            end_stage()
            for n in range(8 * NQ):
                pool.wait_ge(S["f_hi"], n + 1)
                g.tensor_tensor(RF["r"][:, n % 2, :], RF["r"][:, n % 2, :], RF["r"][:, n % 2, :], ALU.mult).then_inc(S["f_q"], 1)
            end_stage()

        @block.sync
        def _(sp):
            slot_last = {}

            def load(i):
                name, s_, src = loads[i]
                if s_ in slot_last:
                    sem_, val = released[slot_last[s_]]
                    sp.wait_ge(sem_, val)
                dst = arena[:, s_, :, :]
                if src.shape[2] != 512:
                    dst = dst[:, :, 0:src.shape[2]]
                sp.dma_start(dst, src).then_inc(slot_full[s_], 16)
                slot_last[s_] = name

            sp.dma_start(xtm, dram["x_tokens"].rearrange("(t p) d -> p t d", p=128)).then_inc(in_xtm, 16)
            sp.dma_start(consts[:, :], dram["tables"]).then_inc(in_consts, 16)
            sp.dma_start(cols[:, :], dram["columns"]).then_inc(in_consts, 16)
            c32 = dram["ctx"].rearrange("(t b) m d -> b m t d", b=4)
            for b4 in range(4):
                sp.dma_start(ctm[32 * b4:32 * b4 + 32, :, :], c32[b4, 0:32, :, :]).then_inc(in_ctx32, 16)
            sp.dma_start(RA["bq"][0:1, 0, :], dram["L0_xattn_bq"]).then_inc(in_small, 16)
            sp.dma_start(RA["bk"][0:1, 0, :], dram["L0_xattn_bk"]).then_inc(in_small, 16)
            load(0)
            load(1)
            sp.dma_start(XT[:, :, :], dram["xT"].rearrange("(k p) n -> p k n", p=128)).then_inc(in_xT, 16)
            for i in range(2, 6):
                load(i)
            sp.wait_ge(w_ready, 1)
            scratch = dram["scratch"]
            sp.dma_start(scratch.rearrange("b (r j) -> b r j", j=64),
                         RA["w2"][0:32].rearrange("p a b -> p (a b)").unsqueeze(1).to_broadcast([32, 32, 64])
                         ).then_inc(w_stored, 16)
            sp.wait_ge(w_stored, 16)
            sp.wait_ge(m_zero, 1)
            skew = scratch[:, 32:2048].rearrange("b (l s) -> b l s", s=63)[:, :, 0:32].rearrange("(t b) l m -> b l t m", b=4)
            for b4 in range(4):
                sp.dma_start(RA["m"][32 * b4:32 * b4 + 32, :, 32 * b4:32 * b4 + 32], skew[b4]).then_inc(m_loaded, 16)
            for i in range(6, 9):
                load(i)
            sp.wait_ge(ln_out, C2)
            sp.dma_start(RB["cw"], dram["L0_attn_clock_w"].rearrange("(k p) n -> p k n", p=128)).then_inc(in_small, 16)
            first_split = [i for i, l_ in enumerate(loads) if l_[0] == ("cg", 0)][0]
            for i in range(9, first_split):
                load(i)
            sp.wait_ge(S["x_low"], C2)
            sp.dma_start(CWQ, rows4("L0_ffn_Wq")).then_inc(S["c_wq"], 16)
            load(first_split)
            load(first_split + 1)
            sp.wait_ge(ln_out, 3 * C2)
            sp.dma_start(RC["kb"], dram["key_blocks"]).then_inc(S["c_kb"], 16)
            for i in range(first_split + 2, D_FIRST):
                if loads[i][0] == ("ce", 2):
                    slot_last.update({s_: "pieces" for s_ in range(2, 6)})
                load(i)
            per = (E_FIRST - D_FIRST - 2) // NCH

            def load_ct(pr):
                if pr:
                    sp.wait_ge(S["d_clo"], pr)
                sp.dma_start(RD["ct"], dram["ctxT"].rearrange("(k p) n -> p k n", p=128)[:, :, 514 * pr:514 * pr + 514]
                             ).then_inc(S["d_ct"], 16)

            load(D_FIRST)
            load(D_FIRST + 1)
            sp.wait_ge(stage_done, 4 * 4)
            sp.dma_start(RD["c256"], dram["ctx_lastT"].rearrange("(k p) b -> p k b", p=128)).then_inc(S["d_ct256"], 16)
            load(D_FIRST + 2)
            load(D_FIRST + 3)
            load_ct(0)
            load_ct(1)
            for cc in range(NCH):
                lo = D_FIRST + 2 + per * cc
                for i in range(lo + (2 if cc == 0 else 0), lo + per):
                    load(i)
                for pr in range(CB // 2 * cc + 2, min(CB // 2 * (cc + 1) + 2, B // 2)):
                    load_ct(pr)
            load(E_FIRST)
            load(E_FIRST + 1)
            sp.wait_ge(ln_out, 5 * C2)
            sp.dma_start(RE["wc"][:, 0, :], dram["L1_attn_Wc"]).then_inc(in_small, 16)

            def load_raw(i):
                kind, j = last_loads[i]
                if i >= 2:
                    before = last_loads[i - 2]
                    if before[0] == "fa":
                        sp.wait_ge(S["f_abs"], MAGS.index(before) + 1)
                    else:
                        sp.wait_ge(S["f_wf" if before[0] == "ff" else "f_wp"], before[1] + 1)
                src = rows4("w_fcT", 0, 512 * j) if kind == "ff" else rows4("w_projT", 512 * j)
                sp.dma_start(raw[i % 2], src).then_inc(raw_full[i % 2], 16)

            load_raw(0)
            load_raw(1)
            sp.wait_ge(ln_out, 6 * C2)
            sp.dma_start(RF["vT"], dram["vT"].rearrange("(k p) n -> p k n", p=128)).then_inc(in_small, 16)
            sp.dma_start(RF["fb"][0:16, 0, :], dram["fast_bT"]).then_inc(in_small, 16)
            sp.dma_start(RF["uT"][0:16, 0, :], dram["uT"]).then_inc(in_small, 16)
            for i in range(2, len(last_loads)):
                load_raw(i)
            sp.wait_ge(stage_done, 4 * 7)
            sp.dma_start(out.rearrange("(k p) n -> p k n", p=128), XT[:, :, :]).then_inc(out_stored, 16)
            sp.wait_ge(out_stored, 16)


_PLAIN = ["L0_xattn_Wq", "L0_xattn_Wk", "L0_xattn_Wv", "L0_xattn_Wo", "L0_attn_Wq", "L0_attn_Wk", "L0_attn_Wv",
          "L0_attn_gate_w", "L0_attn_p_w", "L0_attn_out_w", "L0_attn_clock_w", "L0_attn_mlp_w1", "L0_attn_mlp_w2",
          "L0_ffn_Wg", "L0_ffn_Wu", "L0_ffn_Wd", "L0_ffn_Wq", "L0_ffn_up_embed", "L1_xattn_Wq", "L1_xattn_Wkv",
          "L1_xattn_Wm", "L1_xattn_Wo", "L1_attn_Wc", "L1_attn_Wd"]


def layouts(inputs):
    a = {k: np.ascontiguousarray(v) for k, v in inputs.items()}
    got = {k: a[k] for k in _PLAIN}
    x = a["x"].reshape(N, D)
    got["x_tokens"] = x
    got["xT"] = np.ascontiguousarray(x.T)
    got["ctx"] = a["ctx_1024"]
    got["ctxT"] = np.ascontiguousarray(a["ctx_1024"].reshape(B * M, D).T)
    got["ctx_lastT"] = np.ascontiguousarray(a["ctx_1024"][:, M - 1, :].T)
    got["tables"] = np.concatenate([TABLES[k] for k in TABLES], axis=1)
    columns = np.zeros((128, COLUMN_COLS), np.float32)
    for name, n in COLUMNS:
        at_ = COLUMN_AT[name]
        if name == "clock_b":
            columns[0:16, at_] = a["L0_attn_clock_b"]
        elif name == "gate":
            columns[:, at_] = np.broadcast_to(a["L1_ffn_gate"].reshape(1), (128,))
        else:
            columns[:, at_:at_ + n] = a[name].reshape(n, 128).T
    got["columns"] = columns
    got["L0_xattn_bq"] = a["L0_xattn_bq"].reshape(1, D)
    got["L0_xattn_bk"] = a["L0_xattn_bk"].reshape(1, D)
    keys = a["L0_ffn_keys"]
    kb = np.zeros((128, 4, 128), np.float32)
    for part in range(2):
        for h in range(4):
            o = 64 * (h % 2)
            kb[o:o + 64, 2 * part + h // 2, o:o + 64] = keys[h, :, part, :].T
    got["key_blocks"] = kb
    got["downT"] = np.ascontiguousarray(a["L0_ffn_down_embed"].T)
    got["L1_delta_b"] = np.ascontiguousarray(np.concatenate([a["L1_attn_Wdelta"], a["L1_attn_Wb"]], axis=1))
    got["w_fcT"] = np.ascontiguousarray(a["L1_ffn_w_fc"].T)
    got["w_projT"] = np.ascontiguousarray(a["L1_ffn_w_proj"].T)
    got["vT"] = np.ascontiguousarray(a["L1_ffn_v"].T)
    got["fast_bT"] = np.ascontiguousarray(a["L1_ffn_fast_b"].T)
    got["uT"] = np.ascontiguousarray(a["L1_ffn_u"].T)
    return got


def kernel(**inputs):
    import concourse.bacc as _bacc
    from concourse.bass_utils import run_bass_kernel_spmd as _run

    nc = _bacc.Bacc("TRN2", target_bir_lowering=False, num_devices=1)
    arrays = layouts(inputs)
    f32 = mybir.dt.float32
    dram = {k: nc.dram_tensor(f"in_{k}", v.shape, f32, kind="ExternalInput").ap() for k, v in arrays.items()}
    dram["scratch"] = nc.dram_tensor("scratch", (32, 2048), f32).ap()
    out = nc.dram_tensor("out_xT", (D, N), f32, kind="ExternalOutput").ap()
    perceiver(nc, dram, out)
    r = _run(nc, [{f"in_{k}": v for k, v in arrays.items()}], core_ids=[0])
    return np.ascontiguousarray(r.results[0]["out_xT"].T).reshape(B, L, D)
```
